# Optimizing a Trainium2 kernel written in Bass

```python
import numpy as np
import jax
import jax.numpy as jnp

def _softmax(x, axis=-1):
    return jax.nn.softmax(x, axis=axis)

def _gelu(x):
    return jax.nn.gelu(x, approximate=True)

def _silu(x):
    return jax.nn.silu(x)

def _sigmoid(x):
    return jax.nn.sigmoid(x)

def _layernorm(x, axis=-1, eps=1e-05):
    m = jnp.mean(x, axis=axis, keepdims=True)
    v = jnp.var(x, axis=axis, keepdims=True)
    return (x - m) / jnp.sqrt(v + eps)

def _scatter_add(tgt, idx, src, axis=0):
    return tgt.at[idx].add(src)

def _segment_sum(src, seg, n):
    return jax.ops.segment_sum(src, seg, n)
kernel_name = 'mk_gnn_preln_d4_gnn_r32_7efe1f'

def setup_inputs(seed: int=0):
    np.random.seed(seed)
    _w = jnp.asarray

    def _rec_inputs():
        import jax
        import jax.numpy as jnp
        _gk = jax.random.key(seed)
        x = -0.0002928 + 1 * jax.random.normal(jax.random.fold_in(_gk, 1), (3125, 64), jnp.float32)
        _s = jax.random.randint(jax.random.fold_in(_gk, 2), (50000,), 0, 3125, jnp.int32)
        _d = jax.random.randint(jax.random.fold_in(_gk, 3), (50000,), 0, 3125, jnp.int32)
        _loop = jnp.arange(3125, dtype=jnp.int32)
        src = jnp.concatenate([_s, _d, _loop])
        dst = jnp.concatenate([_d, _s, _loop])
        _o = jnp.argsort(dst, stable=True)
        src = src[_o]
        dst = dst[_o]
        edge_attr_16 = 0.000196303 + 1.00016 * jax.random.normal(jax.random.fold_in(_gk, 11), (103125, 16), jnp.float32)
        edge_weight = jax.random.uniform(jax.random.fold_in(_gk, 13), (103125,), jnp.float32, 0.0, 0.999999)
        edge_weight_n2 = jax.random.uniform(jax.random.fold_in(_gk, 14), (103125,), jnp.float32, 0.0, 0.999999)
        return (x, src, dst, edge_attr_16, edge_weight, edge_weight_n2)
    x, src, dst, edge_attr_16, edge_weight, edge_weight_n2 = _rec_inputs()

    def _L0_gnn_setup():
        import jax, jax.numpy as jnp
        import numpy as np
        N, E, D_IN, D_OUT = (2048, 32768, 64, 64)
        EPS = 1e-08
        key = jax.random.key(seed)
        ks = jax.random.split(key, 8)
        h = jax.random.normal(ks[0], (N, D_IN), dtype=jnp.float32)
        edge_index = jax.random.randint(ks[1], (2, E), 0, N, dtype=jnp.int64 if jax.config.jax_enable_x64 else jnp.int32)
        adj_v = jax.random.uniform(ks[2], (E,), dtype=jnp.float32)
        deg_v = jax.random.uniform(ks[3], (E,), dtype=jnp.float32)
        W = jax.random.normal(ks[4], (D_IN, D_OUT), dtype=jnp.float32) / np.sqrt(D_IN)
        b = jax.random.normal(ks[5], (D_OUT,), dtype=jnp.float32) * 0.01
        deg_coeff = jnp.array([0.5, 0.0], dtype=jnp.float32)
        coeff_param = jnp.zeros((3,), dtype=jnp.float32)
        scale_param = 2.0 * jnp.ones((1,), dtype=jnp.float32)
        return {'h': h, 'edge_index': edge_index, 'adj_v': adj_v, 'deg_v': deg_v, 'W': W, 'b': b, 'deg_coeff': deg_coeff, 'coeff_param': coeff_param, 'scale_param': scale_param}
    _L0_gnn_all = _L0_gnn_setup()
    _L0_gnn_in = {k: v for k, v in _L0_gnn_all.items() if k in ('W', 'b', 'deg_coeff', 'coeff_param', 'scale_param')}
    del _L0_gnn_all

    def _L1_gnn_setup():
        import jax, jax.numpy as jnp
        import numpy as np
        NUM_NODES = 3125
        EMBED_DIM = 64
        NUM_LAYERS = 3
        NUM_EDGES = 100000

        def _lightgcn_embedding(emb, edge_index):
            n = emb.shape[0]
            src, dst = (edge_index[0], edge_index[1])
            deg = jax.ops.segment_sum(jnp.ones(src.shape[0], dtype=emb.dtype), dst, num_segments=n)
            deg_inv_sqrt = jnp.where(deg > 0, jax.lax.rsqrt(jnp.maximum(deg, 1.0)), 0.0)
            w = deg_inv_sqrt[src] * deg_inv_sqrt[dst]
            x = emb
            out = emb
            for _ in range(NUM_LAYERS):
                x = jax.ops.segment_sum(w[:, None] * x[src], dst, num_segments=n)
                out = out + x
            return out / (NUM_LAYERS + 1)
        key = jax.random.key(seed)
        k_emb, k_edge = jax.random.split(key)
        emb = jax.random.normal(k_emb, (NUM_NODES, EMBED_DIM), dtype=jnp.float32) * 0.1
        edge_index = jax.random.randint(k_edge, (2, NUM_EDGES), 0, NUM_NODES, dtype=jnp.int64)
        return {'emb': emb, 'edge_index': edge_index}
    _L1_gnn_all = _L1_gnn_setup()
    _L1_gnn_in = {k: v for k, v in _L1_gnn_all.items() if k in ()}
    del _L1_gnn_all

    def _L2_gnn_setup():
        import jax, jax.numpy as jnp
        import numpy as np
        N_NODES = 3125
        N_EDGES = 50000
        DIM = 64
        key = jax.random.key(seed)
        ks = jax.random.split(key, 5)
        x = jax.random.normal(ks[0], (N_NODES, DIM), dtype=jnp.float32)
        edge_index = jax.random.randint(ks[1], (2, N_EDGES), 0, N_NODES, dtype=jnp.int64)
        scale = 1.0 / np.sqrt(DIM)
        W1 = jax.random.normal(ks[2], (DIM, DIM), dtype=jnp.float32) * scale
        b1 = jnp.zeros((DIM,), dtype=jnp.float32)
        W2 = jax.random.normal(ks[3], (DIM, DIM), dtype=jnp.float32) * scale
        b2 = jnp.zeros((DIM,), dtype=jnp.float32)
        return {'x': x, 'edge_index': edge_index, 'W1': W1, 'b1': b1, 'W2': W2, 'b2': b2}
    _L2_gnn_all = _L2_gnn_setup()
    _L2_gnn_in = {k: v for k, v in _L2_gnn_all.items() if k in ('W1', 'b1', 'W2', 'b2')}
    del _L2_gnn_all

    def _L3_gnn_setup():
        import jax, jax.numpy as jnp
        import numpy as np
        N_NODES = 3125
        N_EDGES = 50000
        D_IN = 64
        D_OUT = 64
        EDGE_DIM = 16
        key = jax.random.key(seed)
        ks = jax.random.split(key, 6)
        x = jax.random.normal(ks[0], (N_NODES, D_IN), dtype=jnp.float32)
        edge_index = jax.random.randint(ks[1], (2, N_EDGES), 0, N_NODES, dtype=jnp.int64)
        edge_feature = jax.random.normal(ks[2], (N_EDGES, EDGE_DIM), dtype=jnp.float32)
        W_edge = jax.random.normal(ks[3], (EDGE_DIM, 1), dtype=jnp.float32) * (1.0 / np.sqrt(EDGE_DIM))
        b_edge = jnp.zeros((1,), dtype=jnp.float32)
        W_node = jax.random.normal(ks[4], (D_OUT, D_IN), dtype=jnp.float32) * (1.0 / np.sqrt(D_IN))
        b_node = jnp.zeros((D_OUT,), dtype=jnp.float32)
        return {'x': x, 'edge_index': edge_index, 'edge_feature': edge_feature, 'W_edge': W_edge, 'b_edge': b_edge, 'W_node': W_node, 'b_node': b_node}
    _L3_gnn_all = _L3_gnn_setup()
    _L3_gnn_in = {k: v for k, v in _L3_gnn_all.items() if k in ('W_edge', 'b_edge', 'W_node', 'b_node')}
    del _L3_gnn_all
    return {'x': x, 'src': src, 'dst': dst, 'edge_attr_16': edge_attr_16, 'edge_weight': edge_weight, 'edge_weight_n2': edge_weight_n2, 'L0_gnn_W': _L0_gnn_in['W'], 'L0_gnn_b': _L0_gnn_in['b'], 'L0_gnn_deg_coeff': _L0_gnn_in['deg_coeff'], 'L0_gnn_coeff_param': _L0_gnn_in['coeff_param'], 'L0_gnn_scale_param': _L0_gnn_in['scale_param'], 'L2_gnn_W1': _L2_gnn_in['W1'], 'L2_gnn_b1': _L2_gnn_in['b1'], 'L2_gnn_W2': _L2_gnn_in['W2'], 'L2_gnn_b2': _L2_gnn_in['b2'], 'L3_gnn_W_edge': _L3_gnn_in['W_edge'], 'L3_gnn_b_edge': _L3_gnn_in['b_edge'], 'L3_gnn_W_node': _L3_gnn_in['W_node'], 'L3_gnn_b_node': _L3_gnn_in['b_node']}

def reference(x, src, dst, edge_attr_16, edge_weight, edge_weight_n2, L0_gnn_W, L0_gnn_b, L0_gnn_deg_coeff, L0_gnn_coeff_param, L0_gnn_scale_param, L2_gnn_W1, L2_gnn_b1, L2_gnn_W2, L2_gnn_b2, L3_gnn_W_edge, L3_gnn_b_edge, L3_gnn_W_node, L3_gnn_b_node):
    import jax
    import jax.numpy as jnp

    def _L0_gnn_ref(h, edge_index, adj_v, deg_v, W, b, deg_coeff, coeff_param, scale_param):
        import jax, jax.numpy as jnp
        import numpy as np
        N, E, D_IN, D_OUT = (2048, 32768, 64, 64)
        EPS = 1e-08
        n_nodes = h.shape[0]
        Wh = h @ W + b
        row, col = (edge_index[0], edge_index[1])
        sc = jax.nn.softplus(deg_coeff[0] * deg_v + deg_coeff[1])
        Wr = Wh[row]
        Wc = Wh[col]
        dot = jnp.sum(Wr * Wc, axis=-1)
        nr = jnp.sqrt(jnp.sum(Wr * Wr, axis=-1))
        nc = jnp.sqrt(jnp.sum(Wc * Wc, axis=-1))
        sim = dot / jnp.maximum(nr * nc, EPS)
        sim_pos = jax.nn.relu(sim)
        sim_neg = -jax.nn.relu(-sim)
        no_diag = (row != col).astype(Wh.dtype)
        base = adj_v * sc * no_diag
        prop_pos = jax.ops.segment_sum((base * sim_pos)[:, None] * Wc, row, num_segments=n_nodes)
        prop_neg = jax.ops.segment_sum((base * sim_neg)[:, None] * Wc, row, num_segments=n_nodes)
        coeff = jax.nn.softmax(coeff_param)
        scale = jax.nn.softplus(scale_param)
        return scale * (coeff[0] * prop_pos + coeff[1] * prop_neg + coeff[2] * Wh)

    def _L1_gnn_ref(emb, edge_index):
        import jax, jax.numpy as jnp
        import numpy as np
        NUM_NODES = 3125
        EMBED_DIM = 64
        NUM_LAYERS = 3
        NUM_EDGES = 100000

        def _lightgcn_embedding(emb, edge_index):
            n = emb.shape[0]
            src, dst = (edge_index[0], edge_index[1])
            deg = jax.ops.segment_sum(jnp.ones(src.shape[0], dtype=emb.dtype), dst, num_segments=n)
            deg_inv_sqrt = jnp.where(deg > 0, jax.lax.rsqrt(jnp.maximum(deg, 1.0)), 0.0)
            w = deg_inv_sqrt[src] * deg_inv_sqrt[dst]
            x = emb
            out = emb
            for _ in range(NUM_LAYERS):
                x = jax.ops.segment_sum(w[:, None] * x[src], dst, num_segments=n)
                out = out + x
            return out / (NUM_LAYERS + 1)
        return _lightgcn_embedding(emb, edge_index)

    def _L2_gnn_ref(x, edge_index, W1, b1, W2, b2):
        import jax, jax.numpy as jnp
        import numpy as np
        N_NODES = 3125
        N_EDGES = 50000
        DIM = 64
        src, dst = (edge_index[0], edge_index[1])
        msg = jax.nn.relu(x[src])
        agg = jax.ops.segment_sum(msg, dst, num_segments=x.shape[0])
        h = (1.0 + 0.0) * x + agg
        h = jax.nn.relu(h @ W1 + b1) @ W2 + b2
        return jax.nn.relu(h)

    def _L3_gnn_ref(x, edge_index, edge_feature, W_edge, b_edge, W_node, b_node):
        import jax, jax.numpy as jnp
        import numpy as np
        N_NODES = 3125
        N_EDGES = 50000
        D_IN = 64
        D_OUT = 64
        EDGE_DIM = 16
        gate = jax.nn.sigmoid(edge_feature @ W_edge + b_edge)[:, 0]
        xp = x @ W_node.T + b_node
        row = edge_index[0]
        col = edge_index[1]
        num_nodes = x.shape[0]
        msg = gate[:, None] * xp[col]
        summed = jax.ops.segment_sum(msg, row, num_segments=num_nodes)
        cnt = jax.ops.segment_sum(jnp.ones((row.shape[0],), dtype=xp.dtype), row, num_segments=num_nodes)
        out = summed / jnp.maximum(cnt, 1.0)[:, None]
        return out
    edge_index = jnp.stack([src, dst])
    h = jnp.maximum(_layernorm(x, axis=-1), 0.0)
    x = x + _L0_gnn_ref(h, edge_index, edge_weight, edge_weight_n2, L0_gnn_W, L0_gnn_b, L0_gnn_deg_coeff, L0_gnn_coeff_param, L0_gnn_scale_param)
    h = jnp.maximum(_layernorm(x, axis=-1), 0.0)
    x = x + _L1_gnn_ref(h, edge_index)
    h = jnp.maximum(_layernorm(x, axis=-1), 0.0)
    x = x + _L2_gnn_ref(h, edge_index, L2_gnn_W1, L2_gnn_b1, L2_gnn_W2, L2_gnn_b2)
    h = jnp.maximum(_layernorm(x, axis=-1), 0.0)
    x = x + _L3_gnn_ref(h, edge_index, edge_attr_16, L3_gnn_W_edge, L3_gnn_b_edge, L3_gnn_W_node, L3_gnn_b_node)
    return x

_drawn_inputs = setup_inputs


def setup_inputs(seed=0):
    import zlib

    import numpy as np

    out = dict(_drawn_inputs(seed))
    spreads = {'L0_gnn_coeff_param': (0.0, 0.324),
     'L2_gnn_b1': (0.0, 2.0),
     'L2_gnn_b2': (0.0, 2.0),
     'L3_gnn_b_node': (0.0, 2.0)}
    factors = {'edge_attr_16': 64.0,
     'edge_weight': 2.869,
     'edge_weight_n2': 8.0,
     'L0_gnn_b': 3.4,
     'L3_gnn_W_edge': 64.0}
    for name, (base, spread) in spreads.items():
        noise = np.random.default_rng([zlib.crc32(name.encode()), seed]).standard_normal(out[name].shape)
        drawn = base * np.exp(spread * noise) if base else spread * noise
        out[name] = jnp.asarray(drawn.astype(out[name].dtype))
    for name, factor in factors.items():
        out[name] = (out[name] * factor).astype(out[name].dtype)
    return out
```

```python
from contextlib import ExitStack

import concourse.bass as bass
from concourse import mybir

ALU = mybir.AluOpType
ACT = mybir.ActivationFunctionType
AX = mybir.AxisListType
F32 = mybir.dt.float32
BF16 = mybir.dt.bfloat16
I32 = mybir.dt.int32
U16 = mybir.dt.uint16

P = 128
N = 3125
F = 64
EA = 16
E = 103125
NB = 25
W = N // NB
T = -(-E // P)
EP = T * P
TAIL = E - (P - 1) * T
KEYS = NB + 1
STEP = -(-T // 4)
TQ = 4 * STEP
CODE = 256
CAP = 2
ROUND = CAP * P
HALF = 31
LOOPS = T // (2 * HALF)
MAGIC = 12582912.0
GROUPS = [3, 2] * 5
BANKS = [[0, 1, 2], [3, 4]]
SELF_BANK, DEG_BANK = 5, 6
SENT_COLS = 81
R2_ROWS = 2 * EP + 10 * P
assert 2 * HALF * LOOPS == T and sum(GROUPS) == NB


class Chain:

    def __init__(self, eng, sem, start=0):
        self.eng, self.sem, self.n = eng, sem, start

    def __call__(self, ins):
        self.n += 1
        ins.then_inc(self.sem, 1)
        self.eng.wait_ge(self.sem, self.n)


class Mem:

    def __init__(self, nc, name):
        self.nc, self.name, self.ctx = nc, name, ExitStack()

    def __enter__(self):
        return self

    def __exit__(self, *a):
        return self.ctx.__exit__(*a)

    def sb(self, name, shape, dt=F32):
        return self.ctx.enter_context(self.nc.sbuf_tensor(f"{self.name}_{name}", shape, dt))

    def ps(self, name, shape, dt=F32):
        return self.ctx.enter_context(self.nc.psum_tensor(f"{self.name}_{name}", shape, dt))

    def sem(self, name):
        return self.ctx.enter_context(self.nc.semaphore(f"{self.name}_{name}"))

    def block(self):
        return self.ctx.enter_context(self.nc.Block())


def constants(nc, m, k):
    with Mem(nc, "const") as l:
        col = l.sb("col", [P, P])
        row = l.sb("row", [P, 1])
        s_iota, s_c = l.sem("iota"), l.sem("c")
        block = l.block()

        @block.gpsimd
        def _(pool):
            nc.gpsimd.iota(col[:], [[1, P]], base=0, channel_multiplier=0,
                           allow_small_or_imprecise_dtypes=True).then_inc(s_iota, 1)
            nc.gpsimd.iota(row[:], [[1, 1]], base=0, channel_multiplier=1,
                           allow_small_or_imprecise_dtypes=True).then_inc(s_iota, 1)
            nc.gpsimd.iota(k["codes"][:], [[CODE, NB]], base=0, channel_multiplier=0,
                           allow_small_or_imprecise_dtypes=True).then_inc(s_iota, 1)
            nc.gpsimd.iota(k["numbers"][:, :, :], [[1, P], [0, CAP * max(GROUPS)]], base=0,
                           channel_multiplier=0,
                           allow_small_or_imprecise_dtypes=True).then_inc(s_iota, 1)

        @block.vector
        def _(dve):
            dve.wait_ge(s_iota, 4)
            nc.vector.tensor_scalar(k["ident"][:], col[:], row[:], None, ALU.is_equal).then_inc(s_c, 1)
            nc.vector.tensor_scalar(k["before"][:], col[:], row[:], None, ALU.is_gt).then_inc(s_c, 1)
            nc.vector.memset(k["ones"][:], 1.0).then_inc(s_c, 1)
            nc.vector.memset(k["ones16"][:], 1.0).then_inc(s_c, 1)
            nc.vector.memset(k["zeros"][:], 0.0).then_inc(s_c, 1)
            nc.vector.memset(k["zeros16"][:], 0.0).then_inc(s_c, 1)
            dve.wait_ge(s_c, 6)


def edge_records(nc, rec, src, dst, edge_attr, ew, ewn2, coeff, w_edge, b_edge):
    last = slice(96, P)
    with Mem(nc, "edges") as l:
        srci, dsti = l.sb("srci", [P, T], I32), l.sb("dsti", [P, T], I32)
        adj, deg = l.sb("adj", [P, T]), l.sb("deg", [P, T])
        attr, prod = l.sb("attr", [P, T, EA]), l.sb("prod", [P, T, EA])
        cf, we, be = l.sb("cf", [P, 2]), l.sb("we", [P, EA]), l.sb("be", [P, 1])
        sf, df, q, t1 = (l.sb(x, [P, T]) for x in ("sf", "df", "q", "t1"))
        x, ax, ex, u, lg = (l.sb(y, [P, T]) for y in ("x", "ax", "ex", "u", "lg"))
        z = l.sb("z", [P, T])
        pad = l.sb("pad", [P, T - TAIL])
        s_zero, s_i, s_w, s_a, s_p = (l.sem(y) for y in ("zero", "i", "w", "a", "p"))
        s_dve, s_act, s_pad = l.sem("dve"), l.sem("act"), l.sem("pad")
        block = l.block()

        def load(eng, tile, dram, sem):
            eng.dma_start(tile[0:P - 1, :], dram[0:(P - 1) * T].rearrange("(p t) -> p t", t=T)).then_inc(sem, 16)
            eng.dma_start(tile[P - 1:P, 0:TAIL], dram[(P - 1) * T:E].rearrange("(p t) -> p t", p=1)).then_inc(sem, 16)

        @block.sync
        def _(sp):
            sp.wait_ge(s_zero, 5)
            load(sp, srci, src, s_i)
            load(sp, dsti, dst, s_i)
            sp.dma_start(attr[0:P - 1, :, :], edge_attr[0:(P - 1) * T, :].rearrange("(p t) a -> p t a", t=T)).then_inc(s_a, 16)
            sp.dma_start(attr[P - 1:P, 0:TAIL, :], edge_attr[(P - 1) * T:E, :].rearrange("(p t) a -> p t a", p=1)).then_inc(s_a, 16)

        @block.scalar
        def _(act):
            act.dma_start(cf[:], coeff.rearrange("(a n) -> a n", a=1).to_broadcast([P, 2])).then_inc(s_p, 16)
            act.dma_start(we[:], w_edge.rearrange("a b -> b a").to_broadcast([P, EA])).then_inc(s_p, 16)
            act.dma_start(be[:], b_edge.rearrange("(a n) -> a n", a=1).to_broadcast([P, 1])).then_inc(s_p, 16)
            act.wait_ge(s_zero, 5)
            load(act, adj, ew, s_w)
            load(act, deg, ewn2, s_w)
            act.wait_ge(s_dve, 2)
            nc.scalar.activation(ex[:], ax[:], ACT.Exp, scale=-1.0).then_inc(s_act, 1)
            act.wait_ge(s_dve, 3)
            nc.scalar.activation(lg[:], u[:], ACT.Ln).then_inc(s_act, 1)
            act.wait_ge(s_dve, 10)
            nc.scalar.activation(rec[:, :, 2], z[:], ACT.Sigmoid, bias=be[:]).then_inc(s_act, 1)

        @block.gpsimd
        def _(pool):
            nc.gpsimd.iota(pad[:], [[1, T - TAIL]], base=TAIL, channel_multiplier=T,
                           allow_small_or_imprecise_dtypes=True).then_inc(s_pad, 1)

        @block.vector
        def _(dve):
            nc.vector.memset(srci[last, TAIL:T], 0).then_inc(s_zero, 1)
            nc.vector.memset(dsti[last, TAIL:T], 0).then_inc(s_zero, 1)
            nc.vector.memset(adj[last, TAIL:T], 0.0).then_inc(s_zero, 1)
            nc.vector.memset(deg[last, TAIL:T], 0.0).then_inc(s_zero, 1)
            nc.vector.memset(attr[last, TAIL:T, :], 0.0).then_inc(s_zero, 1)
            c = Chain(dve, s_dve)
            dve.wait_ge(s_p, 48)
            dve.wait_ge(s_w, 64)
            c(nc.vector.tensor_scalar(x[:], deg[:], cf[:, 0:1], cf[:, 1:2], ALU.mult, ALU.add))
            c(nc.vector.scalar_tensor_tensor(ax[:], x[:], -1.0, x[:], ALU.mult, ALU.max))
            dve.wait_ge(s_act, 1)
            c(nc.vector.tensor_scalar(u[:], ex[:], 1.0, None, ALU.add))
            c(nc.vector.tensor_scalar(q[:], u[:], -1.0, None, ALU.add))
            c(nc.vector.tensor_scalar(t1[:], q[:], 0.0, None, ALU.is_equal))
            c(nc.vector.tensor_tensor(q[:], q[:], t1[:], ALU.add))
            c(nc.vector.reciprocal(sf[:], q[:]))
            c(nc.vector.tensor_tensor(df[:], sf[:], ex[:], ALU.mult))
            dve.wait_ge(s_a, 32)
            c(nc.vector.tensor_tensor(prod[:, :, :], attr[:, :, :], we[:, None, :].to_broadcast([P, T, EA]), ALU.mult))
            c(nc.vector.tensor_reduce(z[:], prod[:, :, :], AX.X, ALU.add))
            dve.wait_ge(s_act, 2)
            c(nc.vector.tensor_tensor(lg[:], lg[:], t1[:], ALU.add))
            c(nc.vector.tensor_tensor(lg[:], lg[:], df[:], ALU.mult))
            c(nc.vector.scalar_tensor_tensor(lg[:], x[:], 0.0, lg[:], ALU.max, ALU.add))
            c(nc.vector.tensor_tensor(lg[:], lg[:], adj[:], ALU.mult))
            dve.wait_ge(s_i, 64)
            c(nc.vector.tensor_copy(sf[:], srci[:]))
            c(nc.vector.tensor_copy(df[:], dsti[:]))
            c(nc.vector.tensor_tensor(t1[:], sf[:], df[:], ALU.not_equal))
            c(nc.vector.tensor_tensor(rec[:, :, 3], lg[:], t1[:], ALU.mult))
            c(nc.vector.tensor_scalar(q[:], sf[:], -float(NB // 2), 1.0 / NB, ALU.add, ALU.mult))
            c(nc.vector.tensor_scalar(q[:], q[:], MAGIC, -MAGIC, ALU.add, ALU.add))
            c(nc.vector.tensor_scalar(t1[:], sf[:], float(CODE), None, ALU.mult))
            c(nc.vector.scalar_tensor_tensor(rec[:, :, 0], q[:], float(1 - CODE * NB), t1[:], ALU.mult, ALU.add))
            c(nc.vector.tensor_copy(rec[:, :, 1], df[:]))
            dve.wait_ge(s_pad, 1)
            c(nc.vector.tensor_scalar(pad[:], pad[:], float(E), None, ALU.is_ge))
            c(nc.vector.scalar_tensor_tensor(rec[:, TAIL:T, 0], pad[:], float(CODE * NB), rec[:, TAIL:T, 0], ALU.mult, ALU.add))
            c(nc.vector.scalar_tensor_tensor(rec[:, TAIL:T, 1], pad[:], float(N), rec[:, TAIL:T, 1], ALU.mult, ALU.add))
            dve.wait_ge(s_act, 3)


def mask_steps(nc, dve, c, sem, rec, field, inv, half, masks, key):
    c(nc.vector.memset(masks[:, :, :], 0.0))
    c(nc.vector.tensor_scalar(key[:], rec[:, :, field], -float(half), inv, ALU.add, ALU.mult))
    c(nc.vector.tensor_scalar(key[:], key[:], MAGIC, -MAGIC, ALU.add, ALU.add))
    for j in range(KEYS):
        nc.vector.tensor_scalar(masks[:, j, 0:T], key[:], float(j), None, ALU.is_equal).then_inc(sem, 1)
    c.n += KEYS
    dve.wait_ge(sem, c.n)


def key_masks(nc, rec, field, inv, masks, half):
    with Mem(nc, "masks") as l:
        key, s = l.sb("key", [P, T]), l.sem("s")
        block = l.block()

        @block.vector
        def _(dve):
            mask_steps(nc, dve, Chain(dve, s), s, rec, field, inv, half, masks, key)


def ranks(nc, name, k, rec, field, inv, masks, pos, half):
    with Mem(nc, name) as l:
        key = l.sb("key", [P, T])
        cnt, off, tot, cum = (l.sb(x, [P, KEYS]) for x in ("cnt", "off", "tot", "cum"))
        run = l.sb("run", [P, 2, T])
        both = l.ps("both", [P, 2, 512])
        s_dve, s_pe = l.sem("dve"), l.sem("pe")
        block = l.block()
        n_cnt = [0]

        @block.vector
        def _(dve):
            c = Chain(dve, s_dve)
            mask_steps(nc, dve, c, s_dve, rec, field, inv, half, masks, key)
            c(nc.vector.tensor_reduce(cnt[:], masks[:, 0:KEYS, 0:T], AX.X, ALU.add))
            n_cnt[0] = c.n
            dve.wait_ge(s_pe, 1)
            c(nc.vector.tensor_copy(tot[:], both[:, 1, 0:KEYS]))
            c(nc.vector.tensor_tensor_scan(cum[:], tot[:], tot[:], -1.0, ALU.add, ALU.bypass))
            c(nc.vector.tensor_tensor(cum[:], cum[:], tot[:], ALU.subtract))
            c(nc.vector.tensor_tensor(off[:], cum[:], both[:, 0, 0:KEYS], ALU.add))
            for j in range(KEYS):
                c(nc.vector.tensor_tensor_scan(run[:, j % 2, :], masks[:, j, 0:T], masks[:, j, 0:T], off[:, j:j + 1],
                                               ALU.add, ALU.bypass))
                if j == 0:
                    c(nc.vector.tensor_copy(pos[:], run[:, 0, :]))
                else:
                    c(nc.vector.copy_predicated(pos[:], masks[:, j, 0:T].bitcast(U16), run[:, j % 2, :]))

        @block.tensor
        def _(pe):
            pe.wait_ge(s_dve, n_cnt[0])
            nc.tensor.matmul(both[:, 0, 0:KEYS], k["before"][:], cnt[:], start=True, stop=True)
            nc.tensor.matmul(both[:, 1, 0:KEYS], k["ones"][:], cnt[:], start=True, stop=True).then_inc(s_pe, 1)


def scatter(nc, name, k, rec, pos, out):
    with Mem(nc, name) as l:
        at = l.sb("at", [P, 2, HALF], I32)
        what = l.sb("what", [P, 2, HALF, 4])
        s_staged = [l.sem("staged0"), l.sem("staged1")]
        s_out = [l.sem("out0"), l.sem("out1")]
        s_turn = [l.sem("turn0"), l.sem("turn1")]
        turn, k_one = l.sb("turn", [P, 2]), k["ones"]
        block = l.block()

        @block.vector
        def _(dve):
            with dve.Fori(0, LOOPS) as i:
                for h in range(2):
                    t = bass.ds((2 * i + h) * HALF, HALF)
                    dve.wait_ge(s_out[h], i * (16 * HALF))
                    nc.vector.tensor_copy(at[:, h, :], pos[:, t]).then_inc(s_staged[h], 1)
                    nc.vector.tensor_copy(what[:, h, :, :], rec[:, t, :]).then_inc(s_staged[h], 1)

        @block.gpsimd
        def _(pool):
            with pool.Fori(0, LOOPS) as i:
                for h in range(2):
                    pool.wait_ge(s_staged[h], 2 * i + 2)
                    pool.wait_ge(s_turn[h], i)
                    nc.gpsimd.tensor_tensor(turn[:, h:h + 1], k_one[:, 0:1], k_one[:, 0:1], ALU.add).then_inc(s_turn[h], 1)
                    for t in range(HALF):
                        pool.indirect_dma_start(out, bass.IndirectOffsetOnAxis(ap=at[:, h, t:t + 1], axis=0),
                                                what[:, h, t, :], None).then_inc(s_out[h], 16)
            for h in range(2):
                pool.wait_ge(s_out[h], 16 * HALF * LOOPS)


def reload(nc, name, rec, out):
    with Mem(nc, name) as l:
        s = l.sem("s")
        block = l.block()

        @block.sync
        def _(sp):
            sp.dma_start(rec[:, :, :], out[0:EP, :].rearrange("(p t) f -> p t f", p=P)).then_inc(s, 16)
            sp.wait_ge(s, 16)


def sentinels(nc, out):
    with Mem(nc, "sent") as l:
        tile = l.sb("tile", [P, SENT_COLS, 4])
        s_set, s_out = l.sem("set"), l.sem("out")
        block = l.block()

        @block.vector
        def _(dve):
            nc.vector.memset(tile[:, :, 0], float(CODE * NB)).then_inc(s_set, 1)
            nc.vector.memset(tile[:, :, 1], float(N)).then_inc(s_set, 1)
            nc.vector.memset(tile[:, :, 2:4], 0.0).then_inc(s_set, 1)

        @block.sync
        def _(sp):
            sp.wait_ge(s_set, 3)
            at, n = EP, 0
            while at < R2_ROWS:
                cols = min(SENT_COLS, (R2_ROWS - at) // P)
                sp.dma_start(out[at:at + P * cols, :].rearrange("(p t) f -> p t f", p=P), tile[:, 0:cols, :]).then_inc(s_out, 16)
                at += P * cols
                n += 16
            sp.wait_ge(s_out, n)


def bucket_table(nc, by_src, by_dst, hist_dram, table):
    Q = NB * NB
    with Mem(nc, "hist") as l:
        acc = l.ps("acc", [P, P])
        h = l.sb("h", [P, P])
        row, cum, st = l.sb("row", [1, 4, Q]), l.sb("cum", [1, Q]), l.sb("st", [1, Q])
        mx = l.sb("mx", [1, 4])
        s_pe, s_dve, s_io = l.sem("pe"), l.sem("dve"), l.sem("io")
        block = l.block()

        @block.tensor
        def _(pe):
            a = by_src.rearrange("p j (a t) -> p (j a) t", t=STEP)
            b = by_dst.rearrange("p j (a t) -> p (j a) t", t=STEP)

            def step(t, start=False, stop=False):
                return nc.tensor.matmul(acc[:], a[:, :, t], b[:, :, t], start=start, stop=stop)

            UN = 8
            loops = (STEP - 2) // UN
            step(0, start=True)
            with pe.Fori(0, loops) as i:
                for j in range(UN):
                    step(bass.ds(i * UN + (j + 1), 1))
            for t in range(1 + loops * UN, STEP - 1):
                step(t)
            step(STEP - 1, stop=True).then_inc(s_pe, 1)

        @block.vector
        def _(dve):
            c = Chain(dve, s_dve)
            dve.wait_ge(s_pe, 1)
            c(nc.vector.tensor_copy(h[:], acc[:]))
            dve.wait_ge(s_io, 80)
            for a in range(1, 4):
                c(nc.vector.tensor_tensor(row[:, 0, :], row[:, 0, :], row[:, a, :], ALU.add))
            c(nc.vector.tensor_tensor_scan(cum[:], row[:, 0, :], row[:, 0, :], 0.0, ALU.add, ALU.bypass))
            c(nc.vector.tensor_tensor(st[:], cum[:], row[:, 0, :], ALU.subtract))
            c(nc.vector.tensor_copy(table[0:1, 0:Q], st[:]))
            c(nc.vector.tensor_reduce(mx[:, 0:1], row[:, 0, :], AX.X, ALU.max))
            c(nc.vector.tensor_scalar(mx[:, 1:2], mx[:, 0:1], ROUND / 2 - 0.5, 1.0 / ROUND, ALU.add, ALU.mult))
            c(nc.vector.tensor_scalar(mx[:, 2:3], mx[:, 1:2], MAGIC, -MAGIC, ALU.add, ALU.add))
            c(nc.vector.tensor_copy(table[0:1, Q:Q + 1], mx[:, 2:3]))

        @block.sync
        def _(sp):
            sp.wait_ge(s_dve, 1)
            sp.dma_start(hist_dram, h[:]).then_inc(s_io, 16)
            sp.wait_ge(s_io, 16)
            view = hist_dram.rearrange("(s a) (d b) -> a s d b", a=4, b=4)
            for a in range(4):
                sp.dma_start(row[:, a, :].rearrange("p (s d) -> p s d", s=NB), view[a:a + 1, 0:NB, 0:NB, a],
                             allow_slow_non_contiguous=True).then_inc(s_io, 16)


def d_layout(dram):
    return dram.rearrange("(c p) f -> p c f", p=W)


def s_layout(dram):
    return dram.rearrange("(p c) f -> p c f", c=NB)


def copy_dma(nc, name, pairs):
    with Mem(nc, name) as l:
        s = l.sem("s")
        block = l.block()

        @block.sync
        def _(sp):
            for i, (out, in_) in enumerate(pairs):
                sp.dma_start(out, in_, allow_slow_non_contiguous=True).then_inc(s, 16)
                sp.wait_ge(s, 16 * (i + 1))


def layer_norm_relu(nc, name, x, h):
    with Mem(nc, name) as l:
        xc, sq = l.sb("xc", [W, NB, F]), l.sb("sq", [W, NB, F])
        mean, var, std, inv = (l.sb(y, [W, NB]) for y in ("mean", "var", "std", "inv"))
        eps = l.sb("eps", [W, 1])
        s_dve, s_act = l.sem("dve"), l.sem("act")
        block = l.block()
        full = [W, NB, F]

        @block.vector
        def _(dve):
            c = Chain(dve, s_dve)
            c(nc.vector.memset(eps[:], 1e-5))
            c(nc.vector.tensor_reduce(mean[:], x[:, :, :], AX.X, ALU.add))
            c(nc.vector.tensor_scalar(mean[:], mean[:], 1.0 / F, None, ALU.mult))
            c(nc.vector.tensor_tensor(xc[:, :, :], x[:, :, :], mean[:, :, None].to_broadcast(full), ALU.subtract))
            c(nc.vector.tensor_tensor(sq[:, :, :], xc[:, :, :], xc[:, :, :], ALU.mult))
            c(nc.vector.tensor_reduce(var[:], sq[:, :, :], AX.X, ALU.add))
            dve.wait_ge(s_act, 1)
            c(nc.vector.reciprocal(inv[:], std[:]))
            c(nc.vector.scalar_tensor_tensor(h[:, :, :], xc[:, :, :], 0.0, inv[:, :, None].to_broadcast(full), ALU.max, ALU.mult))

        @block.scalar
        def _(act):
            act.wait_ge(s_dve, 6)
            nc.scalar.activation(std[:], var[:], ACT.Sqrt, bias=eps[:], scale=1.0 / F).then_inc(s_act, 1)


def transpose_nodes(nc, name, k, h, hT):
    with Mem(nc, name) as l:
        ps = l.ps("ps", [F, 2, 512])
        s_pe, s_cp = l.sem("pe"), l.sem("cp")
        block = l.block()
        lots = [list(range(b, min(b + 4, NB))) for b in range(0, NB, 4)]

        @block.tensor
        def _(pe):
            for i, lot in enumerate(lots):
                if i >= 2:
                    pe.wait_ge(s_cp, i - 1)
                for j, b in enumerate(lot):
                    ins = nc.tensor.transpose(ps[:, i % 2, W * j:W * j + W], h[:, b, :], k["ident"][0:W, 0:W])
                ins.then_inc(s_pe, 1)

        @block.vector
        def _(dve):
            for i, lot in enumerate(lots):
                dve.wait_ge(s_pe, i + 1)
                w = W * len(lot)
                nc.vector.tensor_copy(hT[:, W * lot[0]:W * lot[0] + w], ps[:, i % 2, 0:w]).then_inc(s_cp, 1)


def dense_T(nc, name, w, hT, out, bias, relu):
    with Mem(nc, name) as l:
        ps = l.ps("ps", [F, 2, 512])
        s_pe, s_cp = l.sem("pe"), l.sem("cp")
        block = l.block()
        cuts = [(a, min(500, N - a)) for a in range(0, N, 500)]

        @block.tensor
        def _(pe):
            for i, (a, n) in enumerate(cuts):
                if i >= 2:
                    pe.wait_ge(s_cp, i - 1)
                nc.tensor.matmul(ps[:, i % 2, 0:n], w, hT[:, a:a + n], start=True, stop=True).then_inc(s_pe, 1)

        @block.scalar
        def _(act):
            for i, (a, n) in enumerate(cuts):
                act.wait_ge(s_pe, i + 1)
                nc.scalar.activation(out[:, a:a + n], ps[:, i % 2, 0:n], ACT.Relu if relu else ACT.Identity,
                                     bias=bias).then_inc(s_cp, 1)


def dense(nc, name, cols, w, out, bias, relu=False):
    with Mem(nc, name) as l:
        ps = l.ps("ps", [W, 2, 8, F])
        s_pe, s_cp = l.sem("pe"), l.sem("cp")
        block = l.block()
        lots = [list(range(b, min(b + 8, NB))) for b in range(0, NB, 8)]

        @block.tensor
        def _(pe):
            for i, lot in enumerate(lots):
                if i >= 2:
                    pe.wait_ge(s_cp, (i - 1) * (1 + relu))
                for j, b in enumerate(lot):
                    ins = nc.tensor.matmul(ps[:, i % 2, j, :], cols(b), w, start=True, stop=True)
                ins.then_inc(s_pe, 1)

        @block.vector
        def _(dve):
            n = 0
            for i, lot in enumerate(lots):
                dve.wait_ge(s_pe, i + 1)
                part = out[:, lot[0]:lot[0] + len(lot), :]
                nc.vector.tensor_tensor(part, ps[:, i % 2, 0:len(lot), :],
                                        bias[0:W, None, :].to_broadcast([W, len(lot), F]), ALU.add).then_inc(s_cp, 1)
                if relu:
                    n += 2
                    dve.wait_ge(s_cp, n - 1)
                    nc.vector.tensor_scalar(part, part, 0.0, None, ALU.max).then_inc(s_cp, 1)


def inverse_norms(nc, name, wh, rn):
    with Mem(nc, name) as l:
        sq = l.sb("sq", [W, NB, F])
        ss = l.sb("ss", [W, NB])
        nr = l.sb("nr", [W, NB])
        s_dve, s_act = l.sem("dve"), l.sem("act")
        block = l.block()

        @block.vector
        def _(dve):
            c = Chain(dve, s_dve)
            c(nc.vector.tensor_tensor(sq[:, :, :], wh[:, :, :], wh[:, :, :], ALU.mult))
            c(nc.vector.tensor_reduce(ss[:], sq[:, :, :], AX.X, ALU.add))
            dve.wait_ge(s_act, 1)
            c(nc.vector.tensor_scalar(nr[:], nr[:], 1e-18, None, ALU.max))
            c(nc.vector.reciprocal(rn[:], nr[:]))

        @block.scalar
        def _(act):
            act.wait_ge(s_dve, 2)
            nc.scalar.activation(nr[:], ss[:], ACT.Sqrt).then_inc(s_act, 1)


def coefficients(nc, coeff_param, scale_param, coef):
    with Mem(nc, "coef") as l:
        cp, sp_ = l.sb("cp", [P, 3]), l.sb("sp", [P, 1])
        ex, t, u = l.sb("ex", [P, 3]), l.sb("t", [P, 8]), l.sb("u", [P, 1])
        s_in, s_dve, s_act = l.sem("in"), l.sem("dve"), l.sem("act")
        block = l.block()

        @block.sync
        def _(sp):
            sp.dma_start(cp[:], coeff_param.rearrange("(a n) -> a n", a=1).to_broadcast([P, 3])).then_inc(s_in, 16)
            sp.dma_start(sp_[:], scale_param.rearrange("(a n) -> a n", a=1).to_broadcast([P, 1])).then_inc(s_in, 16)

        @block.vector
        def _(dve):
            c = Chain(dve, s_dve)
            dve.wait_ge(s_in, 32)
            c(nc.vector.tensor_reduce(t[:, 0:1], cp[:], AX.X, ALU.max))
            c(nc.vector.tensor_scalar(cp[:], cp[:], t[:, 0:1], None, ALU.subtract))
            c(nc.vector.scalar_tensor_tensor(t[:, 1:2], sp_[:], -1.0, sp_[:], ALU.mult, ALU.max))
            dve.wait_ge(s_act, 2)
            c(nc.vector.tensor_scalar(u[:], t[:, 2:3], 1.0, None, ALU.add))
            c(nc.vector.tensor_scalar(t[:, 3:4], u[:], -1.0, None, ALU.add))
            c(nc.vector.tensor_scalar(t[:, 4:5], t[:, 3:4], 0.0, None, ALU.is_equal))
            c(nc.vector.tensor_tensor(t[:, 3:4], t[:, 3:4], t[:, 4:5], ALU.add))
            c(nc.vector.reciprocal(t[:, 5:6], t[:, 3:4]))
            dve.wait_ge(s_act, 3)
            c(nc.vector.tensor_tensor(t[:, 6:7], t[:, 6:7], t[:, 4:5], ALU.add))
            c(nc.vector.tensor_tensor(t[:, 6:7], t[:, 6:7], t[:, 2:3], ALU.mult))
            c(nc.vector.tensor_tensor(t[:, 6:7], t[:, 6:7], t[:, 5:6], ALU.mult))
            c(nc.vector.scalar_tensor_tensor(t[:, 6:7], sp_[:], 0.0, t[:, 6:7], ALU.max, ALU.add))
            c(nc.vector.tensor_reduce(t[:, 0:1], ex[:], AX.X, ALU.add))
            c(nc.vector.reciprocal(t[:, 7:8], t[:, 0:1]))
            c(nc.vector.tensor_tensor(t[:, 7:8], t[:, 7:8], t[:, 6:7], ALU.mult))
            c(nc.vector.tensor_scalar(coef[:], ex[:], t[:, 7:8], None, ALU.mult))
            c(nc.vector.tensor_scalar(coef[:, 1:2], coef[:, 1:2], -1.0, None, ALU.mult))

        @block.scalar
        def _(act):
            act.wait_ge(s_dve, 3)
            nc.scalar.activation(ex[:], cp[:], ACT.Exp).then_inc(s_act, 1)
            nc.scalar.activation(t[:, 2:3], t[:, 1:2], ACT.Exp, scale=-1.0).then_inc(s_act, 1)
            act.wait_ge(s_dve, 4)
            nc.scalar.activation(t[:, 6:7], u[:], ACT.Ln).then_inc(s_act, 1)


def build_rows(nc, k, sorted_, table, whT, whTs, whD, rnD, rn_row, coef, prop, cnt, deg, c_dram, g_dram):
    NG, LINKS = len(GROUPS), 10
    FIRST = [sum(GROUPS[:g]) for g in range(NG)]
    MAXG, C = max(GROUPS), CAP * NB
    with Mem(nc, "rows") as l:
        recrow = l.sb("recrow", [P, 2, NB, CAP, 4])
        dbase = l.sb("dbase", [P, NB, CAP])
        sbase = l.sb("sbase", [P, 1])
        keys, inside, low = (l.sb(x, [P, 2, C], BF16) for x in ("keys", "inside", "low"))
        skey, dkey = keys[:, 0], keys[:, 1]
        parts = l.sb("parts", [P, 3, 2, C], BF16)
        rest = l.sb("rest", [P, 2, 2, C])
        soh = [l.sb(f"soh{b}", [P, P, CAP * GROUPS[b]], BF16) for b in range(2)]
        doh = [l.sb(f"doh{b}", [P, P, CAP * GROUPS[b]], BF16) for b in range(2)]
        wsrc = [l.sb(f"wsrc{b}", [P, 6, P, CAP * GROUPS[b]], BF16) for b in range(2)]
        out_c = l.sb("out_c", [P, 2, MAXG, W])
        out_g = l.sb("out_g", [P, 2, MAXG, W])
        pos_s, neg_s, fac = (l.sb(x, [W, 2, MAXG, W]) for x in ("pos_s", "neg_s", "fac"))
        b0 = l.sb("b0", [W, 2, MAXG, W])
        rden = l.sb("rden", [W, 2, MAXG, W])
        ps = l.ps("ps", [P, 8, 512])
        names = "loaded taken onehot products freed_act signed factor scaled blocks used row_read link zero kbase"
        s = {x: l.sem(x) for x in names.split()}
        s_st, s_add = [l.sem("st0"), l.sem("st1")], [l.sem("add0"), l.sem("add1")]
        block = l.block()

        def bank(g, lo, width, rows=P):
            a = BANKS[g % 2][0]
            return ps[0:rows, a:a + GROUPS[g], lo:lo + width]

        def plan(eng, body):
            with eng.Fori(0, NB) as row:
                body(row, row, False)
            rounds = eng.value_load(table[0:1, NB * NB:NB * NB + 1], min_val=1, max_val=-(-E // ROUND))
            with eng.If(rounds > 1):
                with eng.Fori(1, rounds) as r:
                    with eng.Fori(0, NB) as row:
                        body(row, r * NB + row, True, r)

        @block.sync
        def _(sp):
            def body(row, w, more, r=0):
                sp.wait_ge(s["loaded"], w * (16 * NB))
                sp.wait_ge(s["taken"], w)
                for d0 in range(0, NB, 5):
                    _, at = nc.values_load_multi_w_load_instructions(
                        table[0:1, bass.ds(row * NB + d0, 5)], engines=[mybir.EngineType.SP], min_val=0, max_val=E)
                    for j in range(5):
                        start = at[j] + r * ROUND if more else at[j]
                        sp.dma_start(recrow[:, bass.ds(w % 2, 1), d0 + j, :, :],
                                     sorted_[bass.ds(start, ROUND), :].rearrange("(p b) f -> p b f", b=CAP)
                                     ).then_inc(s["loaded"], 16)
            plan(sp, body)

        @block.vector
        def _(dve):
            link = s["link"]

            def body(row, w, more, r=0):
                dve.wait_ge(s["loaded"], (w + 1) * (16 * NB))
                base = w * LINKS
                at = [0]

                def c(ins):
                    at[0] += 1
                    ins.then_inc(link, 1)
                    dve.wait_ge(link, base + at[0])

                rec = recrow[:, bass.ds(w % 2, 1), :, :, :].rearrange("p a d c f -> p (a d c) f")
                c(nc.vector.tensor_copy(sbase[:], k["codes"][:, bass.ds(row, 1)]))
                c(nc.vector.tensor_scalar(skey, rec[:, :, 0], sbase[:], None, ALU.subtract))
                c(nc.vector.tensor_tensor(dkey, rec[:, :, 1], dbase[:, :, :].rearrange("p d c -> p (d c)"), ALU.subtract))
                c(nc.vector.tensor_scalar(low[:], keys[:], 0.0, None, ALU.is_ge))
                c(nc.vector.scalar_tensor_tensor(inside[:], keys[:], float(W), low[:], ALU.is_lt, ALU.mult))
                v = rec[:, :, 2:4].rearrange("p c f -> p f c")
                nc.vector.tensor_copy(rest[:, 0], v).then_inc(s["taken"], 1)
                dve.wait_ge(s["taken"], w + 2)
                c(nc.vector.tensor_copy(parts[:, 0], rest[:, 0]))
                c(nc.vector.tensor_tensor(rest[:, 1], rest[:, 0], parts[:, 0], ALU.subtract))
                c(nc.vector.tensor_copy(parts[:, 1], rest[:, 1]))
                c(nc.vector.tensor_tensor(rest[:, 0], rest[:, 1], parts[:, 1], ALU.subtract))
                c(nc.vector.tensor_copy(parts[:, 2], rest[:, 0]))
                for g in range(NG + 1):
                    if g < NG:
                        b, n = g % 2, CAP * GROUPS[g]
                        lo = CAP * FIRST[g]
                        gi = w * NG + g
                        shape = [P, P, n]
                        if g >= 2:
                            dve.wait_ge(s["products"], gi - 1)
                        else:
                            dve.wait_ge(s["products"], w * NG)
                        nums = k["numbers"][:, :, 0:n]
                        one = nc.vector.tensor_tensor(soh[b][:, :, :], nums, keys[:, 0, None, lo:lo + n].to_broadcast(shape), ALU.is_equal)
                        one.then_inc(s["onehot"], 1)
                        nc.vector.tensor_tensor(doh[b][:, :, :], nums, keys[:, 1, None, lo:lo + n].to_broadcast(shape),
                                                ALU.is_equal).then_inc(s["onehot"], 1)
                        dve.wait_ge(s["onehot"], gi * 8 + 1)
                        for q in range(6):
                            nc.vector.tensor_tensor(wsrc[b][:, q, :, :], soh[b][:, :, :],
                                                    parts[:, q // 2, q % 2, None, lo:lo + n].to_broadcast(shape),
                                                    ALU.mult).then_inc(s["onehot"], 1)
                    if g >= 1:
                        h = g - 1
                        hb, hn, hi = h % 2, GROUPS[h], w * NG + h
                        for i in range(hn):
                            d = FIRST[h] + i
                            ins = nc.vector.tensor_scalar(rden[:, hb, i, :], rn_row[:, bass.ds(row * W, W)], rnD[:, d:d + 1],
                                                          1e8, ALU.mult, ALU.min)
                            ins.then_inc(s["factor"], 1)
                        dve.wait_ge(s["factor"], w * NB + FIRST[h] + hn)
                        dve.wait_ge(s["signed"], hi + 1)
                        nc.vector.tensor_tensor(fac[:, hb, 0:hn, :], pos_s[:, hb, 0:hn, :], rden[:, hb, 0:hn, :], ALU.mult).then_inc(s["scaled"], 1)
                        dve.wait_ge(s["scaled"], hi + 1)
                        if h >= 2:
                            dve.wait_ge(s["used"], hi - 1)
                        else:
                            dve.wait_ge(s["used"], w * NG)
                        dve.wait_ge(s["freed_act"], 4 * hi + 4)
                        nc.vector.tensor_tensor(b0[:, hb, 0:hn, :], fac[:, hb, 0:hn, :], bank(h, 256, W, W), ALU.mult).then_inc(s["blocks"], 1)
                dve.wait_ge(s["used"], (w + 1) * NG)
                p_row = prop[:, bass.ds(row, 1), :].rearrange("p a f -> p (a f)")
                nc.vector.tensor_tensor(p_row, p_row, ps[0:W, SELF_BANK, 0:F], ALU.add).then_inc(s["row_read"], 1)
                c_row = cnt[:, bass.ds(row, 1)]
                nc.vector.tensor_tensor(c_row, c_row, ps[0:W, SELF_BANK, F:F + 1], ALU.add).then_inc(s["row_read"], 1)
                dve.wait_ge(s["row_read"], 2 * w + 2)
            dve.wait_ge(s["kbase"], 1)
            nc.vector.memset(sbase[:], 0.0).then_inc(s["taken"], 1)
            dve.wait_ge(s["taken"], 1)
            plan(dve, body)
            nc.vector.tensor_copy(deg[:], ps[0:W, DEG_BANK, 0:NB]).then_inc(s["zero"], 1)
            dve.wait_ge(s["zero"], 1)

        @block.scalar
        def _(act):
            def body(row, w, more, r=0):
                for g in range(NG):
                    b, n, gi = g % 2, GROUPS[g], w * NG + g
                    act.wait_ge(s["products"], gi + 1)
                    if g >= 2:
                        act.wait_ge(s["signed"], gi - 1)
                    else:
                        act.wait_ge(s["signed"], w * NG)
                    if g >= 2:
                        act.wait_ge(s["scaled"], gi - 1)
                    else:
                        act.wait_ge(s["scaled"], w * NG)
                    nc.scalar.activation(pos_s[:, b, 0:n, :], bank(g, 384, W, W), ACT.Relu, scale=coef[0:W, 0:1]).then_inc(s["freed_act"], 1)
                    nc.scalar.activation(neg_s[:, b, 0:n, :], bank(g, 384, W, W), ACT.Relu, scale=coef[0:W, 1:2]).then_inc(s["freed_act"], 1)
                    if more:
                        act.wait_ge(s_st[b], NB * 5 * 32)
                        act.wait_ge(s_add[b], ((w - NB) * 5 + g // 2) * 32)
                    else:
                        act.wait_ge(s_st[b], (w * 5 + g // 2) * 32)
                    nc.scalar.activation(out_c[:, b, 0:n, :], bank(g, 0, W), ACT.Copy).then_inc(s["freed_act"], 1)
                    nc.scalar.activation(out_g[:, b, 0:n, :], bank(g, 128, W), ACT.Copy).then_inc(s["freed_act"], 1)
                    if not more:
                        act.wait_ge(s["freed_act"], 4 * gi + 4)
                        for buf, dram in ((out_c, c_dram), (out_g, g_dram)):
                            act.dma_start(dram[bass.ds(row * P, P), FIRST[g] * W:(FIRST[g] + n) * W],
                                          buf[:, b, 0:n, :].rearrange("p n w -> p (n w)")).then_inc(s_st[b], 16)
            plan(act, body)
            for b in range(2):
                act.wait_ge(s_st[b], NB * 5 * 32)

        @block.gpsimd
        def _(pool):
            nc.gpsimd.iota(dbase[:, :, :], [[W, NB], [0, CAP]], base=0, channel_multiplier=0,
                           allow_small_or_imprecise_dtypes=True).then_inc(s["kbase"], 1)

            def body(row, w, more, r=0):
                for g in range(NG):
                    b, n, gi = g % 2, GROUPS[g], w * NG + g
                    pool.wait_ge(s["freed_act"], 4 * gi + 2)
                    nc.gpsimd.tensor_tensor(pos_s[:, b, 0:n, :], pos_s[:, b, 0:n, :], neg_s[:, b, 0:n, :],
                                            ALU.subtract).then_inc(s["signed"], 1)
                    if more:
                        freed = pool.snap(4 * gi + 4)
                        pool.wait_ge(s_st[0], NB * 5 * 32)
                        pool.wait_ge(s_st[1], NB * 5 * 32)
                        pool.wait_ge(s["freed_act"], freed)
                        for buf, dram in ((out_c, c_dram), (out_g, g_dram)):
                            pool.dma_start(dram[bass.ds(row * P, P), FIRST[g] * W:(FIRST[g] + n) * W],
                                           buf[:, b, 0:n, :].rearrange("p n w -> p (n w)"),
                                           accum_op=ALU.add).then_inc(s_add[b], 16)
                        pool.wait_ge(s_add[b], ((w - NB) * 5 + g // 2 + 1) * 32)
            plan(pool, body)

        @block.tensor
        def _(pe):
            def mm(out, lhsT, rhs, start=False):
                return nc.tensor.matmul(out, lhsT, rhs, start=start, stop=True, skip_group_check=True)

            def propagate(w, g):
                pe.wait_ge(s["blocks"], w * NG + g + 1)
                for i in range(GROUPS[g]):
                    ins = mm(ps[0:W, SELF_BANK, 0:F], b0[:, g % 2, i, :], whD[:, FIRST[g] + i, :])
                ins.then_inc(s["used"], 1)
                return ins

            def body(row, w, more, r=0):
                pe.wait_ge(s["row_read"], 2 * w)
                mm(ps[:, SELF_BANK, 0:F + 1], k["zeros"][:, 0:P], k["zeros"][:, 0:F + 1], True)
                for g in range(NG):
                    b, n, gi = g % 2, GROUPS[g], w * NG + g
                    pe.wait_ge(s["blocks"], gi - 1 if g >= 2 else w * NG)
                    pe.wait_ge(s["freed_act"], 4 * gi - 4 if g >= 2 else w * (4 * NG))
                    mm(ps[:, BANKS[b][0], 0:2], k["zeros16"][:], k["zeros16"][:, 0:2], True)
                    for i in range(n):
                        bk, d = BANKS[b][i], FIRST[g] + i
                        mm(ps[0:W, bk, 384:384 + W], whT[:, d * W:d * W + W], whTs[:, bass.ds(row, 1), :], i > 0)
                    pe.wait_ge(s["onehot"], 8 * gi + 8)
                    for i in range(n):
                        bk, d = BANKS[b][i], FIRST[g] + i
                        out_ga = ps[:, bk, 128:384].rearrange("p (v w) -> p v w", v=2)[:, :, 0:W]
                        for j in range(CAP):
                            cc = CAP * i + j
                            for q in range(3):
                                mm(out_ga, doh[b][:, :, cc], wsrc[b][:, 2 * q:2 * q + 2, 0:W, cc])
                            mm(ps[:, DEG_BANK, d:d + 1], doh[b][:, :, cc], inside[:, 0, CAP * d + j:CAP * d + j + 1])
                            mm(ps[:, bk, 0:W], soh[b][:, :, cc], doh[b][:, 0:W, cc])
                            ins = mm(ps[:, SELF_BANK, F:F + 1], soh[b][:, :, cc], inside[:, 1, CAP * d + j:CAP * d + j + 1])
                    ins.then_inc(s["products"], 1)
                    if g >= 1:
                        propagate(w, g - 1)
                propagate(w, NG - 1)
            mm(ps[:, DEG_BANK, 0:NB], k["zeros"][:, 0:P], k["zeros"][:, 0:NB], True)
            plan(pe, body)


def product_c(nc, name, k, c_dram, u, y):
    NBK = 8
    with Mem(nc, name) as l:
        rows = [l.sb(f"row{b}", [P, N]) for b in range(2)]
        ps = l.ps("ps", [W, 4, NBK * F])
        s_in, s_pe = [l.sem("in0"), l.sem("in1")], [l.sem("pe0"), l.sem("pe1")]
        s_end, s_y = l.sem("end"), l.sem("y")
        block = l.block()
        pairs = NB // 2

        @block.sync
        def _(sp):
            def load(b, row, i):
                sp.wait_ge(s_pe[b], i)
                sp.dma_start(rows[b][:, :], c_dram[bass.ds(row * P, P), :]).then_inc(s_in[b], 16)

            with sp.Fori(0, pairs) as i:
                load(0, 2 * i, i)
                load(1, 2 * i + 1, i)
            load(0, NB - 1, pairs)

        @block.tensor
        def _(pe):
            def mm(out, lhsT, rhs, start=False):
                return nc.tensor.matmul(out, lhsT, rhs, start=start, stop=True, skip_group_check=True)

            def use(b, row, i):
                pe.wait_ge(s_in[b], 16 * i + 16)
                for d in range(NB):
                    ins = mm(ps[:, d // NBK, d % NBK * F:d % NBK * F + F], rows[b][0:W, d * W:d * W + W],
                             u[:, bass.ds(row, 1), :])
                return ins

            for q in range(4):
                mm(ps[:, q, :], k["zeros"][0:W, 0:W], k["zeros"][0:W, :], True)
            with pe.Fori(0, pairs) as i:
                use(0, 2 * i, i).then_inc(s_pe[0], 1)
                use(1, 2 * i + 1, i).then_inc(s_pe[1], 1)
            use(0, NB - 1, pairs).then_inc(s_end, 1)

        @block.vector
        def _(dve):
            dve.wait_ge(s_end, 1)
            for q in range(4):
                n = min(NBK, NB - NBK * q)
                nc.vector.tensor_copy(y[:, NBK * q:NBK * q + n, :],
                                      ps[:, q, 0:n * F].rearrange("p (n f) -> p n f", f=F)).then_inc(s_y, 1)
            dve.wait_ge(s_y, 4)


def product_g(nc, name, g_dram, u, y):
    with Mem(nc, name) as l:
        rows = [l.sb(f"row{b}", [P, N]) for b in range(2)]
        ps = l.ps("ps", [W, 2, 512])
        s_in, s_pe, s_y = [l.sem("in0"), l.sem("in1")], [l.sem("pe0"), l.sem("pe1")], [l.sem("y0"), l.sem("y1")]
        block = l.block()
        pairs = NB // 2

        def plan(eng, step):
            with eng.Fori(0, pairs) as i:
                step(0, 2 * i, i)
                step(1, 2 * i + 1, i)
            step(0, NB - 1, pairs)

        @block.sync
        def _(sp):
            def load(b, row, i):
                sp.wait_ge(s_pe[b], i)
                sp.dma_start(rows[b][:, :], g_dram[bass.ds(row * P, P), :]).then_inc(s_in[b], 16)
            plan(sp, load)

        @block.tensor
        def _(pe):
            def use(b, row, i):
                pe.wait_ge(s_in[b], 16 * i + 16)
                pe.wait_ge(s_y[b], i)
                for d in range(NB):
                    ins = nc.tensor.matmul(ps[:, b, 0:F], rows[b][0:W, d * W:d * W + W], u[:, d, :],
                                           start=d == 0, stop=d == NB - 1)
                ins.then_inc(s_pe[b], 1)
            plan(pe, use)

        @block.vector
        def _(dve):
            def read(b, row, i):
                dve.wait_ge(s_pe[b], i + 1)
                nc.vector.tensor_copy(y[:, bass.ds(row, 1), :], ps[:, b:b + 1, 0:F]).then_inc(s_y[b], 1)
            plan(dve, read)
            dve.wait_ge(s_y[0], pairs + 1)
            dve.wait_ge(s_y[1], pairs)


def chain_block(nc, name, steps):
    with Mem(nc, name) as l:
        s = l.sem("s")
        block = l.block()

        @block.vector
        def _(dve):
            for n, (eng, f) in enumerate(steps):
                if eng == "v":
                    dve.wait_ge(s, n)
                    f().then_inc(s, 1)
            dve.wait_ge(s, len(steps))

        @block.scalar
        def _(act):
            for n, (eng, f) in enumerate(steps):
                if eng == "a":
                    act.wait_ge(s, n)
                    f().then_inc(s, 1)


def four_layers(nc, x, src, dst, edge_attr_16, edge_weight, edge_weight_n2, L0_gnn_W, L0_gnn_b, L0_gnn_deg_coeff,
                L0_gnn_coeff_param, L0_gnn_scale_param, L2_gnn_W1, L2_gnn_b1, L2_gnn_W2, L2_gnn_b2,
                L3_gnn_W_edge, L3_gnn_b_edge, L3_gnn_W_node, L3_gnn_b_node, out):
    v = nc.vector
    by_dst_dram = nc.dram_tensor("by_dst", [EP, 4], F32).ap()
    by_both_dram = nc.dram_tensor("by_both", [R2_ROWS, 4], F32).ap()
    c_dram = nc.dram_tensor("c_blocks", [NB * P, N], F32).ap()
    g_dram = nc.dram_tensor("g_blocks", [NB * P, N], F32).ap()
    hist_dram = nc.dram_tensor("hist", [P, P], F32).ap()
    rn_dram = nc.dram_tensor("rn", [N], F32).ap()
    vec_dram = nc.dram_tensor("vec", [N], F32).ap()
    turn = [nc.dram_tensor(f"turn{i}", [N, F], F32).ap() for i in range(6)]

    with Mem(nc, "k") as top:
        k = {
            "ident": top.sb("ident", [P, P]), "before": top.sb("before", [P, P]), "ones": top.sb("ones", [P, P]),
            "ones16": top.sb("ones16", [P, 2], BF16), "zeros": top.sb("zeros", [P, 512]),
            "zeros16": top.sb("zeros16", [P, P], BF16),
            "numbers": top.sb("numbers", [P, P, CAP * max(GROUPS)], BF16), "codes": top.sb("codes", [P, NB]),
        }
        table = top.sb("table", [1, NB * NB + 7], I32)
        deg, cnt = top.sb("deg", [W, NB]), top.sb("cnt", [W, NB])
        xS = top.sb("xS", [W, NB, F])
        prop = top.sb("prop", [W, NB, F])
        coef = top.sb("coef", [P, 3])
        constants(nc, top, k)
        sentinels(nc, by_both_dram)

        with Mem(nc, "sort") as m:
            rec = m.sb("rec", [P, T, 4])
            edge_records(nc, rec, src, dst, edge_attr_16, edge_weight, edge_weight_n2, L0_gnn_deg_coeff,
                         L3_gnn_W_edge, L3_gnn_b_edge)
            pos = m.sb("pos", [P, T])
            by_dst = m.sb("by_dst_m", [P, 32, TQ], BF16)
            ranks(nc, "rank_d", k, rec, 1, 1.0 / W, by_dst, pos, W // 2)
            scatter(nc, "scat_d", k, rec, pos, by_dst_dram)
            reload(nc, "load_d", rec, by_dst_dram)
            by_src = m.sb("by_src_m", [P, 32, TQ], BF16)
            ranks(nc, "rank_s", k, rec, 0, 1.0 / CODE, by_src, pos, W // 2)
            scatter(nc, "scat_s", k, rec, pos, by_both_dram)
            key_masks(nc, rec, 1, 1.0 / W, by_dst, W // 2)
            bucket_table(nc, by_src, by_dst, hist_dram, table)

        whS = top.sb("whS", [W, NB, F])
        with Mem(nc, "l0") as m:
            xD, hD = m.sb("xD", [W, NB, F]), m.sb("hD", [W, NB, F])
            hT, whT = m.sb("hT", [F, N]), m.sb("whT", [F, N])
            whTs = m.sb("whTs", [F, NB, W])
            whD = m.sb("whD", [W, NB, F])
            rnD, rnS, rn_row = m.sb("rnD", [W, NB]), m.sb("rnS", [W, NB]), m.sb("rn_row", [W, N])
            w0, b_row, b_col = m.sb("w0", [F, F]), m.sb("b_row", [W, F]), m.sb("b_col", [F, 1])
            copy_dma(nc, "in0", [
                (xD[:, :, :], d_layout(x)), (xS[:, :, :], s_layout(x)), (w0[:], L0_gnn_W),
                (b_row[:], L0_gnn_b.rearrange("(a n) -> a n", a=1).to_broadcast([W, F])),
                (b_col[:], L0_gnn_b.rearrange("(n a) -> n a", a=1))])
            coefficients(nc, L0_gnn_coeff_param, L0_gnn_scale_param, coef)
            layer_norm_relu(nc, "ln0", xD, hD)
            transpose_nodes(nc, "tr0", k, hD, hT)
            dense_T(nc, "whT", w0[:], hT, whT, b_col[:], False)
            dense(nc, "whD", lambda b: hT[:, b * W:b * W + W], w0[:], whD, b_row)
            dense(nc, "whS", lambda b: hT[:, b:N:NB], w0[:], whS, b_row)
            inverse_norms(nc, "rnD", whD, rnD)
            inverse_norms(nc, "rnS", whS, rnS)
            copy_dma(nc, "rnrow", [
                (rn_dram.rearrange("(s i) -> i s", s=NB), rnS[:]),
                (rn_row[:], rn_dram.rearrange("(a n) -> a n", a=1).to_broadcast([W, N]))])
            chain_block(nc, "whTs", [
                ("v", lambda: v.tensor_copy(whTs[:, :, :], whT[:].rearrange("f (i s) -> f s i", s=NB))),
                ("v", lambda: v.memset(prop[:, :, :], 0.0)),
                ("v", lambda: v.memset(cnt[:], 0.0))])
            build_rows(nc, k, by_both_dram, table, whT, whTs, whD, rnD, rn_row, coef, prop, cnt, deg, c_dram, g_dram)

        with Mem(nc, "l1") as m:
            full = [W, NB, F]
            xD, hD, hS, u, y, acc = (m.sb(n, full) for n in ("xD", "hD", "hS", "u", "y", "acc"))
            dis, disS, dis2, t = (m.sb(n, [W, NB]) for n in ("dis", "disS", "dis2", "t"))
            wide = lambda a: a[:, :, None].to_broadcast(full)

            chain_block(nc, "x1", [
                ("v", lambda: v.tensor_tensor(xS[:, :, :], xS[:, :, :], prop[:, :, :], ALU.add)),
                ("v", lambda: v.scalar_tensor_tensor(xS[:, :, :], whS[:, :, :], coef[0:W, 2:3], xS[:, :, :], ALU.mult, ALU.add)),
                ("v", lambda: v.tensor_scalar(t[:], deg[:], 1.0, None, ALU.max)),
                ("a", lambda: nc.scalar.activation(t[:], t[:], ACT.Sqrt)),
                ("v", lambda: v.reciprocal(dis[:], t[:])),
                ("v", lambda: v.tensor_scalar(t[:], deg[:], 0.0, None, ALU.is_gt)),
                ("v", lambda: v.tensor_tensor(dis[:], dis[:], t[:], ALU.mult)),
                ("v", lambda: v.tensor_tensor(dis2[:], dis[:], dis[:], ALU.mult))])
            copy_dma(nc, "turn0", [
                (s_layout(turn[0]), xS[:, :, :]), (xD[:, :, :], d_layout(turn[0])),
                (vec_dram.rearrange("(c p) -> p c", p=W), dis[:]), (disS[:], vec_dram.rearrange("(p c) -> p c", c=NB))])
            layer_norm_relu(nc, "ln1s", xS, hS)
            layer_norm_relu(nc, "ln1d", xD, hD)
            chain_block(nc, "u0", [
                ("v", lambda: v.tensor_tensor(u[:, :, :], hS[:, :, :], wide(disS), ALU.mult)),
                ("v", lambda: v.tensor_copy(acc[:, :, :], hD[:, :, :]))])
            for i in range(3):
                product_c(nc, f"gcn{i}", k, c_dram, u, y)
                chain_block(nc, f"acc{i}", [
                    ("v", lambda: v.tensor_tensor(hS[:, :, :], y[:, :, :], wide(dis), ALU.mult)),
                    ("v", lambda: v.tensor_tensor(acc[:, :, :], acc[:, :, :], hS[:, :, :], ALU.add)),
                    ("v", lambda: v.tensor_tensor(y[:, :, :], y[:, :, :], wide(dis2), ALU.mult))])
                if i < 2:
                    copy_dma(nc, f"turn{i + 1}", [(d_layout(turn[i + 1]), y[:, :, :]), (u[:, :, :], s_layout(turn[i + 1]))])
            chain_block(nc, "x2", [
                ("v", lambda: v.scalar_tensor_tensor(xD[:, :, :], acc[:, :, :], 0.25, xD[:, :, :], ALU.mult, ALU.add))])

            layer_norm_relu(nc, "ln2", xD, hD)
            copy_dma(nc, "turn3", [(d_layout(turn[3]), hD[:, :, :]), (u[:, :, :], s_layout(turn[3]))])
            product_c(nc, "gin", k, c_dram, u, y)
            with Mem(nc, "l2") as q:
                zT, z1T = q.sb("zT", [F, N]), q.sb("z1T", [F, N])
                w1, w2, b1, b2 = q.sb("w1", [F, F]), q.sb("w2", [F, F]), q.sb("b1", [F, 1]), q.sb("b2", [W, F])
                copy_dma(nc, "in2", [
                    (w1[:], L2_gnn_W1), (w2[:], L2_gnn_W2), (b1[:], L2_gnn_b1.rearrange("(n a) -> n a", a=1)),
                    (b2[:], L2_gnn_b2.rearrange("(a n) -> a n", a=1).to_broadcast([W, F]))])
                chain_block(nc, "z", [("v", lambda: v.tensor_tensor(y[:, :, :], y[:, :, :], hD[:, :, :], ALU.add))])
                transpose_nodes(nc, "tr2", k, y, zT)
                dense_T(nc, "z1", w1[:], zT, z1T, b1[:], True)
                dense(nc, "z2", lambda b: z1T[:, b * W:b * W + W], w2[:], y, b2, relu=True)
                chain_block(nc, "x3", [("v", lambda: v.tensor_tensor(xD[:, :, :], xD[:, :, :], y[:, :, :], ALU.add))])

            layer_norm_relu(nc, "ln3", xD, hD)
            copy_dma(nc, "turn4", [(d_layout(turn[4]), xD[:, :, :]), (xS[:, :, :], s_layout(turn[4]))])
            with Mem(nc, "l3") as q:
                hT = q.sb("hT", [F, N])
                wn, wnT, bn = q.sb("wn", [F, F]), q.sb("wnT", [F, F]), q.sb("bn", [W, F])
                wps = q.ps("wps", [F, F])
                copy_dma(nc, "in3", [(wn[:], L3_gnn_W_node),
                                     (bn[:], L3_gnn_b_node.rearrange("(a n) -> a n", a=1).to_broadcast([W, F]))])
                with Mem(nc, "wnT") as l:
                    s_t, s_c = l.sem("t"), l.sem("c")
                    block = l.block()

                    @block.tensor
                    def _(pe):
                        nc.tensor.transpose(wps[:], wn[:], k["ident"][0:F, 0:F]).then_inc(s_t, 1)

                    @block.vector
                    def _(dve):
                        dve.wait_ge(s_t, 1)
                        v.tensor_copy(wnT[:], wps[:]).then_inc(s_c, 1)
                        dve.wait_ge(s_c, 1)
                transpose_nodes(nc, "tr3", k, hD, hT)
                dense(nc, "xp", lambda b: hT[:, b * W:b * W + W], wnT[:], u, bn)
            product_g(nc, "gated", g_dram, u, y)
            chain_block(nc, "x4", [
                ("v", lambda: v.tensor_scalar(t[:], cnt[:], 1.0, None, ALU.max)),
                ("v", lambda: v.reciprocal(dis[:], t[:])),
                ("v", lambda: v.tensor_tensor(y[:, :, :], y[:, :, :], wide(dis), ALU.mult)),
                ("v", lambda: v.tensor_tensor(xS[:, :, :], xS[:, :, :], y[:, :, :], ALU.add))])
            copy_dma(nc, "end", [(s_layout(out), xS[:, :, :])])


_INS = ["x", "src", "dst", "edge_attr_16", "edge_weight", "edge_weight_n2", "L0_gnn_W", "L0_gnn_b", "L0_gnn_deg_coeff",
        "L0_gnn_coeff_param", "L0_gnn_scale_param", "L2_gnn_W1", "L2_gnn_b1", "L2_gnn_W2", "L2_gnn_b2",
        "L3_gnn_W_edge", "L3_gnn_b_edge", "L3_gnn_W_node", "L3_gnn_b_node"]


def kernel(**inputs):
    import numpy as _np
    import concourse.bacc as _bacc
    from concourse import mybir as _mybir
    from concourse.bass_utils import run_bass_kernel_spmd as _run

    nc = _bacc.Bacc("TRN2", target_bir_lowering=False, num_devices=1)
    arrays, args = {}, []
    for name in _INS:
        a = _np.ascontiguousarray(inputs[name])
        arrays[f"in_{name}"] = a
        args.append(nc.dram_tensor(f"in_{name}", a.shape, _mybir.dt.from_np(a.dtype), kind="ExternalInput").ap())
    args.append(nc.dram_tensor("out_x", (N, F), F32, kind="ExternalOutput").ap())
    four_layers(nc, *args)
    r = _run(nc, [arrays], core_ids=[0])
    return r.results[0]["out_x"]
```

```python
from contextlib import ExitStack, contextmanager

import concourse.bass as bass
from concourse import mybir

ALU = mybir.AluOpType
ACT = mybir.ActivationFunctionType
AX = mybir.AxisListType
F32 = mybir.dt.float32
BF16 = mybir.dt.bfloat16
I32 = mybir.dt.int32
U16 = mybir.dt.uint16

P = 128
N = 3125
F = 64
EA = 16
E = 103125
NB = 25
W = N // NB
T = -(-E // P)
EP = T * P
TAIL = E - (P - 1) * T
KEYS = NB + 1
STEP = -(-T // 4)
TQ = 4 * STEP
CODE = 256
CAP = 2
ROUND = CAP * P
HALF = 31
LOOPS = T // (2 * HALF)
MAGIC = 12582912.0
GROUPS = [3, 2] * 5
BANKS = [[0, 1, 2], [3, 4]]
SELF_BANK, DEG_BANK = 5, 6
SENT_COLS = 81
R2_ROWS = 2 * EP + 10 * P
assert 2 * HALF * LOOPS == T and sum(GROUPS) == NB


class Chain:

    def __init__(self, eng, sem, start=0):
        self.eng, self.sem, self.n = eng, sem, start

    def __call__(self, ins):
        self.n += 1
        ins.then_inc(self.sem, 1)
        self.eng.wait_ge(self.sem, self.n)


class Running:
    sems = {}

    def __init__(self, name):
        self.name = name
        self.sem, self.start = Running.sems[name]

    def at(self, n):
        return self.start + n

    def close(self, n):
        Running.sems[self.name] = (self.sem, self.start + n)


class Mem:

    def __init__(self, nc, name):
        self.nc, self.name, self.ctx = nc, name, ExitStack()

    def __enter__(self):
        return self

    def __exit__(self, *a):
        return self.ctx.__exit__(*a)

    def sb(self, name, shape, dt=F32):
        return self.ctx.enter_context(self.nc.sbuf_tensor(f"{self.name}_{name}", shape, dt))

    def ps(self, name, shape, dt=F32):
        return self.ctx.enter_context(self.nc.psum_tensor(f"{self.name}_{name}", shape, dt))

    def sem(self, name):
        return self.ctx.enter_context(self.nc.semaphore(f"{self.name}_{name}"))

    def block(self):
        return self.ctx.enter_context(self.nc.Block())


def constants(nc, m, k):
    with Mem(nc, "const") as l:
        col = l.sb("col", [P, P])
        row = l.sb("row", [P, 1])
        s_iota, s_c = l.sem("iota"), l.sem("c")
        block = l.block()

        @block.gpsimd
        def _(pool):
            nc.gpsimd.iota(col[:], [[1, P]], base=0, channel_multiplier=0,
                           allow_small_or_imprecise_dtypes=True).then_inc(s_iota, 1)
            nc.gpsimd.iota(row[:], [[1, 1]], base=0, channel_multiplier=1,
                           allow_small_or_imprecise_dtypes=True).then_inc(s_iota, 1)
            nc.gpsimd.iota(k["codes"][:], [[CODE, NB]], base=0, channel_multiplier=0,
                           allow_small_or_imprecise_dtypes=True).then_inc(s_iota, 1)
            nc.gpsimd.iota(k["numbers"][:, :, :], [[1, P], [0, CAP * max(GROUPS)]], base=0,
                           channel_multiplier=0,
                           allow_small_or_imprecise_dtypes=True).then_inc(s_iota, 1)

        @block.vector
        def _(dve):
            dve.wait_ge(s_iota, 4)
            nc.vector.tensor_scalar(k["ident"][:], col[:], row[:], None, ALU.is_equal).then_inc(s_c, 1)
            nc.vector.tensor_scalar(k["before"][:], col[:], row[:], None, ALU.is_gt).then_inc(s_c, 1)
            nc.vector.memset(k["ones"][:], 1.0).then_inc(s_c, 1)
            nc.vector.memset(k["ones16"][:], 1.0).then_inc(s_c, 1)
            nc.vector.memset(k["zeros"][:], 0.0).then_inc(s_c, 1)
            nc.vector.memset(k["zeros16"][:], 0.0).then_inc(s_c, 1)
            dve.wait_ge(s_c, 6)


def edge_records(nc, rec, src, dst, edge_attr, ew, ewn2, coeff, w_edge, b_edge):
    last = slice(96, P)
    with Mem(nc, "edges") as l:
        srci, dsti = l.sb("srci", [P, T], I32), l.sb("dsti", [P, T], I32)
        adj, deg = l.sb("adj", [P, T]), l.sb("deg", [P, T])
        attr, prod = l.sb("attr", [P, T, EA]), l.sb("prod", [P, T, EA])
        cf, we, be = l.sb("cf", [P, 2]), l.sb("we", [P, EA]), l.sb("be", [P, 1])
        sf, df, q, t1 = (l.sb(x, [P, T]) for x in ("sf", "df", "q", "t1"))
        x, ax, ex, u, lg = (l.sb(y, [P, T]) for y in ("x", "ax", "ex", "u", "lg"))
        z = l.sb("z", [P, T])
        pad = l.sb("pad", [P, T - TAIL])
        s_zero, s_i, s_w, s_a, s_p = (l.sem(y) for y in ("zero", "i", "w", "a", "p"))
        s_dve, s_act, s_pad = l.sem("dve"), l.sem("act"), l.sem("pad")
        block = l.block()

        def load(eng, tile, dram, sem):
            eng.dma_start(tile[0:P - 1, :], dram[0:(P - 1) * T].rearrange("(p t) -> p t", t=T)).then_inc(sem, 16)
            eng.dma_start(tile[P - 1:P, 0:TAIL], dram[(P - 1) * T:E].rearrange("(p t) -> p t", p=1)).then_inc(sem, 16)

        @block.sync
        def _(sp):
            sp.wait_ge(s_zero, 5)
            load(sp, srci, src, s_i)
            load(sp, dsti, dst, s_i)
            sp.dma_start(attr[0:P - 1, :, :], edge_attr[0:(P - 1) * T, :].rearrange("(p t) a -> p t a", t=T)).then_inc(s_a, 16)
            sp.dma_start(attr[P - 1:P, 0:TAIL, :], edge_attr[(P - 1) * T:E, :].rearrange("(p t) a -> p t a", p=1)).then_inc(s_a, 16)

        @block.scalar
        def _(act):
            act.dma_start(cf[:], coeff.rearrange("(a n) -> a n", a=1).to_broadcast([P, 2])).then_inc(s_p, 16)
            act.dma_start(we[:], w_edge.rearrange("a b -> b a").to_broadcast([P, EA])).then_inc(s_p, 16)
            act.dma_start(be[:], b_edge.rearrange("(a n) -> a n", a=1).to_broadcast([P, 1])).then_inc(s_p, 16)
            act.wait_ge(s_zero, 5)
            load(act, adj, ew, s_w)
            load(act, deg, ewn2, s_w)
            act.wait_ge(s_dve, 2)
            nc.scalar.activation(ex[:], ax[:], ACT.Exp, scale=-1.0).then_inc(s_act, 1)
            act.wait_ge(s_dve, 3)
            nc.scalar.activation(lg[:], u[:], ACT.Ln).then_inc(s_act, 1)
            act.wait_ge(s_dve, 10)
            nc.scalar.activation(rec[:, :, 2], z[:], ACT.Sigmoid, bias=be[:]).then_inc(s_act, 1)

        @block.gpsimd
        def _(pool):
            nc.gpsimd.iota(pad[:], [[1, T - TAIL]], base=TAIL, channel_multiplier=T,
                           allow_small_or_imprecise_dtypes=True).then_inc(s_pad, 1)

        @block.vector
        def _(dve):
            nc.vector.memset(srci[last, TAIL:T], 0).then_inc(s_zero, 1)
            nc.vector.memset(dsti[last, TAIL:T], 0).then_inc(s_zero, 1)
            nc.vector.memset(adj[last, TAIL:T], 0.0).then_inc(s_zero, 1)
            nc.vector.memset(deg[last, TAIL:T], 0.0).then_inc(s_zero, 1)
            nc.vector.memset(attr[last, TAIL:T, :], 0.0).then_inc(s_zero, 1)
            c = Chain(dve, s_dve)
            dve.wait_ge(s_p, 48)
            dve.wait_ge(s_w, 64)
            c(nc.vector.tensor_scalar(x[:], deg[:], cf[:, 0:1], cf[:, 1:2], ALU.mult, ALU.add))
            c(nc.vector.scalar_tensor_tensor(ax[:], x[:], -1.0, x[:], ALU.mult, ALU.max))
            dve.wait_ge(s_act, 1)
            c(nc.vector.tensor_scalar(u[:], ex[:], 1.0, None, ALU.add))
            c(nc.vector.tensor_scalar(q[:], u[:], -1.0, None, ALU.add))
            c(nc.vector.tensor_scalar(t1[:], q[:], 0.0, None, ALU.is_equal))
            c(nc.vector.tensor_tensor(q[:], q[:], t1[:], ALU.add))
            c(nc.vector.reciprocal(sf[:], q[:]))
            c(nc.vector.tensor_tensor(df[:], sf[:], ex[:], ALU.mult))
            dve.wait_ge(s_a, 32)
            c(nc.vector.tensor_tensor(prod[:, :, :], attr[:, :, :], we[:, None, :].to_broadcast([P, T, EA]), ALU.mult))
            c(nc.vector.tensor_reduce(z[:], prod[:, :, :], AX.X, ALU.add))
            dve.wait_ge(s_act, 2)
            c(nc.vector.tensor_tensor(lg[:], lg[:], t1[:], ALU.add))
            c(nc.vector.tensor_tensor(lg[:], lg[:], df[:], ALU.mult))
            c(nc.vector.scalar_tensor_tensor(lg[:], x[:], 0.0, lg[:], ALU.max, ALU.add))
            c(nc.vector.tensor_tensor(lg[:], lg[:], adj[:], ALU.mult))
            dve.wait_ge(s_i, 64)
            c(nc.vector.tensor_copy(sf[:], srci[:]))
            c(nc.vector.tensor_copy(df[:], dsti[:]))
            c(nc.vector.tensor_tensor(t1[:], sf[:], df[:], ALU.not_equal))
            c(nc.vector.tensor_tensor(rec[:, :, 3], lg[:], t1[:], ALU.mult))
            c(nc.vector.tensor_scalar(q[:], sf[:], -float(NB // 2), 1.0 / NB, ALU.add, ALU.mult))
            c(nc.vector.tensor_scalar(q[:], q[:], MAGIC, -MAGIC, ALU.add, ALU.add))
            c(nc.vector.tensor_scalar(t1[:], sf[:], float(CODE), None, ALU.mult))
            c(nc.vector.scalar_tensor_tensor(rec[:, :, 0], q[:], float(1 - CODE * NB), t1[:], ALU.mult, ALU.add))
            c(nc.vector.tensor_copy(rec[:, :, 1], df[:]))
            dve.wait_ge(s_pad, 1)
            c(nc.vector.tensor_scalar(pad[:], pad[:], float(E), None, ALU.is_ge))
            c(nc.vector.scalar_tensor_tensor(rec[:, TAIL:T, 0], pad[:], float(CODE * NB), rec[:, TAIL:T, 0], ALU.mult, ALU.add))
            c(nc.vector.scalar_tensor_tensor(rec[:, TAIL:T, 1], pad[:], float(N), rec[:, TAIL:T, 1], ALU.mult, ALU.add))
            dve.wait_ge(s_act, 3)


def mask_steps(nc, dve, c, sem, rec, field, inv, half, masks, key):
    c(nc.vector.memset(masks[:, :, :], 0.0))
    c(nc.vector.tensor_scalar(key[:], rec[:, :, field], -float(half), inv, ALU.add, ALU.mult))
    c(nc.vector.tensor_scalar(key[:], key[:], MAGIC, -MAGIC, ALU.add, ALU.add))
    for j in range(KEYS):
        nc.vector.tensor_scalar(masks[:, j, 0:T], key[:], float(j), None, ALU.is_equal).then_inc(sem, 1)
    c.n += KEYS
    dve.wait_ge(sem, c.n)


def key_masks(nc, rec, field, inv, masks, half):
    with Mem(nc, "masks") as l:
        key, s = l.sb("key", [P, T]), l.sem("s")
        block = l.block()

        @block.vector
        def _(dve):
            mask_steps(nc, dve, Chain(dve, s), s, rec, field, inv, half, masks, key)


@contextmanager
def only_if(eng, flag):
    if flag is None:
        yield
    else:
        with eng.If(eng.value_load(flag, min_val=0, max_val=1) > 0):
            yield


def order_check(nc, k, rec, flag):
    with Mem(nc, "order") as l:
        key, falls = l.sb("key", [P, T]), l.sb("falls", [P, T])
        total = l.sb("total", [P, 2])
        ps = l.ps("ps", [P, 2, 512])
        s_dve, s_pe = l.sem("dve"), l.sem("pe")
        block = l.block()

        @block.vector
        def _(dve):
            c = Chain(dve, s_dve)
            c(nc.vector.tensor_scalar(key[:], rec[:, :, 1], -float(W // 2), 1.0 / W, ALU.add, ALU.mult))
            c(nc.vector.tensor_scalar(key[:], key[:], MAGIC, -MAGIC, ALU.add, ALU.add))
            c(nc.vector.tensor_tensor(falls[:, 0:T - 1], key[:, 0:T - 1], key[:, 1:T], ALU.is_gt))
            c(nc.vector.memset(falls[:, T - 1:T], 0.0))
            dve.wait_ge(s_pe, 1)
            c(nc.vector.tensor_tensor(falls[0:P - 1, T - 1:T], key[0:P - 1, T - 1:T], ps[0:P - 1, 0, 0:1], ALU.is_gt))
            c(nc.vector.tensor_reduce(total[:, 0:1], falls[:], AX.X, ALU.add))
            dve.wait_ge(s_pe, 2)
            c(nc.vector.tensor_scalar(total[:, 1:2], ps[:, 1, 0:1], 1.0, None, ALU.min))
            c(nc.vector.tensor_copy(flag, total[0:1, 1:2]))

        @block.tensor
        def _(pe):
            pe.wait_ge(s_dve, 2)
            nc.tensor.matmul(ps[0:P - 1, 0, 0:1], k["ident"][:, 1:P], key[:, 0:1], start=True, stop=True).then_inc(s_pe, 1)
            pe.wait_ge(s_dve, 6)
            nc.tensor.matmul(ps[:, 1, 0:1], k["ones"][:], total[:, 0:1], start=True, stop=True).then_inc(s_pe, 1)


def ranks(nc, name, k, rec, field, inv, masks, pos, half, flag=None):
    with Mem(nc, name) as l:
        key = l.sb("key", [P, T])
        cnt, off, tot, cum = (l.sb(x, [P, KEYS]) for x in ("cnt", "off", "tot", "cum"))
        run = l.sb("run", [P, 2, T])
        both = l.ps("both", [P, 2, 512])
        s_dve, s_pe = l.sem("dve"), l.sem("pe")
        block = l.block()
        n_cnt = [0]

        @block.vector
        def _(dve):
            with only_if(dve, flag):
                c = Chain(dve, s_dve)
                mask_steps(nc, dve, c, s_dve, rec, field, inv, half, masks, key)
                c(nc.vector.tensor_reduce(cnt[:], masks[:, 0:KEYS, 0:T], AX.X, ALU.add))
                n_cnt[0] = c.n
                dve.wait_ge(s_pe, 1)
                c(nc.vector.tensor_copy(tot[:], both[:, 1, 0:KEYS]))
                c(nc.vector.tensor_tensor_scan(cum[:], tot[:], tot[:], -1.0, ALU.add, ALU.bypass))
                c(nc.vector.tensor_tensor(cum[:], cum[:], tot[:], ALU.subtract))
                c(nc.vector.tensor_tensor(off[:], cum[:], both[:, 0, 0:KEYS], ALU.add))
                for j in range(KEYS):
                    c(nc.vector.tensor_tensor_scan(run[:, j % 2, :], masks[:, j, 0:T], masks[:, j, 0:T], off[:, j:j + 1],
                                                   ALU.add, ALU.bypass))
                    if j == 0:
                        c(nc.vector.tensor_copy(pos[:], run[:, 0, :]))
                    else:
                        c(nc.vector.copy_predicated(pos[:], masks[:, j, 0:T].bitcast(U16), run[:, j % 2, :]))

        @block.tensor
        def _(pe):
            with only_if(pe, flag):
                pe.wait_ge(s_dve, n_cnt[0])
                nc.tensor.matmul(both[:, 0, 0:KEYS], k["before"][:], cnt[:], start=True, stop=True)
                nc.tensor.matmul(both[:, 1, 0:KEYS], k["ones"][:], cnt[:], start=True, stop=True).then_inc(s_pe, 1)


def scatter(nc, name, k, rec, pos, out, flag=None):
    with Mem(nc, name) as l:
        at = l.sb("at", [P, 2, HALF], I32)
        what = l.sb("what", [P, 2, HALF, 4])
        s_staged = [l.sem("staged0"), l.sem("staged1")]
        s_out = [l.sem("out0"), l.sem("out1")]
        s_turn = [l.sem("turn0"), l.sem("turn1")]
        turn, k_one = l.sb("turn", [P, 2]), k["ones"]
        block = l.block()

        @block.vector
        def _(dve):
            with only_if(dve, flag):
                with dve.Fori(0, LOOPS) as i:
                    for h in range(2):
                        t = bass.ds((2 * i + h) * HALF, HALF)
                        dve.wait_ge(s_out[h], i * (16 * HALF))
                        nc.vector.tensor_copy(at[:, h, :], pos[:, t]).then_inc(s_staged[h], 1)
                        nc.vector.tensor_copy(what[:, h, :, :], rec[:, t, :]).then_inc(s_staged[h], 1)

        @block.gpsimd
        def _(pool):
            with only_if(pool, flag):
                with pool.Fori(0, LOOPS) as i:
                    for h in range(2):
                        pool.wait_ge(s_staged[h], 2 * i + 2)
                        pool.wait_ge(s_turn[h], i)
                        nc.gpsimd.tensor_tensor(turn[:, h:h + 1], k_one[:, 0:1], k_one[:, 0:1], ALU.add).then_inc(s_turn[h], 1)
                        for t in range(HALF):
                            pool.indirect_dma_start(out, bass.IndirectOffsetOnAxis(ap=at[:, h, t:t + 1], axis=0),
                                                    what[:, h, t, :], None).then_inc(s_out[h], 16)
                for h in range(2):
                    pool.wait_ge(s_out[h], 16 * HALF * LOOPS)


def reload(nc, name, rec, out, flag=None):
    with Mem(nc, name) as l:
        s = l.sem("s")
        block = l.block()

        @block.sync
        def _(sp):
            with only_if(sp, flag):
                sp.dma_start(rec[:, :, :], out[0:EP, :].rearrange("(p t) f -> p t f", p=P)).then_inc(s, 16)
                sp.wait_ge(s, 16)


def sentinels(nc, out):
    with Mem(nc, "sent") as l:
        tile = l.sb("tile", [P, SENT_COLS, 4])
        s_set, s_out = l.sem("set"), l.sem("out")
        block = l.block()

        @block.vector
        def _(dve):
            nc.vector.memset(tile[:, :, 0], float(CODE * NB)).then_inc(s_set, 1)
            nc.vector.memset(tile[:, :, 1], float(N)).then_inc(s_set, 1)
            nc.vector.memset(tile[:, :, 2:4], 0.0).then_inc(s_set, 1)

        @block.sync
        def _(sp):
            sp.wait_ge(s_set, 3)
            at, n = EP, 0
            while at < R2_ROWS:
                cols = min(SENT_COLS, (R2_ROWS - at) // P)
                sp.dma_start(out[at:at + P * cols, :].rearrange("(p t) f -> p t f", p=P), tile[:, 0:cols, :]).then_inc(s_out, 16)
                at += P * cols
                n += 16
            sp.wait_ge(s_out, n)


def bucket_table(nc, by_src, by_dst, hist_dram, table):
    Q = NB * NB
    with Mem(nc, "hist") as l:
        acc = l.ps("acc", [P, P])
        h = l.sb("h", [P, P])
        row, cum, st = l.sb("row", [1, 4, Q]), l.sb("cum", [1, Q]), l.sb("st", [1, Q])
        mx = l.sb("mx", [1, 4])
        s_pe, s_dve, s_io = l.sem("pe"), l.sem("dve"), l.sem("io")
        block = l.block()

        @block.tensor
        def _(pe):
            a = by_src.rearrange("p j (a t) -> p (j a) t", t=STEP)
            b = by_dst.rearrange("p j (a t) -> p (j a) t", t=STEP)

            def step(t, start=False, stop=False):
                return nc.tensor.matmul(acc[:], a[:, :, t], b[:, :, t], start=start, stop=stop)

            UN = 8
            loops = (STEP - 2) // UN
            step(0, start=True)
            with pe.Fori(0, loops) as i:
                for j in range(UN):
                    step(bass.ds(i * UN + (j + 1), 1))
            for t in range(1 + loops * UN, STEP - 1):
                step(t)
            step(STEP - 1, stop=True).then_inc(s_pe, 1)

        @block.vector
        def _(dve):
            c = Chain(dve, s_dve)
            dve.wait_ge(s_pe, 1)
            c(nc.vector.tensor_copy(h[:], acc[:]))
            dve.wait_ge(s_io, 80)
            for a in range(1, 4):
                c(nc.vector.tensor_tensor(row[:, 0, :], row[:, 0, :], row[:, a, :], ALU.add))
            c(nc.vector.tensor_tensor_scan(cum[:], row[:, 0, :], row[:, 0, :], 0.0, ALU.add, ALU.bypass))
            c(nc.vector.tensor_tensor(st[:], cum[:], row[:, 0, :], ALU.subtract))
            c(nc.vector.tensor_copy(table[0:1, 0:Q], st[:]))
            c(nc.vector.tensor_reduce(mx[:, 0:1], row[:, 0, :], AX.X, ALU.max))
            c(nc.vector.tensor_scalar(mx[:, 1:2], mx[:, 0:1], ROUND / 2 - 0.5, 1.0 / ROUND, ALU.add, ALU.mult))
            c(nc.vector.tensor_scalar(mx[:, 2:3], mx[:, 1:2], MAGIC, -MAGIC, ALU.add, ALU.add))
            c(nc.vector.tensor_copy(table[0:1, Q:Q + 1], mx[:, 2:3]))

        @block.sync
        def _(sp):
            sp.wait_ge(s_dve, 1)
            sp.dma_start(hist_dram, h[:]).then_inc(s_io, 16)
            sp.wait_ge(s_io, 16)
            view = hist_dram.rearrange("(s a) (d b) -> a s d b", a=4, b=4)
            for a in range(4):
                sp.dma_start(row[:, a, :].rearrange("p (s d) -> p s d", s=NB), view[a:a + 1, 0:NB, 0:NB, a],
                             allow_slow_non_contiguous=True).then_inc(s_io, 16)


def d_layout(dram):
    return dram.rearrange("(c p) f -> p c f", p=W)


def s_layout(dram):
    return dram.rearrange("(p c) f -> p c f", c=NB)


def copy_dma(nc, name, pairs):
    with Mem(nc, name) as l:
        moved = Running("moved")
        block = l.block()

        @block.sync
        def _(sp):
            for i, (out, in_) in enumerate(pairs):
                sp.dma_start(out, in_, allow_slow_non_contiguous=True).then_inc(moved.sem, 16)
                sp.wait_ge(moved.sem, moved.at(16 * (i + 1)))
        moved.close(16 * len(pairs))


def layer_norm_relu(nc, name, x, h, xc):
    with Mem(nc, name) as l:
        mean, var, std, inv = (l.sb(y, [W, NB]) for y in ("mean", "var", "std", "inv"))
        eps = l.sb("eps", [W, 1])
        r_dve, r_act = Running("norm_dve"), Running("norm_act")
        block = l.block()
        full = [W, NB, F]

        @block.vector
        def _(dve):
            c = Chain(dve, r_dve.sem, r_dve.start)
            c(nc.vector.memset(eps[:], 1e-5))
            c(nc.vector.tensor_reduce(mean[:], x[:, :, :], AX.X, ALU.add))
            c(nc.vector.tensor_scalar(mean[:], mean[:], 1.0 / F, None, ALU.mult))
            c(nc.vector.tensor_tensor(xc[:, :, :], x[:, :, :], mean[:, :, None].to_broadcast(full), ALU.subtract))
            c(nc.vector.tensor_tensor(h[:, :, :], xc[:, :, :], xc[:, :, :], ALU.mult))
            c(nc.vector.tensor_reduce(var[:], h[:, :, :], AX.X, ALU.add))
            dve.wait_ge(r_act.sem, r_act.at(1))
            c(nc.vector.reciprocal(inv[:], std[:]))
            c(nc.vector.scalar_tensor_tensor(h[:, :, :], xc[:, :, :], 0.0, inv[:, :, None].to_broadcast(full), ALU.max, ALU.mult))

        @block.scalar
        def _(act):
            act.wait_ge(r_dve.sem, r_dve.at(6))
            nc.scalar.activation(std[:], var[:], ACT.Sqrt, bias=eps[:], scale=1.0 / F).then_inc(r_act.sem, 1)
        r_dve.close(8)
        r_act.close(1)


def transpose_nodes(nc, name, k, h, hT):
    with Mem(nc, name) as l:
        ps = l.ps("ps", [F, 2, 512])
        r_pe, r_cp = Running("made"), Running("read_dve")
        block = l.block()
        lots = [list(range(b, min(b + 4, NB))) for b in range(0, NB, 4)]

        @block.tensor
        def _(pe):
            for i, lot in enumerate(lots):
                if i >= 2:
                    pe.wait_ge(r_cp.sem, r_cp.at(i - 1))
                for j, b in enumerate(lot):
                    ins = nc.tensor.transpose(ps[:, i % 2, W * j:W * j + W], h[:, b, :], k["ident"][0:W, 0:W])
                ins.then_inc(r_pe.sem, 1)

        @block.vector
        def _(dve):
            for i, lot in enumerate(lots):
                dve.wait_ge(r_pe.sem, r_pe.at(i + 1))
                w = W * len(lot)
                nc.vector.tensor_copy(hT[:, W * lot[0]:W * lot[0] + w], ps[:, i % 2, 0:w]).then_inc(r_cp.sem, 1)
        r_pe.close(len(lots))
        r_cp.close(len(lots))


def dense_T(nc, name, w, hT, out, bias, relu):
    with Mem(nc, name) as l:
        ps = l.ps("ps", [F, 2, 512])
        r_pe, r_cp = Running("made"), Running("read_act")
        block = l.block()
        cuts = [(a, min(500, N - a)) for a in range(0, N, 500)]

        @block.tensor
        def _(pe):
            for i, (a, n) in enumerate(cuts):
                if i >= 2:
                    pe.wait_ge(r_cp.sem, r_cp.at(i - 1))
                nc.tensor.matmul(ps[:, i % 2, 0:n], w, hT[:, a:a + n], start=True, stop=True).then_inc(r_pe.sem, 1)

        @block.scalar
        def _(act):
            for i, (a, n) in enumerate(cuts):
                act.wait_ge(r_pe.sem, r_pe.at(i + 1))
                nc.scalar.activation(out[:, a:a + n], ps[:, i % 2, 0:n], ACT.Relu if relu else ACT.Identity,
                                     bias=bias).then_inc(r_cp.sem, 1)
        r_pe.close(len(cuts))
        r_cp.close(len(cuts))


def dense(nc, name, cols, w, out, bias, relu=False):
    with Mem(nc, name) as l:
        ps = l.ps("ps", [W, 2, 8, F])
        r_pe, r_cp = Running("made"), Running("read_dve")
        block = l.block()
        lots = [list(range(b, min(b + 8, NB))) for b in range(0, NB, 8)]

        @block.tensor
        def _(pe):
            for i, lot in enumerate(lots):
                if i >= 2:
                    pe.wait_ge(r_cp.sem, r_cp.at((i - 1) * (1 + relu)))
                for j, b in enumerate(lot):
                    ins = nc.tensor.matmul(ps[:, i % 2, j, :], cols(b), w, start=True, stop=True)
                ins.then_inc(r_pe.sem, 1)

        @block.vector
        def _(dve):
            n = 0
            for i, lot in enumerate(lots):
                dve.wait_ge(r_pe.sem, r_pe.at(i + 1))
                part = out[:, lot[0]:lot[0] + len(lot), :]
                nc.vector.tensor_tensor(part, ps[:, i % 2, 0:len(lot), :],
                                        bias[0:W, None, :].to_broadcast([W, len(lot), F]), ALU.add).then_inc(r_cp.sem, 1)
                if relu:
                    n += 2
                    dve.wait_ge(r_cp.sem, r_cp.at(n - 1))
                    nc.vector.tensor_scalar(part, part, 0.0, None, ALU.max).then_inc(r_cp.sem, 1)
        r_pe.close(len(lots))
        r_cp.close(len(lots) * (1 + relu))


def inverse_norms(nc, name, wh, rn):
    with Mem(nc, name) as l:
        sq = l.sb("sq", [W, NB, F])
        ss = l.sb("ss", [W, NB])
        nr = l.sb("nr", [W, NB])
        s_dve, s_act = l.sem("dve"), l.sem("act")
        block = l.block()

        @block.vector
        def _(dve):
            c = Chain(dve, s_dve)
            c(nc.vector.tensor_tensor(sq[:, :, :], wh[:, :, :], wh[:, :, :], ALU.mult))
            c(nc.vector.tensor_reduce(ss[:], sq[:, :, :], AX.X, ALU.add))
            dve.wait_ge(s_act, 1)
            c(nc.vector.tensor_scalar(nr[:], nr[:], 1e-18, None, ALU.max))
            c(nc.vector.reciprocal(rn[:], nr[:]))

        @block.scalar
        def _(act):
            act.wait_ge(s_dve, 2)
            nc.scalar.activation(nr[:], ss[:], ACT.Sqrt).then_inc(s_act, 1)


def coefficients(nc, coeff_param, scale_param, coef):
    with Mem(nc, "coef") as l:
        cp, sp_ = l.sb("cp", [P, 3]), l.sb("sp", [P, 1])
        ex, t, u = l.sb("ex", [P, 3]), l.sb("t", [P, 8]), l.sb("u", [P, 1])
        s_in, s_dve, s_act = l.sem("in"), l.sem("dve"), l.sem("act")
        block = l.block()

        @block.sync
        def _(sp):
            sp.dma_start(cp[:], coeff_param.rearrange("(a n) -> a n", a=1).to_broadcast([P, 3])).then_inc(s_in, 16)
            sp.dma_start(sp_[:], scale_param.rearrange("(a n) -> a n", a=1).to_broadcast([P, 1])).then_inc(s_in, 16)

        @block.vector
        def _(dve):
            c = Chain(dve, s_dve)
            dve.wait_ge(s_in, 32)
            c(nc.vector.tensor_reduce(t[:, 0:1], cp[:], AX.X, ALU.max))
            c(nc.vector.tensor_scalar(cp[:], cp[:], t[:, 0:1], None, ALU.subtract))
            c(nc.vector.scalar_tensor_tensor(t[:, 1:2], sp_[:], -1.0, sp_[:], ALU.mult, ALU.max))
            dve.wait_ge(s_act, 2)
            c(nc.vector.tensor_scalar(u[:], t[:, 2:3], 1.0, None, ALU.add))
            c(nc.vector.tensor_scalar(t[:, 3:4], u[:], -1.0, None, ALU.add))
            c(nc.vector.tensor_scalar(t[:, 4:5], t[:, 3:4], 0.0, None, ALU.is_equal))
            c(nc.vector.tensor_tensor(t[:, 3:4], t[:, 3:4], t[:, 4:5], ALU.add))
            c(nc.vector.reciprocal(t[:, 5:6], t[:, 3:4]))
            dve.wait_ge(s_act, 3)
            c(nc.vector.tensor_tensor(t[:, 6:7], t[:, 6:7], t[:, 4:5], ALU.add))
            c(nc.vector.tensor_tensor(t[:, 6:7], t[:, 6:7], t[:, 2:3], ALU.mult))
            c(nc.vector.tensor_tensor(t[:, 6:7], t[:, 6:7], t[:, 5:6], ALU.mult))
            c(nc.vector.scalar_tensor_tensor(t[:, 6:7], sp_[:], 0.0, t[:, 6:7], ALU.max, ALU.add))
            c(nc.vector.tensor_reduce(t[:, 0:1], ex[:], AX.X, ALU.add))
            c(nc.vector.reciprocal(t[:, 7:8], t[:, 0:1]))
            c(nc.vector.tensor_tensor(t[:, 7:8], t[:, 7:8], t[:, 6:7], ALU.mult))
            c(nc.vector.tensor_scalar(coef[:], ex[:], t[:, 7:8], None, ALU.mult))
            c(nc.vector.tensor_scalar(coef[:, 1:2], coef[:, 1:2], -1.0, None, ALU.mult))

        @block.scalar
        def _(act):
            act.wait_ge(s_dve, 3)
            nc.scalar.activation(ex[:], cp[:], ACT.Exp).then_inc(s_act, 1)
            nc.scalar.activation(t[:, 2:3], t[:, 1:2], ACT.Exp, scale=-1.0).then_inc(s_act, 1)
            act.wait_ge(s_dve, 4)
            nc.scalar.activation(t[:, 6:7], u[:], ACT.Ln).then_inc(s_act, 1)


def build_rows(nc, k, sorted_, table, whT, whTs, whD, rnD, rn_row, coef, prop, cnt, deg, c16_dram, c_dram,
               g_dram):
    NG, LINKS = len(GROUPS), 10
    FIRST = [sum(GROUPS[:g]) for g in range(NG)]
    MAXG, C = max(GROUPS), CAP * NB
    with Mem(nc, "rows") as l:
        recrow = l.sb("recrow", [P, 2, NB, CAP, 4])
        dbase = l.sb("dbase", [P, NB, CAP])
        sbase = l.sb("sbase", [P, 1])
        keys, inside, low = (l.sb(x, [P, 2, C], BF16) for x in ("keys", "inside", "low"))
        skey, dkey = keys[:, 0], keys[:, 1]
        parts = l.sb("parts", [P, 3, 2, C], BF16)
        rest = l.sb("rest", [P, 2, 2, C])
        soh = [l.sb(f"soh{b}", [P, P, CAP * GROUPS[b]], BF16) for b in range(2)]
        doh = [l.sb(f"doh{b}", [P, P, CAP * GROUPS[b]], BF16) for b in range(2)]
        wsrc = [l.sb(f"wsrc{b}", [P, 6, P, CAP * GROUPS[b]], BF16) for b in range(2)]
        out_c16, out_c = l.sb("out_c16", [P, 2, MAXG, W], BF16), l.sb("out_c", [P, 2, MAXG, W])
        out_g = l.sb("out_g", [P, 2, MAXG, W])
        pos_s, neg_s, fac = (l.sb(x, [W, 2, MAXG, W]) for x in ("pos_s", "neg_s", "fac"))
        b0 = l.sb("b0", [W, 2, MAXG, W])
        rden = l.sb("rden", [W, 2, MAXG, W])
        ps = l.ps("ps", [P, 8, 512])
        names = "loaded taken onehot products freed_act signed factor scaled blocks used row_read link zero kbase widened"
        s = {x: l.sem(x) for x in names.split()}
        s_st, s_add = [l.sem("st0"), l.sem("st1")], [l.sem("add0"), l.sem("add1")]
        block = l.block()

        def bank(g, lo, width, rows=P):
            a = BANKS[g % 2][0]
            return ps[0:rows, a:a + GROUPS[g], lo:lo + width]

        def plan(eng, body, between=None):
            with eng.Fori(0, NB) as row:
                body(row, row, False)
            rounds = eng.value_load(table[0:1, NB * NB:NB * NB + 1], min_val=1, max_val=-(-E // ROUND))
            with eng.If(rounds > 1):
                if between:
                    between()
                with eng.Fori(1, rounds) as r:
                    with eng.Fori(0, NB) as row:
                        body(row, r * NB + row, True, r)

        @block.sync
        def _(sp):
            def body(row, w, more, r=0):
                sp.wait_ge(s["loaded"], w * (16 * NB))
                sp.wait_ge(s["taken"], w)
                for d0 in range(0, NB, 5):
                    _, at = nc.values_load_multi_w_load_instructions(
                        table[0:1, bass.ds(row * NB + d0, 5)], engines=[mybir.EngineType.SP], min_val=0, max_val=E)
                    for j in range(5):
                        start = at[j] + r * ROUND if more else at[j]
                        sp.dma_start(recrow[:, bass.ds(w % 2, 1), d0 + j, :, :],
                                     sorted_[bass.ds(start, ROUND), :].rearrange("(p b) f -> p b f", b=CAP)
                                     ).then_inc(s["loaded"], 16)
            plan(sp, body)

        @block.vector
        def _(dve):
            link = s["link"]

            def body(row, w, more, r=0):
                dve.wait_ge(s["loaded"], (w + 1) * (16 * NB))
                base = w * LINKS
                at = [0]

                def c(ins):
                    at[0] += 1
                    ins.then_inc(link, 1)
                    dve.wait_ge(link, base + at[0])

                rec = recrow[:, bass.ds(w % 2, 1), :, :, :].rearrange("p a d c f -> p (a d c) f")
                c(nc.vector.tensor_copy(sbase[:], k["codes"][:, bass.ds(row, 1)]))
                c(nc.vector.tensor_scalar(skey, rec[:, :, 0], sbase[:], None, ALU.subtract))
                c(nc.vector.tensor_tensor(dkey, rec[:, :, 1], dbase[:, :, :].rearrange("p d c -> p (d c)"), ALU.subtract))
                c(nc.vector.tensor_scalar(low[:], keys[:], 0.0, None, ALU.is_ge))
                c(nc.vector.scalar_tensor_tensor(inside[:], keys[:], float(W), low[:], ALU.is_lt, ALU.mult))
                v = rec[:, :, 2:4].rearrange("p c f -> p f c")
                nc.vector.tensor_copy(rest[:, 0], v).then_inc(s["taken"], 1)
                dve.wait_ge(s["taken"], w + 2)
                c(nc.vector.tensor_copy(parts[:, 0], rest[:, 0]))
                c(nc.vector.tensor_tensor(rest[:, 1], rest[:, 0], parts[:, 0], ALU.subtract))
                c(nc.vector.tensor_copy(parts[:, 1], rest[:, 1]))
                c(nc.vector.tensor_tensor(rest[:, 0], rest[:, 1], parts[:, 1], ALU.subtract))
                c(nc.vector.tensor_copy(parts[:, 2], rest[:, 0]))
                for g in range(NG + 1):
                    if g < NG:
                        b, n = g % 2, CAP * GROUPS[g]
                        lo = CAP * FIRST[g]
                        gi = w * NG + g
                        shape = [P, P, n]
                        if g >= 2:
                            dve.wait_ge(s["products"], gi - 1)
                        else:
                            dve.wait_ge(s["products"], w * NG)
                        nums = k["numbers"][:, :, 0:n]
                        one = nc.vector.tensor_tensor(soh[b][:, :, :], nums, keys[:, 0, None, lo:lo + n].to_broadcast(shape), ALU.is_equal)
                        one.then_inc(s["onehot"], 1)
                        nc.vector.tensor_tensor(doh[b][:, :, :], nums, keys[:, 1, None, lo:lo + n].to_broadcast(shape),
                                                ALU.is_equal).then_inc(s["onehot"], 1)
                        dve.wait_ge(s["onehot"], gi * 8 + 1)
                        for q in range(6):
                            nc.vector.tensor_tensor(wsrc[b][:, q, :, :], soh[b][:, :, :],
                                                    parts[:, q // 2, q % 2, None, lo:lo + n].to_broadcast(shape),
                                                    ALU.mult).then_inc(s["onehot"], 1)
                    if g >= 1:
                        h = g - 1
                        hb, hn, hi = h % 2, GROUPS[h], w * NG + h
                        for i in range(hn):
                            d = FIRST[h] + i
                            ins = nc.vector.tensor_scalar(rden[:, hb, i, :], rn_row[:, bass.ds(row * W, W)], rnD[:, d:d + 1],
                                                          1e8, ALU.mult, ALU.min)
                            ins.then_inc(s["factor"], 1)
                        dve.wait_ge(s["factor"], w * NB + FIRST[h] + hn)
                        dve.wait_ge(s["signed"], hi + 1)
                        nc.vector.tensor_tensor(fac[:, hb, 0:hn, :], pos_s[:, hb, 0:hn, :], rden[:, hb, 0:hn, :], ALU.mult).then_inc(s["scaled"], 1)
                        dve.wait_ge(s["scaled"], hi + 1)
                        if h >= 2:
                            dve.wait_ge(s["used"], hi - 1)
                        else:
                            dve.wait_ge(s["used"], w * NG)
                        dve.wait_ge(s["freed_act"], 4 * hi + 4)
                        nc.vector.tensor_tensor(b0[:, hb, 0:hn, :], fac[:, hb, 0:hn, :], bank(h, 256, W, W), ALU.mult).then_inc(s["blocks"], 1)
                dve.wait_ge(s["used"], (w + 1) * NG)
                p_row = prop[:, bass.ds(row, 1), :].rearrange("p a f -> p (a f)")
                nc.vector.tensor_tensor(p_row, p_row, ps[0:W, SELF_BANK, 0:F], ALU.add).then_inc(s["row_read"], 1)
                c_row = cnt[:, bass.ds(row, 1)]
                nc.vector.tensor_tensor(c_row, c_row, ps[0:W, SELF_BANK, F:F + 1], ALU.add).then_inc(s["row_read"], 1)
                dve.wait_ge(s["row_read"], 2 * w + 2)
            dve.wait_ge(s["kbase"], 1)
            nc.vector.memset(sbase[:], 0.0).then_inc(s["taken"], 1)
            dve.wait_ge(s["taken"], 1)
            plan(dve, body)
            nc.vector.tensor_copy(deg[:], ps[0:W, DEG_BANK, 0:NB]).then_inc(s["zero"], 1)
            dve.wait_ge(s["zero"], 1)

        @block.scalar
        def _(act):
            def body(row, w, more, r=0):
                for g in range(NG):
                    b, n, gi = g % 2, GROUPS[g], w * NG + g
                    act.wait_ge(s["products"], gi + 1)
                    if g >= 2:
                        act.wait_ge(s["signed"], gi - 1)
                    else:
                        act.wait_ge(s["signed"], w * NG)
                    if g >= 2:
                        act.wait_ge(s["scaled"], gi - 1)
                    else:
                        act.wait_ge(s["scaled"], w * NG)
                    nc.scalar.activation(pos_s[:, b, 0:n, :], bank(g, 384, W, W), ACT.Relu, scale=coef[0:W, 0:1]).then_inc(s["freed_act"], 1)
                    nc.scalar.activation(neg_s[:, b, 0:n, :], bank(g, 384, W, W), ACT.Relu, scale=coef[0:W, 1:2]).then_inc(s["freed_act"], 1)
                    if more:
                        act.wait_ge(s_st[b], NB * 5 * 32)
                        act.wait_ge(s_add[b], ((w - NB) * 5 + g // 2) * 32)
                    else:
                        act.wait_ge(s_st[b], (w * 5 + g // 2) * 32)
                    c_tile = out_c if more else out_c16
                    nc.scalar.activation(c_tile[:, b, 0:n, :], bank(g, 0, W), ACT.Copy).then_inc(s["freed_act"], 1)
                    nc.scalar.activation(out_g[:, b, 0:n, :], bank(g, 128, W), ACT.Copy).then_inc(s["freed_act"], 1)
                    if not more:
                        act.wait_ge(s["freed_act"], 4 * gi + 4)
                        for buf, dram in ((out_c16, c16_dram), (out_g, g_dram)):
                            act.dma_start(dram[bass.ds(row * P, P), FIRST[g] * W:(FIRST[g] + n) * W],
                                          buf[:, b, 0:n, :].rearrange("p n w -> p (n w)")).then_inc(s_st[b], 16)
            plan(act, body)
            for b in range(2):
                act.wait_ge(s_st[b], NB * 5 * 32)

        @block.gpsimd
        def _(pool):
            nc.gpsimd.iota(dbase[:, :, :], [[W, NB], [0, CAP]], base=0, channel_multiplier=0,
                           allow_small_or_imprecise_dtypes=True).then_inc(s["kbase"], 1)

            def body(row, w, more, r=0):
                for g in range(NG):
                    b, n, gi = g % 2, GROUPS[g], w * NG + g
                    pool.wait_ge(s["freed_act"], 4 * gi + 2)
                    nc.gpsimd.tensor_tensor(pos_s[:, b, 0:n, :], pos_s[:, b, 0:n, :], neg_s[:, b, 0:n, :],
                                            ALU.subtract).then_inc(s["signed"], 1)
                    if more:
                        freed = pool.snap(4 * gi + 4)
                        pool.wait_ge(s_st[0], NB * 5 * 32)
                        pool.wait_ge(s_st[1], NB * 5 * 32)
                        pool.wait_ge(s["freed_act"], freed)
                        for buf, dram in ((out_c, c_dram), (out_g, g_dram)):
                            pool.dma_start(dram[bass.ds(row * P, P), FIRST[g] * W:(FIRST[g] + n) * W],
                                           buf[:, b, 0:n, :].rearrange("p n w -> p (n w)"),
                                           accum_op=ALU.add).then_inc(s_add[b], 16)
                        pool.wait_ge(s_add[b], ((w - NB) * 5 + g // 2 + 1) * 32)

            def widen():
                for b in range(2):
                    pool.wait_ge(s_st[b], NB * 5 * 32)
                pool.dma_start(c_dram, c16_dram).then_inc(s["widened"], 16)
                pool.wait_ge(s["widened"], 16)
            plan(pool, body, widen)

        @block.tensor
        def _(pe):
            def mm(out, lhsT, rhs, start=False):
                return nc.tensor.matmul(out, lhsT, rhs, start=start, stop=True, skip_group_check=True)

            def propagate(w, g):
                pe.wait_ge(s["blocks"], w * NG + g + 1)
                for i in range(GROUPS[g]):
                    ins = mm(ps[0:W, SELF_BANK, 0:F], b0[:, g % 2, i, :], whD[:, FIRST[g] + i, :])
                ins.then_inc(s["used"], 1)
                return ins

            def body(row, w, more, r=0):
                pe.wait_ge(s["row_read"], 2 * w)
                mm(ps[:, SELF_BANK, 0:F + 1], k["zeros"][:, 0:P], k["zeros"][:, 0:F + 1], True)
                for g in range(NG):
                    b, n, gi = g % 2, GROUPS[g], w * NG + g
                    pe.wait_ge(s["blocks"], gi - 1 if g >= 2 else w * NG)
                    pe.wait_ge(s["freed_act"], 4 * gi - 4 if g >= 2 else w * (4 * NG))
                    mm(ps[:, BANKS[b][0], 0:2], k["zeros16"][:], k["zeros16"][:, 0:2], True)
                    for i in range(n):
                        bk, d = BANKS[b][i], FIRST[g] + i
                        mm(ps[0:W, bk, 384:384 + W], whT[:, d * W:d * W + W], whTs[:, bass.ds(row, 1), :], i > 0)
                    pe.wait_ge(s["onehot"], 8 * gi + 8)
                    for i in range(n):
                        bk, d = BANKS[b][i], FIRST[g] + i
                        out_ga = ps[:, bk, 128:384].rearrange("p (v w) -> p v w", v=2)[:, :, 0:W]
                        for j in range(CAP):
                            cc = CAP * i + j
                            for q in range(3):
                                mm(out_ga, doh[b][:, :, cc], wsrc[b][:, 2 * q:2 * q + 2, 0:W, cc])
                            mm(ps[:, DEG_BANK, d:d + 1], doh[b][:, :, cc], inside[:, 0, CAP * d + j:CAP * d + j + 1])
                            mm(ps[:, bk, 0:W], soh[b][:, :, cc], doh[b][:, 0:W, cc])
                            ins = mm(ps[:, SELF_BANK, F:F + 1], soh[b][:, :, cc], inside[:, 1, CAP * d + j:CAP * d + j + 1])
                    ins.then_inc(s["products"], 1)
                    if g >= 1:
                        propagate(w, g - 1)
                propagate(w, NG - 1)
            mm(ps[:, DEG_BANK, 0:NB], k["zeros"][:, 0:P], k["zeros"][:, 0:NB], True)
            plan(pe, body)


def product_c(nc, name, k, c16, c16_dram, c_dram, rounds_, u, u3, y, load):
    NBK = 8
    HALVES = [range(0, 12), range(12, NB)]
    LOT = 5
    with Mem(nc, name) as l:
        rows = [c16[:, b * 2 * N:(b + 1) * 2 * N].bitcast(F32) for b in range(2)]
        c_rows = c16[:, 0:NB * N].rearrange("p (s n) -> p s n", s=NB)
        ps = l.ps("ps", [P, 8, 512])
        s_in, s_pe = [l.sem("in0"), l.sem("in1")], [l.sem("pe0"), l.sem("pe1")]
        s_end, s_y = l.sem("end"), l.sem("y")
        s_c = [l.sem(f"c{q}") for q in range(NB // LOT)]
        s_split, s_half, s_sum = l.sem("split"), l.sem("half"), l.sem("sum")
        block = l.block()
        pairs = NB // 2
        sums = [(h, d, len(HALVES[h][i:i + 2]), (i // 2 + 6 * h) % 8)
                for h in range(2) for i, d in enumerate(HALVES[h]) if i % 2 == 0]

        def paths(eng, narrow, wide):
            rounds = eng.value_load(rounds_, min_val=1, max_val=-(-E // ROUND))
            with eng.If(rounds < 2):
                narrow()
            with eng.If(rounds > 1):
                wide()

        @block.sync
        def _(sp):
            def narrow():
                if load:
                    for q in range(NB // LOT):
                        sp.dma_start(c_rows[:, q * LOT:(q + 1) * LOT, :],
                                     c16_dram[q * LOT * P:(q + 1) * LOT * P, :].rearrange("(s p) n -> p s n", p=P)
                                     ).then_inc(s_c[q], 16)
                    for q in range(NB // LOT):
                        sp.wait_ge(s_c[q], 16)

            def wide():
                def fetch(b, row, i):
                    sp.wait_ge(s_pe[b], i)
                    sp.dma_start(rows[b], c_dram[bass.ds(row * P, P), :]).then_inc(s_in[b], 16)

                with sp.Fori(0, pairs) as i:
                    fetch(0, 2 * i, i)
                    fetch(1, 2 * i + 1, i)
                fetch(0, NB - 1, pairs)
            paths(sp, narrow, wide)

        @block.tensor
        def _(pe):
            def mm(out, lhsT, rhs, start=False):
                return nc.tensor.matmul(out, lhsT, rhs, start=start, stop=True, skip_group_check=True)

            def narrow():
                pe.wait_ge(s_split, 5)
                for h in range(2):
                    mine = [x for x in sums if x[0] == h]
                    for _, d0, n, bk in mine:
                        if h == 1 and bk < 6:
                            pe.wait_ge(s_sum, bk + 1)
                        mm(ps[:, bk, 0:384], k["zeros16"][:], k["zeros16"][:, 0, None].to_broadcast([P, 384]), True)
                    for q in range(NB // LOT):
                        if load and h == 0:
                            pe.wait_ge(s_c[q], 16)
                        with pe.Fori(q * LOT, (q + 1) * LOT) as row:
                            for _, d0, n, bk in mine:
                                for i in range(n):
                                    d = d0 + i
                                    mm(ps[0:W, bk, i * 192:i * 192 + 192],
                                       c_rows[0:W, bass.ds(row, 1), d * W:d * W + W].rearrange("p a w -> p (a w)"),
                                       u3[:, bass.ds(row, 1), :, :].rearrange("p a q f -> p (a q f)"))
                    mm(ps[:, mine[-1][3], 0:2], k["zeros16"][:], k["zeros16"][:, 0:2]).then_inc(s_half, 1)

            def wide():
                def use(b, row, i):
                    pe.wait_ge(s_in[b], 16 * i + 16)
                    for d in range(NB):
                        ins = mm(ps[0:W, d // NBK, d % NBK * F:d % NBK * F + F], rows[b][0:W, d * W:d * W + W],
                                 u[:, bass.ds(row, 1), :])
                    return ins

                for q in range(4):
                    mm(ps[0:W, q, :], k["zeros"][0:W, 0:W], k["zeros"][0:W, :], True)
                with pe.Fori(0, pairs) as i:
                    use(0, 2 * i, i).then_inc(s_pe[0], 1)
                    use(1, 2 * i + 1, i).then_inc(s_pe[1], 1)
                use(0, NB - 1, pairs).then_inc(s_end, 1)
            paths(pe, narrow, wide)

        @block.vector
        def _(dve):
            def narrow():
                c = Chain(dve, s_split)
                part = [u3[:, :, q, :] for q in range(3)]
                c(nc.vector.tensor_copy(part[0], u[:, :, :]))
                c(nc.vector.tensor_tensor(y[:, :, :], u[:, :, :], part[0], ALU.subtract))
                c(nc.vector.tensor_copy(part[1], y[:, :, :]))
                c(nc.vector.tensor_tensor(y[:, :, :], y[:, :, :], part[1], ALU.subtract))
                c(nc.vector.tensor_copy(part[2], y[:, :, :]))
                for n_, (h, d0, n, bk) in enumerate(sums):
                    dve.wait_ge(s_half, h + 1)
                    nc.vector.tensor_reduce(y[:, d0:d0 + n, :],
                                            ps[0:W, bk, 0:n * 192].rearrange("p (n q f) -> p n f q", n=n, q=3),
                                            AX.X, ALU.add).then_inc(s_sum, 1)
                dve.wait_ge(s_sum, len(sums))

            def wide():
                dve.wait_ge(s_end, 1)
                for q in range(4):
                    n = min(NBK, NB - NBK * q)
                    nc.vector.tensor_copy(y[:, NBK * q:NBK * q + n, :],
                                          ps[0:W, q, 0:n * F].rearrange("p (n f) -> p n f", f=F)).then_inc(s_y, 1)
                dve.wait_ge(s_y, 4)
            paths(dve, narrow, wide)


def product_g(nc, name, g_dram, u, y):
    with Mem(nc, name) as l:
        rows = [l.sb(f"row{b}", [P, N]) for b in range(2)]
        ps = l.ps("ps", [W, 2, 512])
        s_in, s_pe, s_y = [l.sem("in0"), l.sem("in1")], [l.sem("pe0"), l.sem("pe1")], [l.sem("y0"), l.sem("y1")]
        block = l.block()
        pairs = NB // 2

        def plan(eng, step):
            with eng.Fori(0, pairs) as i:
                step(0, 2 * i, i)
                step(1, 2 * i + 1, i)
            step(0, NB - 1, pairs)

        @block.sync
        def _(sp):
            def load(b, row, i):
                sp.wait_ge(s_pe[b], i)
                sp.dma_start(rows[b][:, :], g_dram[bass.ds(row * P, P), :]).then_inc(s_in[b], 16)
            plan(sp, load)

        @block.tensor
        def _(pe):
            def use(b, row, i):
                pe.wait_ge(s_in[b], 16 * i + 16)
                pe.wait_ge(s_y[b], i)
                for d in range(NB):
                    ins = nc.tensor.matmul(ps[:, b, 0:F], rows[b][0:W, d * W:d * W + W], u[:, d, :],
                                           start=d == 0, stop=d == NB - 1)
                ins.then_inc(s_pe[b], 1)
            plan(pe, use)

        @block.vector
        def _(dve):
            def read(b, row, i):
                dve.wait_ge(s_pe[b], i + 1)
                nc.vector.tensor_copy(y[:, bass.ds(row, 1), :], ps[:, b:b + 1, 0:F]).then_inc(s_y[b], 1)
            plan(dve, read)
            dve.wait_ge(s_y[0], pairs + 1)
            dve.wait_ge(s_y[1], pairs)


def chain_block(nc, name, steps):
    with Mem(nc, name) as l:
        step = Running("step")
        block = l.block()

        @block.vector
        def _(dve):
            for n, (eng, f) in enumerate(steps):
                if eng == "v":
                    dve.wait_ge(step.sem, step.at(n))
                    f().then_inc(step.sem, 1)
            dve.wait_ge(step.sem, step.at(len(steps)))

        @block.scalar
        def _(act):
            for n, (eng, f) in enumerate(steps):
                if eng == "a":
                    act.wait_ge(step.sem, step.at(n))
                    f().then_inc(step.sem, 1)
        step.close(len(steps))


def four_layers(nc, x, src, dst, edge_attr_16, edge_weight, edge_weight_n2, L0_gnn_W, L0_gnn_b, L0_gnn_deg_coeff,
                L0_gnn_coeff_param, L0_gnn_scale_param, L2_gnn_W1, L2_gnn_b1, L2_gnn_W2, L2_gnn_b2,
                L3_gnn_W_edge, L3_gnn_b_edge, L3_gnn_W_node, L3_gnn_b_node, out):
    v = nc.vector
    by_dst_dram = nc.dram_tensor("by_dst", [EP, 4], F32).ap()
    by_both_dram = nc.dram_tensor("by_both", [R2_ROWS, 4], F32).ap()
    c_dram = nc.dram_tensor("c_blocks", [NB * P, N], F32).ap()
    c16_dram = nc.dram_tensor("c_blocks16", [NB * P, N], BF16).ap()
    g_dram = nc.dram_tensor("g_blocks", [NB * P, N], F32).ap()
    hist_dram = nc.dram_tensor("hist", [P, P], F32).ap()
    rn_dram = nc.dram_tensor("rn", [N], F32).ap()
    vec_dram = nc.dram_tensor("vec", [N], F32).ap()
    turn = [nc.dram_tensor(f"turn{i}", [N, F], F32).ap() for i in range(6)]

    with Mem(nc, "k") as top:
        k = {
            "ident": top.sb("ident", [P, P]), "before": top.sb("before", [P, P]), "ones": top.sb("ones", [P, P]),
            "ones16": top.sb("ones16", [P, 2], BF16), "zeros": top.sb("zeros", [P, 512]),
            "zeros16": top.sb("zeros16", [P, P], BF16),
            "numbers": top.sb("numbers", [P, P, CAP * max(GROUPS)], BF16), "codes": top.sb("codes", [P, NB]),
        }
        table = top.sb("table", [1, NB * NB + 7], I32)
        deg, cnt = top.sb("deg", [W, NB]), top.sb("cnt", [W, NB])
        coef = top.sb("coef", [P, 3])
        Running.sems = {n: (top.sem(n), 0) for n in ("moved", "norm_dve", "norm_act", "made", "read_act", "read_dve", "step")}
        constants(nc, top, k)
        sentinels(nc, by_both_dram)

        with Mem(nc, "sort") as m:
            rec = m.sb("rec", [P, T, 4])
            edge_records(nc, rec, src, dst, edge_attr_16, edge_weight, edge_weight_n2, L0_gnn_deg_coeff,
                         L3_gnn_W_edge, L3_gnn_b_edge)
            pos = m.sb("pos", [P, T])
            by_dst = m.sb("by_dst_m", [P, 32, TQ], BF16)
            unordered = table[0:1, NB * NB + 1:NB * NB + 2]
            order_check(nc, k, rec, unordered)
            ranks(nc, "rank_d", k, rec, 1, 1.0 / W, by_dst, pos, W // 2, unordered)
            scatter(nc, "scat_d", k, rec, pos, by_dst_dram, unordered)
            reload(nc, "load_d", rec, by_dst_dram, unordered)
            by_src = m.sb("by_src_m", [P, 32, TQ], BF16)
            ranks(nc, "rank_s", k, rec, 0, 1.0 / CODE, by_src, pos, W // 2)
            scatter(nc, "scat_s", k, rec, pos, by_both_dram)
            key_masks(nc, rec, 1, 1.0 / W, by_dst, W // 2)
            bucket_table(nc, by_src, by_dst, hist_dram, table)

        full = [W, NB, F]
        wide = lambda a: a[:, :, None].to_broadcast(full)
        dis, disS, dis2, t = (top.sb(n, [W, NB]) for n in ("dis", "disS", "dis2", "t"))
        with Mem(nc, "l0") as m:
            xS, prop, whS = (m.sb(n, full) for n in ("xS", "prop", "whS"))
            xD, hD = m.sb("xD", [W, NB, F]), m.sb("hD", [W, NB, F])
            hT, whT = m.sb("hT", [F, N]), m.sb("whT", [F, N])
            whTs = m.sb("whTs", [F, NB, W])
            whD = m.sb("whD", [W, NB, F])
            rnD, rnS, rn_row = m.sb("rnD", [W, NB]), m.sb("rnS", [W, NB]), m.sb("rn_row", [W, N])
            w0, b_row, b_col = m.sb("w0", [F, F]), m.sb("b_row", [W, F]), m.sb("b_col", [F, 1])
            copy_dma(nc, "in0", [
                (xD[:, :, :], d_layout(x)), (xS[:, :, :], s_layout(x)), (w0[:], L0_gnn_W),
                (b_row[:], L0_gnn_b.rearrange("(a n) -> a n", a=1).to_broadcast([W, F])),
                (b_col[:], L0_gnn_b.rearrange("(n a) -> n a", a=1))])
            coefficients(nc, L0_gnn_coeff_param, L0_gnn_scale_param, coef)
            layer_norm_relu(nc, "ln0", xD, hD, whS)
            transpose_nodes(nc, "tr0", k, hD, hT)
            dense_T(nc, "whT", w0[:], hT, whT, b_col[:], False)
            dense(nc, "whD", lambda b: hT[:, b * W:b * W + W], w0[:], whD, b_row)
            dense(nc, "whS", lambda b: hT[:, b:N:NB], w0[:], whS, b_row)
            inverse_norms(nc, "rnD", whD, rnD)
            inverse_norms(nc, "rnS", whS, rnS)
            copy_dma(nc, "rnrow", [
                (rn_dram.rearrange("(s i) -> i s", s=NB), rnS[:]),
                (rn_row[:], rn_dram.rearrange("(a n) -> a n", a=1).to_broadcast([W, N]))])
            chain_block(nc, "whTs", [
                ("v", lambda: v.tensor_copy(whTs[:, :, :], whT[:].rearrange("f (i s) -> f s i", s=NB))),
                ("v", lambda: v.memset(prop[:, :, :], 0.0)),
                ("v", lambda: v.memset(cnt[:], 0.0))])
            build_rows(nc, k, by_both_dram, table, whT, whTs, whD, rnD, rn_row, coef, prop, cnt, deg,
                       c16_dram, c_dram, g_dram)

            chain_block(nc, "x1", [
                ("v", lambda: v.tensor_tensor(xS[:, :, :], xS[:, :, :], prop[:, :, :], ALU.add)),
                ("v", lambda: v.scalar_tensor_tensor(xS[:, :, :], whS[:, :, :], coef[0:W, 2:3], xS[:, :, :], ALU.mult, ALU.add)),
                ("v", lambda: v.tensor_scalar(t[:], deg[:], 1.0, None, ALU.max)),
                ("a", lambda: nc.scalar.activation(t[:], t[:], ACT.Sqrt)),
                ("v", lambda: v.reciprocal(dis[:], t[:])),
                ("v", lambda: v.tensor_scalar(t[:], deg[:], 0.0, None, ALU.is_gt)),
                ("v", lambda: v.tensor_tensor(dis[:], dis[:], t[:], ALU.mult)),
                ("v", lambda: v.tensor_tensor(dis2[:], dis[:], dis[:], ALU.mult))])
            copy_dma(nc, "turn0", [
                (s_layout(turn[0]), xS[:, :, :]),
                (vec_dram.rearrange("(c p) -> p c", p=W), dis[:]), (disS[:], vec_dram.rearrange("(p c) -> p c", c=NB))])

        with Mem(nc, "l1") as m:
            xD, u, y, acc, xS = (m.sb(n, full) for n in ("xD", "u", "y", "acc", "xS"))
            copy_dma(nc, "in1", [(xD[:, :, :], d_layout(turn[0])), (acc[:, :, :], s_layout(turn[0]))])
            layer_norm_relu(nc, "ln1s", acc, u, y)
            layer_norm_relu(nc, "ln1d", xD, acc, y)
            chain_block(nc, "u0", [("v", lambda: v.tensor_tensor(u[:, :, :], u[:, :, :], wide(disS), ALU.mult))])
            with Mem(nc, "c") as q:
                c16 = q.sb("c16", [P, NB * N + 1], BF16)
                u3 = q.sb("u3", [W, NB, 3, F], BF16)
                rounds_ = table[0:1, NB * NB:NB * NB + 1]
                for i in range(3):
                    product_c(nc, f"gcn{i}", k, c16, c16_dram, c_dram, rounds_, u, u3, y, i == 0)
                    chain_block(nc, f"acc{i}", [
                        ("v", lambda: v.tensor_tensor(u[:, :, :], y[:, :, :], wide(dis), ALU.mult)),
                        ("v", lambda: v.tensor_tensor(acc[:, :, :], acc[:, :, :], u[:, :, :], ALU.add)),
                        ("v", lambda: v.tensor_tensor(y[:, :, :], y[:, :, :], wide(dis2), ALU.mult))])
                    if i < 2:
                        copy_dma(nc, f"turn{i + 1}", [(d_layout(turn[i + 1]), y[:, :, :]), (u[:, :, :], s_layout(turn[i + 1]))])
                chain_block(nc, "x2", [
                    ("v", lambda: v.scalar_tensor_tensor(xD[:, :, :], acc[:, :, :], 0.25, xD[:, :, :], ALU.mult, ALU.add))])

                layer_norm_relu(nc, "ln2", xD, acc, y)
                copy_dma(nc, "turn3", [(d_layout(turn[3]), acc[:, :, :]), (u[:, :, :], s_layout(turn[3]))])
                product_c(nc, "gin", k, c16, c16_dram, c_dram, rounds_, u, u3, y, False)
            with Mem(nc, "l2") as q:
                zT, z1T = q.sb("zT", [F, N]), q.sb("z1T", [F, N])
                w1, w2, b1, b2 = q.sb("w1", [F, F]), q.sb("w2", [F, F]), q.sb("b1", [F, 1]), q.sb("b2", [W, F])
                copy_dma(nc, "in2", [
                    (w1[:], L2_gnn_W1), (w2[:], L2_gnn_W2), (b1[:], L2_gnn_b1.rearrange("(n a) -> n a", a=1)),
                    (b2[:], L2_gnn_b2.rearrange("(a n) -> a n", a=1).to_broadcast([W, F]))])
                chain_block(nc, "z", [("v", lambda: v.tensor_tensor(y[:, :, :], y[:, :, :], acc[:, :, :], ALU.add))])
                transpose_nodes(nc, "tr2", k, y, zT)
                dense_T(nc, "z1", w1[:], zT, z1T, b1[:], True)
                dense(nc, "z2", lambda b: z1T[:, b * W:b * W + W], w2[:], y, b2, relu=True)
                chain_block(nc, "x3", [("v", lambda: v.tensor_tensor(xD[:, :, :], xD[:, :, :], y[:, :, :], ALU.add))])

            layer_norm_relu(nc, "ln3", xD, acc, y)
            copy_dma(nc, "turn4", [(d_layout(turn[4]), xD[:, :, :]), (xS[:, :, :], s_layout(turn[4]))])
            with Mem(nc, "l3") as q:
                hT = q.sb("hT", [F, N])
                wn, wnT, bn = q.sb("wn", [F, F]), q.sb("wnT", [F, F]), q.sb("bn", [W, F])
                wps = q.ps("wps", [F, F])
                copy_dma(nc, "in3", [(wn[:], L3_gnn_W_node),
                                     (bn[:], L3_gnn_b_node.rearrange("(a n) -> a n", a=1).to_broadcast([W, F]))])
                with Mem(nc, "wnT") as l:
                    s_t, s_c = l.sem("t"), l.sem("c")
                    block = l.block()

                    @block.tensor
                    def _(pe):
                        nc.tensor.transpose(wps[:], wn[:], k["ident"][0:F, 0:F]).then_inc(s_t, 1)

                    @block.vector
                    def _(dve):
                        dve.wait_ge(s_t, 1)
                        v.tensor_copy(wnT[:], wps[:]).then_inc(s_c, 1)
                        dve.wait_ge(s_c, 1)
                transpose_nodes(nc, "tr3", k, acc, hT)
                dense(nc, "xp", lambda b: hT[:, b * W:b * W + W], wnT[:], u, bn)
            product_g(nc, "gated", g_dram, u, y)
            chain_block(nc, "x4", [
                ("v", lambda: v.tensor_scalar(t[:], cnt[:], 1.0, None, ALU.max)),
                ("v", lambda: v.reciprocal(dis[:], t[:])),
                ("v", lambda: v.tensor_tensor(y[:, :, :], y[:, :, :], wide(dis), ALU.mult)),
                ("v", lambda: v.tensor_tensor(xS[:, :, :], xS[:, :, :], y[:, :, :], ALU.add))])
            copy_dma(nc, "end", [(s_layout(out), xS[:, :, :])])


_INS = ["x", "src", "dst", "edge_attr_16", "edge_weight", "edge_weight_n2", "L0_gnn_W", "L0_gnn_b", "L0_gnn_deg_coeff",
        "L0_gnn_coeff_param", "L0_gnn_scale_param", "L2_gnn_W1", "L2_gnn_b1", "L2_gnn_W2", "L2_gnn_b2",
        "L3_gnn_W_edge", "L3_gnn_b_edge", "L3_gnn_W_node", "L3_gnn_b_node"]


def kernel(**inputs):
    import numpy as _np
    import concourse.bacc as _bacc
    from concourse import mybir as _mybir
    from concourse.bass_utils import run_bass_kernel_spmd as _run

    nc = _bacc.Bacc("TRN2", target_bir_lowering=False, num_devices=1)
    arrays, args = {}, []
    for name in _INS:
        a = _np.ascontiguousarray(inputs[name])
        arrays[f"in_{name}"] = a
        args.append(nc.dram_tensor(f"in_{name}", a.shape, _mybir.dt.from_np(a.dtype), kind="ExternalInput").ap())
    args.append(nc.dram_tensor("out_x", (N, F), F32, kind="ExternalOutput").ap())
    four_layers(nc, *args)
    r = _run(nc, [arrays], core_ids=[0])
    return r.results[0]["out_x"]
```

```python
from contextlib import ExitStack, contextmanager

import concourse.bass as bass
from concourse import mybir

ALU = mybir.AluOpType
ACT = mybir.ActivationFunctionType
AX = mybir.AxisListType
F32 = mybir.dt.float32
BF16 = mybir.dt.bfloat16
I32 = mybir.dt.int32
U16 = mybir.dt.uint16

P = 128
N = 3125
F = 64
EA = 16
E = 103125
NB = 25
W = N // NB
T = -(-E // P)
EP = T * P
TAIL = E - (P - 1) * T
KEYS = NB + 1
STEP = -(-T // 4)
TQ = 4 * STEP
CODE = 256
CAP = 2
ROUND = CAP * P
HALF = 31
LOOPS = T // (2 * HALF)
MAGIC = 12582912.0
GROUPS = [3, 2] * 5
BANKS = [[0, 1, 2], [3, 4]]
SENT_COLS = 81
R2_ROWS = 2 * EP + 10 * P
assert 2 * HALF * LOOPS == T and sum(GROUPS) == NB


class Chain:

    def __init__(self, eng, sem, start=0):
        self.eng, self.sem, self.n = eng, sem, start

    def __call__(self, ins):
        self.n += 1
        ins.then_inc(self.sem, 1)
        self.eng.wait_ge(self.sem, self.n)


class Running:
    sems = {}

    def __init__(self, name):
        self.name = name
        self.sem, self.start = Running.sems[name]

    def at(self, n):
        return self.start + n

    def close(self, n):
        Running.sems[self.name] = (self.sem, self.start + n)


class Mem:

    def __init__(self, nc, name):
        self.nc, self.name, self.ctx = nc, name, ExitStack()

    def __enter__(self):
        return self

    def __exit__(self, *a):
        return self.ctx.__exit__(*a)

    def sb(self, name, shape, dt=F32):
        return self.ctx.enter_context(self.nc.sbuf_tensor(f"{self.name}_{name}", shape, dt))

    def ps(self, name, shape, dt=F32):
        return self.ctx.enter_context(self.nc.psum_tensor(f"{self.name}_{name}", shape, dt))

    def sem(self, name):
        return self.ctx.enter_context(self.nc.semaphore(f"{self.name}_{name}"))

    def block(self):
        return self.ctx.enter_context(self.nc.Block())


def constants(nc, m, k):
    with Mem(nc, "const") as l:
        col = l.sb("col", [P, P])
        row = l.sb("row", [P, 1])
        s_iota, s_c = l.sem("iota"), l.sem("c")
        block = l.block()

        @block.gpsimd
        def _(pool):
            nc.gpsimd.iota(col[:], [[1, P]], base=0, channel_multiplier=0,
                           allow_small_or_imprecise_dtypes=True).then_inc(s_iota, 1)
            nc.gpsimd.iota(row[:], [[1, 1]], base=0, channel_multiplier=1,
                           allow_small_or_imprecise_dtypes=True).then_inc(s_iota, 1)
            nc.gpsimd.iota(k["codes"][:], [[CODE, NB]], base=0, channel_multiplier=0,
                           allow_small_or_imprecise_dtypes=True).then_inc(s_iota, 1)
            nc.gpsimd.iota(k["numbers"][:, :, :], [[1, P], [0, CAP * max(GROUPS)]], base=0,
                           channel_multiplier=0,
                           allow_small_or_imprecise_dtypes=True).then_inc(s_iota, 1)

        @block.vector
        def _(dve):
            dve.wait_ge(s_iota, 4)
            nc.vector.tensor_scalar(k["ident"][:], col[:], row[:], None, ALU.is_equal).then_inc(s_c, 1)
            nc.vector.tensor_scalar(k["before"][:], col[:], row[:], None, ALU.is_gt).then_inc(s_c, 1)
            nc.vector.memset(k["ones"][:], 1.0).then_inc(s_c, 1)
            nc.vector.memset(k["ones16"][:], 1.0).then_inc(s_c, 1)
            nc.vector.memset(k["zeros"][:], 0.0).then_inc(s_c, 1)
            nc.vector.memset(k["zeros16"][:], 0.0).then_inc(s_c, 1)
            dve.wait_ge(s_c, 6)


def edge_records(nc, rec, src, dst, edge_attr, ew, ewn2, coeff, w_edge, b_edge):
    last = slice(96, P)
    with Mem(nc, "edges") as l:
        srci, dsti = l.sb("srci", [P, T], I32), l.sb("dsti", [P, T], I32)
        adj, deg = l.sb("adj", [P, T]), l.sb("deg", [P, T])
        attr, prod = l.sb("attr", [P, T, EA]), l.sb("prod", [P, T, EA])
        cf, we, be = l.sb("cf", [P, 2]), l.sb("we", [P, EA]), l.sb("be", [P, 1])
        sf, df, q, t1 = (l.sb(x, [P, T]) for x in ("sf", "df", "q", "t1"))
        x, ax, ex, u, lg = (l.sb(y, [P, T]) for y in ("x", "ax", "ex", "u", "lg"))
        z = l.sb("z", [P, T])
        pad = l.sb("pad", [P, T - TAIL])
        s_zero, s_i, s_w, s_a, s_p = (l.sem(y) for y in ("zero", "i", "w", "a", "p"))
        s_dve, s_act, s_pad = l.sem("dve"), l.sem("act"), l.sem("pad")
        block = l.block()

        def load(eng, tile, dram, sem):
            eng.dma_start(tile[0:P - 1, :], dram[0:(P - 1) * T].rearrange("(p t) -> p t", t=T)).then_inc(sem, 16)
            eng.dma_start(tile[P - 1:P, 0:TAIL], dram[(P - 1) * T:E].rearrange("(p t) -> p t", p=1)).then_inc(sem, 16)

        @block.sync
        def _(sp):
            sp.wait_ge(s_zero, 5)
            load(sp, srci, src, s_i)
            load(sp, dsti, dst, s_i)
            sp.dma_start(attr[0:P - 1, :, :], edge_attr[0:(P - 1) * T, :].rearrange("(p t) a -> p t a", t=T)).then_inc(s_a, 16)
            sp.dma_start(attr[P - 1:P, 0:TAIL, :], edge_attr[(P - 1) * T:E, :].rearrange("(p t) a -> p t a", p=1)).then_inc(s_a, 16)

        @block.scalar
        def _(act):
            act.dma_start(cf[:], coeff.rearrange("(a n) -> a n", a=1).to_broadcast([P, 2])).then_inc(s_p, 16)
            act.dma_start(we[:], w_edge.rearrange("a b -> b a").to_broadcast([P, EA])).then_inc(s_p, 16)
            act.dma_start(be[:], b_edge.rearrange("(a n) -> a n", a=1).to_broadcast([P, 1])).then_inc(s_p, 16)
            act.wait_ge(s_zero, 5)
            load(act, adj, ew, s_w)
            load(act, deg, ewn2, s_w)
            act.wait_ge(s_dve, 2)
            nc.scalar.activation(ex[:], ax[:], ACT.Exp, scale=-1.0).then_inc(s_act, 1)
            act.wait_ge(s_dve, 3)
            nc.scalar.activation(lg[:], u[:], ACT.Ln).then_inc(s_act, 1)
            act.wait_ge(s_dve, 10)
            nc.scalar.activation(rec[:, :, 2], z[:], ACT.Sigmoid, bias=be[:]).then_inc(s_act, 1)

        @block.gpsimd
        def _(pool):
            nc.gpsimd.iota(pad[:], [[1, T - TAIL]], base=TAIL, channel_multiplier=T,
                           allow_small_or_imprecise_dtypes=True).then_inc(s_pad, 1)

        @block.vector
        def _(dve):
            nc.vector.memset(srci[last, TAIL:T], 0).then_inc(s_zero, 1)
            nc.vector.memset(dsti[last, TAIL:T], 0).then_inc(s_zero, 1)
            nc.vector.memset(adj[last, TAIL:T], 0.0).then_inc(s_zero, 1)
            nc.vector.memset(deg[last, TAIL:T], 0.0).then_inc(s_zero, 1)
            nc.vector.memset(attr[last, TAIL:T, :], 0.0).then_inc(s_zero, 1)
            c = Chain(dve, s_dve)
            dve.wait_ge(s_p, 48)
            dve.wait_ge(s_w, 64)
            c(nc.vector.tensor_scalar(x[:], deg[:], cf[:, 0:1], cf[:, 1:2], ALU.mult, ALU.add))
            c(nc.vector.scalar_tensor_tensor(ax[:], x[:], -1.0, x[:], ALU.mult, ALU.max))
            dve.wait_ge(s_act, 1)
            c(nc.vector.tensor_scalar(u[:], ex[:], 1.0, None, ALU.add))
            c(nc.vector.tensor_scalar(q[:], u[:], -1.0, None, ALU.add))
            c(nc.vector.tensor_scalar(t1[:], q[:], 0.0, None, ALU.is_equal))
            c(nc.vector.tensor_tensor(q[:], q[:], t1[:], ALU.add))
            c(nc.vector.reciprocal(sf[:], q[:]))
            c(nc.vector.tensor_tensor(df[:], sf[:], ex[:], ALU.mult))
            dve.wait_ge(s_a, 32)
            c(nc.vector.tensor_tensor(prod[:, :, :], attr[:, :, :], we[:, None, :].to_broadcast([P, T, EA]), ALU.mult))
            c(nc.vector.tensor_reduce(z[:], prod[:, :, :], AX.X, ALU.add))
            dve.wait_ge(s_act, 2)
            c(nc.vector.tensor_tensor(lg[:], lg[:], t1[:], ALU.add))
            c(nc.vector.tensor_tensor(lg[:], lg[:], df[:], ALU.mult))
            c(nc.vector.scalar_tensor_tensor(lg[:], x[:], 0.0, lg[:], ALU.max, ALU.add))
            c(nc.vector.tensor_tensor(lg[:], lg[:], adj[:], ALU.mult))
            dve.wait_ge(s_i, 64)
            c(nc.vector.tensor_copy(sf[:], srci[:]))
            c(nc.vector.tensor_copy(df[:], dsti[:]))
            c(nc.vector.tensor_tensor(t1[:], sf[:], df[:], ALU.not_equal))
            c(nc.vector.tensor_tensor(rec[:, :, 3], lg[:], t1[:], ALU.mult))
            c(nc.vector.tensor_scalar(q[:], sf[:], -float(NB // 2), 1.0 / NB, ALU.add, ALU.mult))
            c(nc.vector.tensor_scalar(q[:], q[:], MAGIC, -MAGIC, ALU.add, ALU.add))
            c(nc.vector.tensor_scalar(t1[:], sf[:], float(CODE), None, ALU.mult))
            c(nc.vector.scalar_tensor_tensor(rec[:, :, 0], q[:], float(1 - CODE * NB), t1[:], ALU.mult, ALU.add))
            c(nc.vector.tensor_copy(rec[:, :, 1], df[:]))
            dve.wait_ge(s_pad, 1)
            c(nc.vector.tensor_scalar(pad[:], pad[:], float(E), None, ALU.is_ge))
            c(nc.vector.scalar_tensor_tensor(rec[:, TAIL:T, 0], pad[:], float(CODE * NB), rec[:, TAIL:T, 0], ALU.mult, ALU.add))
            c(nc.vector.scalar_tensor_tensor(rec[:, TAIL:T, 1], pad[:], float(N), rec[:, TAIL:T, 1], ALU.mult, ALU.add))
            dve.wait_ge(s_act, 3)


def mask_steps(nc, dve, c, sem, rec, field, inv, half, masks, key):
    c(nc.vector.memset(masks[:, :, :], 0.0))
    c(nc.vector.tensor_scalar(key[:], rec[:, :, field], -float(half), inv, ALU.add, ALU.mult))
    c(nc.vector.tensor_scalar(key[:], key[:], MAGIC, -MAGIC, ALU.add, ALU.add))
    for j in range(KEYS):
        nc.vector.tensor_scalar(masks[:, j, 0:T], key[:], float(j), None, ALU.is_equal).then_inc(sem, 1)
    c.n += KEYS
    dve.wait_ge(sem, c.n)


def key_masks(nc, rec, field, inv, masks, half):
    with Mem(nc, "masks") as l:
        key, s = l.sb("key", [P, T]), l.sem("s")
        block = l.block()

        @block.vector
        def _(dve):
            mask_steps(nc, dve, Chain(dve, s), s, rec, field, inv, half, masks, key)


@contextmanager
def only_if(eng, flag):
    if flag is None:
        yield
    else:
        with eng.If(eng.value_load(flag, min_val=0, max_val=1) > 0):
            yield


def order_check(nc, k, rec, flag):
    with Mem(nc, "order") as l:
        key, falls = l.sb("key", [P, T]), l.sb("falls", [P, T])
        total = l.sb("total", [P, 2])
        ps = l.ps("ps", [P, 2, 512])
        s_dve, s_pe = l.sem("dve"), l.sem("pe")
        block = l.block()

        @block.vector
        def _(dve):
            c = Chain(dve, s_dve)
            c(nc.vector.tensor_scalar(key[:], rec[:, :, 1], -float(W // 2), 1.0 / W, ALU.add, ALU.mult))
            c(nc.vector.tensor_scalar(key[:], key[:], MAGIC, -MAGIC, ALU.add, ALU.add))
            c(nc.vector.tensor_tensor(falls[:, 0:T - 1], key[:, 0:T - 1], key[:, 1:T], ALU.is_gt))
            c(nc.vector.memset(falls[:, T - 1:T], 0.0))
            dve.wait_ge(s_pe, 1)
            c(nc.vector.tensor_tensor(falls[0:P - 1, T - 1:T], key[0:P - 1, T - 1:T], ps[0:P - 1, 0, 0:1], ALU.is_gt))
            c(nc.vector.tensor_reduce(total[:, 0:1], falls[:], AX.X, ALU.add))
            dve.wait_ge(s_pe, 2)
            c(nc.vector.tensor_scalar(total[:, 1:2], ps[:, 1, 0:1], 1.0, None, ALU.min))
            c(nc.vector.tensor_copy(flag, total[0:1, 1:2]))

        @block.tensor
        def _(pe):
            pe.wait_ge(s_dve, 2)
            nc.tensor.matmul(ps[0:P - 1, 0, 0:1], k["ident"][:, 1:P], key[:, 0:1], start=True, stop=True).then_inc(s_pe, 1)
            pe.wait_ge(s_dve, 6)
            nc.tensor.matmul(ps[:, 1, 0:1], k["ones"][:], total[:, 0:1], start=True, stop=True).then_inc(s_pe, 1)


def ranks(nc, name, k, rec, field, inv, masks, pos, half, flag=None):
    with Mem(nc, name) as l:
        key = l.sb("key", [P, T])
        cnt, off, tot, cum = (l.sb(x, [P, KEYS]) for x in ("cnt", "off", "tot", "cum"))
        run = l.sb("run", [P, 2, T])
        both = l.ps("both", [P, 2, 512])
        s_dve, s_pe = l.sem("dve"), l.sem("pe")
        block = l.block()
        n_cnt = [0]

        @block.vector
        def _(dve):
            with only_if(dve, flag):
                c = Chain(dve, s_dve)
                mask_steps(nc, dve, c, s_dve, rec, field, inv, half, masks, key)
                c(nc.vector.tensor_reduce(cnt[:], masks[:, 0:KEYS, 0:T], AX.X, ALU.add))
                n_cnt[0] = c.n
                dve.wait_ge(s_pe, 1)
                c(nc.vector.tensor_copy(tot[:], both[:, 1, 0:KEYS]))
                c(nc.vector.tensor_tensor_scan(cum[:], tot[:], tot[:], -1.0, ALU.add, ALU.bypass))
                c(nc.vector.tensor_tensor(cum[:], cum[:], tot[:], ALU.subtract))
                c(nc.vector.tensor_tensor(off[:], cum[:], both[:, 0, 0:KEYS], ALU.add))
                for j in range(KEYS):
                    c(nc.vector.tensor_tensor_scan(run[:, j % 2, :], masks[:, j, 0:T], masks[:, j, 0:T], off[:, j:j + 1],
                                                   ALU.add, ALU.bypass))
                    if j == 0:
                        c(nc.vector.tensor_copy(pos[:], run[:, 0, :]))
                    else:
                        c(nc.vector.copy_predicated(pos[:], masks[:, j, 0:T].bitcast(U16), run[:, j % 2, :]))

        @block.tensor
        def _(pe):
            with only_if(pe, flag):
                pe.wait_ge(s_dve, n_cnt[0])
                nc.tensor.matmul(both[:, 0, 0:KEYS], k["before"][:], cnt[:], start=True, stop=True)
                nc.tensor.matmul(both[:, 1, 0:KEYS], k["ones"][:], cnt[:], start=True, stop=True).then_inc(s_pe, 1)


def scatter(nc, name, k, rec, pos, out, flag=None):
    with Mem(nc, name) as l:
        at = l.sb("at", [P, 2, HALF], I32)
        what = l.sb("what", [P, 2, HALF, 4])
        s_staged = [l.sem("staged0"), l.sem("staged1")]
        s_out = [l.sem("out0"), l.sem("out1")]
        s_turn = [l.sem("turn0"), l.sem("turn1")]
        turn, k_one = l.sb("turn", [P, 2]), k["ones"]
        block = l.block()

        @block.vector
        def _(dve):
            with only_if(dve, flag):
                def stage(h, t):
                    nc.vector.tensor_copy(at[:, h, :], pos[:, t]).then_inc(s_staged[h], 1)
                    nc.vector.tensor_copy(what[:, h, :, :], rec[:, t, :]).then_inc(s_staged[h], 1)

                for h in range(2):
                    stage(h, slice(h * HALF, (h + 1) * HALF))
                with dve.Fori(1, LOOPS) as i:
                    for h in range(2):
                        dve.wait_ge(s_out[h], i * (16 * HALF))
                        stage(h, bass.ds((2 * i + h) * HALF, HALF))

        @block.gpsimd
        def _(pool):
            with only_if(pool, flag):
                for h in range(2):
                    nc.gpsimd.memset(turn[:, h:h + 1], 0.0).then_inc(s_turn[h], 1)
                with pool.Fori(0, LOOPS) as i:
                    for h in range(2):
                        pool.wait_ge(s_staged[h], 2 * i + 2)
                        pool.wait_ge(s_turn[h], i + 1)
                        nc.gpsimd.tensor_tensor(turn[:, h:h + 1], k_one[:, 0:1], k_one[:, 0:1], ALU.add).then_inc(s_turn[h], 1)
                        for t in range(HALF):
                            pool.indirect_dma_start(out, bass.IndirectOffsetOnAxis(ap=at[:, h, t:t + 1], axis=0),
                                                    what[:, h, t, :], None).then_inc(s_out[h], 16)
                for h in range(2):
                    pool.wait_ge(s_out[h], 16 * HALF * LOOPS)


def reload(nc, name, rec, out, flag=None):
    with Mem(nc, name) as l:
        s = l.sem("s")
        block = l.block()

        @block.sync
        def _(sp):
            with only_if(sp, flag):
                sp.dma_start(rec[:, :, :], out[0:EP, :].rearrange("(p t) f -> p t f", p=P)).then_inc(s, 16)
                sp.wait_ge(s, 16)


def sentinels(nc, out):
    with Mem(nc, "sent") as l:
        tile = l.sb("tile", [P, SENT_COLS, 4])
        s_set, s_out = l.sem("set"), l.sem("out")
        block = l.block()

        @block.vector
        def _(dve):
            nc.vector.memset(tile[:, :, 0], float(CODE * NB)).then_inc(s_set, 1)
            nc.vector.memset(tile[:, :, 1], float(N)).then_inc(s_set, 1)
            nc.vector.memset(tile[:, :, 2:4], 0.0).then_inc(s_set, 1)

        @block.sync
        def _(sp):
            sp.wait_ge(s_set, 3)
            at, n = EP, 0
            while at < R2_ROWS:
                cols = min(SENT_COLS, (R2_ROWS - at) // P)
                sp.dma_start(out[at:at + P * cols, :].rearrange("(p t) f -> p t f", p=P), tile[:, 0:cols, :]).then_inc(s_out, 16)
                at += P * cols
                n += 16
            sp.wait_ge(s_out, n)


def bucket_table(nc, by_src, by_dst, hist_dram, table):
    Q = NB * NB
    with Mem(nc, "hist") as l:
        acc = l.ps("acc", [P, P])
        h = l.sb("h", [P, P])
        row, cum, st = l.sb("row", [1, 4, Q]), l.sb("cum", [1, Q]), l.sb("st", [1, Q])
        mx = l.sb("mx", [1, 4])
        s_pe, s_dve, s_io = l.sem("pe"), l.sem("dve"), l.sem("io")
        block = l.block()

        @block.tensor
        def _(pe):
            a = by_src.rearrange("p j (a t) -> p (j a) t", t=STEP)
            b = by_dst.rearrange("p j (a t) -> p (j a) t", t=STEP)

            def step(t, start=False, stop=False):
                return nc.tensor.matmul(acc[:], a[:, :, t], b[:, :, t], start=start, stop=stop)

            UN = 8
            loops = (STEP - 2) // UN
            step(0, start=True)
            with pe.Fori(0, loops) as i:
                for j in range(UN):
                    step(bass.ds(i * UN + (j + 1), 1))
            for t in range(1 + loops * UN, STEP - 1):
                step(t)
            step(STEP - 1, stop=True).then_inc(s_pe, 1)

        @block.vector
        def _(dve):
            c = Chain(dve, s_dve)
            dve.wait_ge(s_pe, 1)
            c(nc.vector.tensor_copy(h[:], acc[:]))
            dve.wait_ge(s_io, 80)
            for a in range(1, 4):
                c(nc.vector.tensor_tensor(row[:, 0, :], row[:, 0, :], row[:, a, :], ALU.add))
            c(nc.vector.tensor_tensor_scan(cum[:], row[:, 0, :], row[:, 0, :], 0.0, ALU.add, ALU.bypass))
            c(nc.vector.tensor_tensor(st[:], cum[:], row[:, 0, :], ALU.subtract))
            c(nc.vector.tensor_copy(table[0:1, 0:Q], st[:]))
            c(nc.vector.tensor_reduce(mx[:, 0:1], row[:, 0, :], AX.X, ALU.max))
            c(nc.vector.tensor_scalar(mx[:, 1:2], mx[:, 0:1], ROUND / 2 - 0.5, 1.0 / ROUND, ALU.add, ALU.mult))
            c(nc.vector.tensor_scalar(mx[:, 2:3], mx[:, 1:2], MAGIC, -MAGIC, ALU.add, ALU.add))
            c(nc.vector.tensor_copy(table[0:1, Q:Q + 1], mx[:, 2:3]))

        @block.sync
        def _(sp):
            sp.wait_ge(s_dve, 1)
            sp.dma_start(hist_dram, h[:]).then_inc(s_io, 16)
            sp.wait_ge(s_io, 16)
            view = hist_dram.rearrange("(s a) (d b) -> a s d b", a=4, b=4)
            for a in range(4):
                sp.dma_start(row[:, a, :].rearrange("p (s d) -> p s d", s=NB), view[a:a + 1, 0:NB, 0:NB, a],
                             allow_slow_non_contiguous=True).then_inc(s_io, 16)


def d_layout(dram):
    return dram.rearrange("(c p) f -> p c f", p=W)


def s_layout(dram):
    return dram.rearrange("(p c) f -> p c f", c=NB)


def copy_dma(nc, name, pairs):
    with Mem(nc, name) as l:
        moved = Running("moved")
        block = l.block()

        @block.sync
        def _(sp):
            for i, (out, in_) in enumerate(pairs):
                sp.dma_start(out, in_, allow_slow_non_contiguous=True).then_inc(moved.sem, 16)
                sp.wait_ge(moved.sem, moved.at(16 * (i + 1)))
        moved.close(16 * len(pairs))


def layer_norm_relu(nc, name, x, h, xc):
    with Mem(nc, name) as l:
        mean, var, std, inv = (l.sb(y, [W, NB]) for y in ("mean", "var", "std", "inv"))
        eps = l.sb("eps", [W, 1])
        r_dve, r_act = Running("norm_dve"), Running("norm_act")
        block = l.block()
        full = [W, NB, F]

        @block.vector
        def _(dve):
            c = Chain(dve, r_dve.sem, r_dve.start)
            c(nc.vector.memset(eps[:], 1e-5))
            c(nc.vector.tensor_reduce(mean[:], x[:, :, :], AX.X, ALU.add))
            c(nc.vector.tensor_scalar(mean[:], mean[:], 1.0 / F, None, ALU.mult))
            c(nc.vector.tensor_tensor(xc[:, :, :], x[:, :, :], mean[:, :, None].to_broadcast(full), ALU.subtract))
            c(nc.vector.tensor_tensor(h[:, :, :], xc[:, :, :], xc[:, :, :], ALU.mult))
            c(nc.vector.tensor_reduce(var[:], h[:, :, :], AX.X, ALU.add))
            dve.wait_ge(r_act.sem, r_act.at(1))
            c(nc.vector.reciprocal(inv[:], std[:]))
            c(nc.vector.scalar_tensor_tensor(h[:, :, :], xc[:, :, :], 0.0, inv[:, :, None].to_broadcast(full), ALU.max, ALU.mult))

        @block.scalar
        def _(act):
            act.wait_ge(r_dve.sem, r_dve.at(6))
            nc.scalar.activation(std[:], var[:], ACT.Sqrt, bias=eps[:], scale=1.0 / F).then_inc(r_act.sem, 1)
        r_dve.close(8)
        r_act.close(1)


def transpose_nodes(nc, name, k, h, hT):
    with Mem(nc, name) as l:
        ps = l.ps("ps", [F, 2, 512])
        r_pe, r_cp = Running("made"), Running("read_dve")
        block = l.block()
        lots = [list(range(b, min(b + 4, NB))) for b in range(0, NB, 4)]

        @block.tensor
        def _(pe):
            for i, lot in enumerate(lots):
                if i >= 2:
                    pe.wait_ge(r_cp.sem, r_cp.at(i - 1))
                for j, b in enumerate(lot):
                    ins = nc.tensor.transpose(ps[:, i % 2, W * j:W * j + W], h[:, b, :], k["ident"][0:W, 0:W])
                ins.then_inc(r_pe.sem, 1)

        @block.vector
        def _(dve):
            for i, lot in enumerate(lots):
                dve.wait_ge(r_pe.sem, r_pe.at(i + 1))
                w = W * len(lot)
                nc.vector.tensor_copy(hT[:, W * lot[0]:W * lot[0] + w], ps[:, i % 2, 0:w]).then_inc(r_cp.sem, 1)
        r_pe.close(len(lots))
        r_cp.close(len(lots))


def dense_T(nc, name, w, hT, out, bias, relu):
    with Mem(nc, name) as l:
        ps = l.ps("ps", [F, 2, 512])
        r_pe, r_cp = Running("made"), Running("read_act")
        block = l.block()
        cuts = [(a, min(500, N - a)) for a in range(0, N, 500)]

        @block.tensor
        def _(pe):
            for i, (a, n) in enumerate(cuts):
                if i >= 2:
                    pe.wait_ge(r_cp.sem, r_cp.at(i - 1))
                nc.tensor.matmul(ps[:, i % 2, 0:n], w, hT[:, a:a + n], start=True, stop=True).then_inc(r_pe.sem, 1)

        @block.scalar
        def _(act):
            for i, (a, n) in enumerate(cuts):
                act.wait_ge(r_pe.sem, r_pe.at(i + 1))
                nc.scalar.activation(out[:, a:a + n], ps[:, i % 2, 0:n], ACT.Relu if relu else ACT.Identity,
                                     bias=bias).then_inc(r_cp.sem, 1)
        r_pe.close(len(cuts))
        r_cp.close(len(cuts))


def dense(nc, name, cols, w, out, bias, relu=False):
    with Mem(nc, name) as l:
        ps = l.ps("ps", [W, 2, 8, F])
        r_pe, r_cp = Running("made"), Running("read_dve")
        block = l.block()
        lots = [list(range(b, min(b + 8, NB))) for b in range(0, NB, 8)]

        @block.tensor
        def _(pe):
            for i, lot in enumerate(lots):
                if i >= 2:
                    pe.wait_ge(r_cp.sem, r_cp.at((i - 1) * (1 + relu)))
                for j, b in enumerate(lot):
                    ins = nc.tensor.matmul(ps[:, i % 2, j, :], cols(b), w, start=True, stop=True)
                ins.then_inc(r_pe.sem, 1)

        @block.vector
        def _(dve):
            n = 0
            for i, lot in enumerate(lots):
                dve.wait_ge(r_pe.sem, r_pe.at(i + 1))
                part = out[:, lot[0]:lot[0] + len(lot), :]
                nc.vector.tensor_tensor(part, ps[:, i % 2, 0:len(lot), :],
                                        bias[0:W, None, :].to_broadcast([W, len(lot), F]), ALU.add).then_inc(r_cp.sem, 1)
                if relu:
                    n += 2
                    dve.wait_ge(r_cp.sem, r_cp.at(n - 1))
                    nc.vector.tensor_scalar(part, part, 0.0, None, ALU.max).then_inc(r_cp.sem, 1)
        r_pe.close(len(lots))
        r_cp.close(len(lots) * (1 + relu))


def inverse_norms(nc, name, wh, rn):
    with Mem(nc, name) as l:
        sq = l.sb("sq", [W, NB, F])
        ss = l.sb("ss", [W, NB])
        nr = l.sb("nr", [W, NB])
        s_dve, s_act = l.sem("dve"), l.sem("act")
        block = l.block()

        @block.vector
        def _(dve):
            c = Chain(dve, s_dve)
            c(nc.vector.tensor_tensor(sq[:, :, :], wh[:, :, :], wh[:, :, :], ALU.mult))
            c(nc.vector.tensor_reduce(ss[:], sq[:, :, :], AX.X, ALU.add))
            dve.wait_ge(s_act, 1)
            c(nc.vector.tensor_scalar(nr[:], nr[:], 1e-18, None, ALU.max))
            c(nc.vector.reciprocal(rn[:], nr[:]))

        @block.scalar
        def _(act):
            act.wait_ge(s_dve, 2)
            nc.scalar.activation(nr[:], ss[:], ACT.Sqrt).then_inc(s_act, 1)


def coefficients(nc, coeff_param, scale_param, coef):
    with Mem(nc, "coef") as l:
        cp, sp_ = l.sb("cp", [P, 3]), l.sb("sp", [P, 1])
        ex, t, u = l.sb("ex", [P, 3]), l.sb("t", [P, 8]), l.sb("u", [P, 1])
        s_in, s_dve, s_act = l.sem("in"), l.sem("dve"), l.sem("act")
        block = l.block()

        @block.sync
        def _(sp):
            sp.dma_start(cp[:], coeff_param.rearrange("(a n) -> a n", a=1).to_broadcast([P, 3])).then_inc(s_in, 16)
            sp.dma_start(sp_[:], scale_param.rearrange("(a n) -> a n", a=1).to_broadcast([P, 1])).then_inc(s_in, 16)

        @block.vector
        def _(dve):
            c = Chain(dve, s_dve)
            dve.wait_ge(s_in, 32)
            c(nc.vector.tensor_reduce(t[:, 0:1], cp[:], AX.X, ALU.max))
            c(nc.vector.tensor_scalar(cp[:], cp[:], t[:, 0:1], None, ALU.subtract))
            c(nc.vector.scalar_tensor_tensor(t[:, 1:2], sp_[:], -1.0, sp_[:], ALU.mult, ALU.max))
            dve.wait_ge(s_act, 2)
            c(nc.vector.tensor_scalar(u[:], t[:, 2:3], 1.0, None, ALU.add))
            c(nc.vector.tensor_scalar(t[:, 3:4], u[:], -1.0, None, ALU.add))
            c(nc.vector.tensor_scalar(t[:, 4:5], t[:, 3:4], 0.0, None, ALU.is_equal))
            c(nc.vector.tensor_tensor(t[:, 3:4], t[:, 3:4], t[:, 4:5], ALU.add))
            c(nc.vector.reciprocal(t[:, 5:6], t[:, 3:4]))
            dve.wait_ge(s_act, 3)
            c(nc.vector.tensor_tensor(t[:, 6:7], t[:, 6:7], t[:, 4:5], ALU.add))
            c(nc.vector.tensor_tensor(t[:, 6:7], t[:, 6:7], t[:, 2:3], ALU.mult))
            c(nc.vector.tensor_tensor(t[:, 6:7], t[:, 6:7], t[:, 5:6], ALU.mult))
            c(nc.vector.scalar_tensor_tensor(t[:, 6:7], sp_[:], 0.0, t[:, 6:7], ALU.max, ALU.add))
            c(nc.vector.tensor_reduce(t[:, 0:1], ex[:], AX.X, ALU.add))
            c(nc.vector.reciprocal(t[:, 7:8], t[:, 0:1]))
            c(nc.vector.tensor_tensor(t[:, 7:8], t[:, 7:8], t[:, 6:7], ALU.mult))
            c(nc.vector.tensor_scalar(coef[:], ex[:], t[:, 7:8], None, ALU.mult))
            c(nc.vector.tensor_scalar(coef[:, 1:2], coef[:, 1:2], -1.0, None, ALU.mult))

        @block.scalar
        def _(act):
            act.wait_ge(s_dve, 3)
            nc.scalar.activation(ex[:], cp[:], ACT.Exp).then_inc(s_act, 1)
            nc.scalar.activation(t[:, 2:3], t[:, 1:2], ACT.Exp, scale=-1.0).then_inc(s_act, 1)
            act.wait_ge(s_dve, 4)
            nc.scalar.activation(t[:, 6:7], u[:], ACT.Ln).then_inc(s_act, 1)


def build_rows(nc, k, sorted_, table, whT, whTs, whD, rnD, rn_row, coef, prop, cnt, deg, c16_dram, c_dram,
               g_dram, prime_dram):
    NG, LINKS = len(GROUPS), 10
    FIRST = [sum(GROUPS[:g]) for g in range(NG)]
    MAXG, C = max(GROUPS), CAP * NB
    OH, EV = 10, 6
    V = W + 1
    with Mem(nc, "rows") as l:
        recrow = l.sb("recrow", [P, 2, NB, CAP, 4])
        dbase = l.sb("dbase", [P, NB, CAP])
        sbase = l.sb("sbase", [P, 1])
        keys, inside, low = (l.sb(x, [P, 2, C], BF16) for x in ("keys", "inside", "low"))
        skey, dkey = keys[:, 0], keys[:, 1]
        parts = l.sb("parts", [P, 3, 2, C], BF16)
        rest = l.sb("rest", [P, 2, 2, C])
        soh = [l.sb(f"soh{b}", [P, P, CAP * GROUPS[b]], BF16) for b in range(2)]
        doh = [l.sb(f"doh{b}", [P, P, CAP * GROUPS[b]], BF16) for b in range(2)]
        wsrc = [l.sb(f"wsrc{b}", [P, 6, P, CAP * GROUPS[b]], BF16) for b in range(2)]
        c16_row, g_row, c_row = l.sb("c16_row", [P, 2, N], BF16), l.sb("g_row", [P, 2, N]), l.sb("c_row", [P, N])
        pos_s, neg_s, wt, fac = (l.sb(x, [W, 2, MAXG, W]) for x in ("pos_s", "neg_s", "wt", "fac"))
        b0 = l.sb("b0", [W, 2, MAXG, W])
        counts = l.sb("counts", [W, NB, NB, 2])
        count = l.sb("count", [W, 2, NB])
        ps = l.ps("ps", [P, 8, 512])
        names = ("loaded taken onehot products evacuated factor signed blocks used added link ready counted stored_c "
                 "stored_g further start")
        s = {x: l.sem(x) for x in names.split()}
        block = l.block()
        MAIN, TAIL_ = 5, 6

        def bank(g, lo, width, rows=P):
            a = BANKS[g % 2][0]
            return ps[0:rows, a:a + GROUPS[g], lo:lo + width]

        def plan(eng, body, after, between=None):
            with eng.Fori(0, NB) as row:
                body(row, row, 0, False)
            after(0)
            rounds = eng.value_load(table[0:1, NB * NB:NB * NB + 1], min_val=1, max_val=-(-E // ROUND))
            with eng.If(rounds > 1):
                if between:
                    between()
                with eng.Fori(1, rounds) as r:
                    with eng.Fori(0, NB) as row:
                        body(row, r * NB + row, r, True)
                    after(r)

        @block.sync
        def _(sp):
            def load(row, w, start_at):
                for d0 in range(0, NB, 5):
                    _, at = nc.values_load_multi_w_load_instructions(
                        table[0:1, bass.ds(row * NB + d0, 5)] if not isinstance(row, int) else table[0:1, row * NB + d0:row * NB + d0 + 5],
                        engines=[mybir.EngineType.SP], min_val=0, max_val=E)
                    for j in range(5):
                        dest = recrow[:, 0, d0 + j, :, :] if isinstance(w, int) else recrow[:, bass.ds(w % 2, 1), d0 + j, :, :]
                        sp.dma_start(dest, sorted_[bass.ds(start_at(at[j]), ROUND), :].rearrange("(p b) f -> p b f", b=CAP)
                                     ).then_inc(s["loaded"], 16)

            def body(row, w, r, more):
                sp.wait_ge(s["loaded"], w * (16 * NB))
                sp.wait_ge(s["taken"], w)
                load(row, w, (lambda a: a + r * ROUND) if more else (lambda a: a))

            load(0, 0, lambda a: a)
            with sp.Fori(1, NB) as row:
                body(row, row, 0, False)
            rounds = sp.value_load(table[0:1, NB * NB:NB * NB + 1], min_val=1, max_val=-(-E // ROUND))
            with sp.If(rounds > 1):
                with sp.Fori(1, rounds) as r:
                    with sp.Fori(0, NB) as row:
                        body(row, r * NB + row, r, True)

        @block.vector
        def _(dve):
            link = s["link"]

            def onehots(w, g):
                b, n = g % 2, CAP * GROUPS[g]
                lo = CAP * FIRST[g]
                gi = w * NG + g
                shape = [P, W, n]
                dve.wait_ge(s["products"], gi + 1)
                nums = k["numbers"][:, 0:W, 0:n]
                nc.vector.tensor_tensor(soh[b][:, 0:W, :], nums, keys[:, 0, None, lo:lo + n].to_broadcast(shape),
                                        ALU.is_equal).then_inc(s["onehot"], 1)
                nc.vector.tensor_tensor(doh[b][:, 0:W, :], nums, keys[:, 1, None, lo:lo + n].to_broadcast(shape),
                                        ALU.is_equal).then_inc(s["onehot"], 1)
                nc.vector.tensor_copy(wsrc[b][:, 0, W, :], inside[:, 0, lo:lo + n]).then_inc(s["onehot"], 1)
                nc.vector.tensor_copy(doh[b][:, W, :], inside[:, 1, lo:lo + n]).then_inc(s["onehot"], 1)
                dve.wait_ge(s["onehot"], gi * OH + 1)
                for q in range(6):
                    nc.vector.tensor_tensor(wsrc[b][:, q, 0:W, :], soh[b][:, 0:W, :],
                                            parts[:, q // 2, q % 2, None, lo:lo + n].to_broadcast(shape),
                                            ALU.mult).then_inc(s["onehot"], 1)

            def add_sums(row, bank_, used, added):
                dve.wait_ge(s["used"], used)
                dve.wait_ge(s["added"], added)
                p_row = prop[:, row, :] if isinstance(row, int) else prop[:, bass.ds(row, 1), :].rearrange("p a f -> p (a f)")
                nc.vector.tensor_tensor(p_row, p_row, ps[0:W, bank_, 0:F], ALU.add).then_inc(s["added"], 1)

            def body(row, w, r, more):
                dve.wait_ge(s["loaded"], (w + 1) * (16 * NB))
                base = w * LINKS
                at = [0]

                def c(ins):
                    at[0] += 1
                    ins.then_inc(link, 1)
                    dve.wait_ge(link, base + at[0])

                rec = recrow[:, bass.ds(w % 2, 1), :, :, :].rearrange("p a d c f -> p (a d c) f")
                c(nc.vector.tensor_copy(sbase[:], k["codes"][:, bass.ds(row, 1)]))
                c(nc.vector.tensor_scalar(skey, rec[:, :, 0], sbase[:], None, ALU.subtract))
                c(nc.vector.tensor_tensor(dkey, rec[:, :, 1], dbase[:, :, :].rearrange("p d c -> p (d c)"), ALU.subtract))
                c(nc.vector.tensor_scalar(low[:], keys[:], 0.0, None, ALU.is_ge))
                c(nc.vector.scalar_tensor_tensor(inside[:], keys[:], float(W), low[:], ALU.is_lt, ALU.mult))
                v = rec[:, :, 2:4].rearrange("p c f -> p f c")
                nc.vector.tensor_copy(rest[:, 0], v).then_inc(s["taken"], 1)
                dve.wait_ge(s["taken"], w + 2)
                c(nc.vector.tensor_copy(parts[:, 0], rest[:, 0]))
                c(nc.vector.tensor_tensor(rest[:, 1], rest[:, 0], parts[:, 0], ALU.subtract))
                c(nc.vector.tensor_copy(parts[:, 1], rest[:, 1]))
                c(nc.vector.tensor_tensor(rest[:, 0], rest[:, 1], parts[:, 1], ALU.subtract))
                c(nc.vector.tensor_copy(parts[:, 2], rest[:, 0]))
                u = w * NG + 2 * r + 1
                for g in range(NG):
                    onehots(w, g)
                    if g == 1:
                        add_sums(row, MAIN, u, 1 + 2 * w + 2 * r)
                    if g == 3:
                        add_sums(row, TAIL_, u + 2, 2 + 2 * w + 2 * r)

            def after(r):
                end = (r + 1) * NB
                add_sums(NB, MAIN, end * NG + 2 * r + 1, 1 + 2 * end + 2 * r)
                add_sums(NB, TAIL_, end * NG + 2 * r + 3, 2 + 2 * end + 2 * r)
                dve.wait_ge(s["evacuated"], 2 * EV + end * (NG * EV))
                dve.wait_ge(s["counted"], 4 * r + 1)
                nc.vector.tensor_reduce(count[:, 0, :], counts[:, :, :, 0], AX.X, ALU.add).then_inc(s["counted"], 1)
                nc.vector.tensor_reduce(count[:, 1, :], counts[:, :, :, 1].rearrange("p s d -> p d s"), AX.X,
                                        ALU.add).then_inc(s["counted"], 1)
                dve.wait_ge(s["counted"], 4 * r + 3)
                nc.vector.tensor_tensor(cnt[:], cnt[:], count[:, 0, :], ALU.add).then_inc(s["counted"], 1)
                nc.vector.tensor_tensor(deg[:], deg[:], count[:, 1, :], ALU.add).then_inc(s["counted"], 1)
                dve.wait_ge(s["counted"], 4 * r + 5)

            n = 0
            for tile in [cnt[:], deg[:], prop[:, :, :]] + [y[:, :, :] for y in soh + doh] + [y[:, :, :, :] for y in wsrc]:
                nc.vector.memset(tile, 0.0).then_inc(s["ready"], 1)
                n += 1
            nc.vector.memset(sbase[:], 0.0).then_inc(s["taken"], 1)
            nc.vector.memset(count[:, :, :], 0.0).then_inc(s["counted"], 1)
            nc.vector.memset(rest[:, 1], 0.0).then_inc(s["added"], 1)
            dve.wait_ge(s["ready"], n)
            dve.wait_ge(s["taken"], 1)
            dve.wait_ge(s["added"], 1)
            dve.wait_ge(s["start"], 1)
            plan(dve, body, after)

        @block.scalar
        def _(act):
            def body(row, w, r, more):
                if more:
                    act.wait_ge(s["further"], 16 + 32 * (w - NB))
                    act.wait_ge(s["counted"], 4 * r + 1)
                for g in range(NG):
                    b, n, gi = g % 2, GROUPS[g], w * NG + g
                    act.wait_ge(s["blocks"], gi + 1)
                    act.wait_ge(s["products"], gi + 3)
                    nc.scalar.activation(pos_s[:, b, 0:n, :], bank(g, 384, W, W), ACT.Relu, scale=coef[0:W, 0:1]).then_inc(s["evacuated"], 1)
                    nc.scalar.activation(neg_s[:, b, 0:n, :], bank(g, 384, W, W), ACT.Relu, scale=coef[0:W, 1:2]).then_inc(s["evacuated"], 1)
                    nc.scalar.activation(wt[:, b, 0:n, :], bank(g, 256, W, W), ACT.Copy).then_inc(s["evacuated"], 1)
                    for i in range(n):
                        d = FIRST[g] + i
                        nc.scalar.activation(fac[:, b, i, :], rn_row[:, bass.ds(row * W, W)], ACT.Copy,
                                             scale=rnD[:, d:d + 1]).then_inc(s["factor"], 1)
                    cols = slice(FIRST[g] * W, (FIRST[g] + n) * W)
                    half = bass.ds(w % 2, 1)
                    c_out = c_row[:, cols] if more else c16_row[:, half, cols].rearrange("p a w -> p (a w)")
                    nc.scalar.activation(c_out.rearrange("p (n w) -> p n w", w=W), bank(g, 0, W), ACT.Copy).then_inc(s["evacuated"], 1)
                    nc.scalar.activation(g_row[:, half, cols].rearrange("p a (n w) -> p (a n) w", w=W), bank(g, 128, W),
                                         ACT.Copy).then_inc(s["evacuated"], 1)
                    both = ps[0:W, BANKS[b][0]:BANKS[b][0] + n, W:W + 129:128]
                    nc.scalar.activation(counts[:, bass.ds(row, 1), FIRST[g]:FIRST[g] + n, :].rearrange("p a n v -> p (a n) v"),
                                         both, ACT.Copy).then_inc(s["evacuated"], 1)
                if not more:
                    act.wait_ge(s["evacuated"], 2 * EV + (w + 1) * (NG * EV))
                    act.wait_ge(s["stored_c"], 16 + 16 * w)
                    act.dma_start(c16_dram[bass.ds(row * P, P), :], c16_row[:, half, :].rearrange("p a n -> p (a n)")
                                  ).then_inc(s["stored_c"], 16)
                    act.wait_ge(s["stored_g"], 16 + 16 * w)
                    act.dma_start(g_dram[bass.ds(row * P, P), :], g_row[:, half, :].rearrange("p a n -> p (a n)")
                                  ).then_inc(s["stored_g"], 16)

            act.dma_start(prime_dram[0], k["ones"][:, 0:4]).then_inc(s["stored_c"], 16)
            act.dma_start(prime_dram[1], k["ones"][:, 0:4]).then_inc(s["stored_g"], 16)
            nc.scalar.activation(c_row[:, 0:1], k["ones"][:, 0:1], ACT.Copy).then_inc(s["evacuated"], 2 * EV)
            act.wait_ge(s["evacuated"], 2 * EV)
            plan(act, body, lambda r: None)
            act.wait_ge(s["stored_c"], 16 + 16 * NB)
            act.wait_ge(s["stored_g"], 16 + 16 * NB)

        @block.gpsimd
        def _(pool):
            def body(row, w, r, more):
                for g in range(NG):
                    b, n, gi = g % 2, GROUPS[g], w * NG + g
                    at = lambda tile: tile[:, b, 0:n, :]
                    pool.wait_ge(s["evacuated"], 2 * EV + EV * gi + 3)
                    pool.wait_ge(s["factor"], w * NB + FIRST[g] + n)
                    nc.gpsimd.tensor_tensor(at(pos_s), at(pos_s), at(neg_s), ALU.subtract).then_inc(s["signed"], 1)
                    nc.gpsimd.tensor_scalar(at(fac), at(fac), 1e8, None, ALU.min).then_inc(s["signed"], 1)
                    pool.wait_ge(s["signed"], 3 * gi + 2)
                    nc.gpsimd.tensor_tensor(at(wt), at(fac), at(wt), ALU.mult).then_inc(s["signed"], 1)
                    pool.wait_ge(s["used"], gi + 2 * r + 2)
                    pool.wait_ge(s["signed"], 3 * gi + 3)
                    nc.gpsimd.tensor_tensor(at(b0), at(pos_s), at(wt), ALU.mult).then_inc(s["blocks"], 1)
                if more:
                    pool.wait_ge(s["evacuated"], 2 * EV + (w + 1) * (NG * EV))
                    before = 16 + 32 * (w - NB)
                    pool.dma_start(c_dram[bass.ds(row * P, P), :].rearrange("p (b n) -> p b n", b=5),
                                   c_row[:, :].rearrange("p (b n) -> p b n", b=5), accum_op=ALU.add,
                                   max_dma_last_dim=N * 4 // 5).then_inc(s["further"], 16)
                    pool.wait_ge(s["further"], before + 16)
                    pool.dma_start(g_dram[bass.ds(row * P, P), :].rearrange("p (b n) -> p b n", b=5),
                                   g_row[:, bass.ds(w % 2, 1), :].rearrange("p a (b n) -> p (a b) n", b=5),
                                   accum_op=ALU.add,
                                   max_dma_last_dim=N * 4 // 5).then_inc(s["further"], 16)
                    pool.wait_ge(s["further"], before + 32)

            def widen():
                pool.wait_ge(s["stored_c"], 16 + 16 * NB)
                pool.wait_ge(s["stored_g"], 16 + 16 * NB)
                pool.dma_start(c_dram, c16_dram).then_inc(s["further"], 16)
                pool.wait_ge(s["further"], 16)

            nc.gpsimd.iota(dbase[:, :, :], [[W, NB], [0, CAP]], base=0, channel_multiplier=0,
                           allow_small_or_imprecise_dtypes=True).then_inc(s["start"], 1)
            for b in range(2):
                nc.gpsimd.memset(b0[:, b, :, :], 0.0).then_inc(s["blocks"], 1)
            plan(pool, body, lambda r: None, widen)

        @block.tensor
        def _(pe):
            def mm(out, lhsT, rhs, start=False):
                return nc.tensor.matmul(out, lhsT, rhs, start=start, stop=True, skip_group_check=True)

            def clear(bank_):
                return mm(ps[:, bank_, 0:F], k["zeros"][:, 0:P], k["zeros"][:, 0:F], True)

            def propagate(done, bank_, g):
                pe.wait_ge(s["blocks"], done)
                for i in range(GROUPS[g]):
                    ins = mm(ps[0:W, bank_, 0:F], b0[:, g % 2, i, :], whD[:, FIRST[g] + i, :])
                ins.then_inc(s["used"], 1)

            def body(row, w, r, more):
                for g in range(NG):
                    b, n, gi = g % 2, GROUPS[g], w * NG + g
                    pe.wait_ge(s["evacuated"], EV * gi + EV)
                    mm(ps[:, BANKS[b][0], 0:2], k["zeros16"][:], k["zeros16"][:, 0:2], True)
                    for i in range(n):
                        bk, d = BANKS[b][i], FIRST[g] + i
                        mm(ps[0:W, bk, 384:384 + W], whT[:, d * W:d * W + W], whTs[:, bass.ds(row, 1), :], i > 0)
                    pe.wait_ge(s["onehot"], OH * gi + OH)
                    for i in range(n):
                        bk, d = BANKS[b][i], FIRST[g] + i
                        out_ga = ps[:, bk, 128:384].rearrange("p (v w) -> p v w", v=2)
                        for cc in range(CAP * i, CAP * i + CAP):
                            for q in range(3):
                                cols = V if q == 0 else W
                                mm(out_ga[:, :, 0:cols], doh[b][:, :, cc], wsrc[b][:, 2 * q:2 * q + 2, 0:cols, cc])
                            ins = mm(ps[:, bk, 0:V], soh[b][:, :, cc], doh[b][:, 0:V, cc])
                    ins.then_inc(s["products"], 1)
                    if g == 0:
                        pe.wait_ge(s["added"], 1 + 2 * w + 2 * r)
                        clear(TAIL_)
                    if g == 2:
                        pe.wait_ge(s["added"], 2 + 2 * w + 2 * r)
                        clear(MAIN)
                    propagate(gi + 1, TAIL_ if g < 2 else MAIN, (g - 2) % NG)

            def after(r):
                end = (r + 1) * NB
                pe.wait_ge(s["added"], 1 + 2 * end + 2 * r)
                clear(TAIL_)
                propagate(end * NG + 1, TAIL_, NG - 2)
                propagate(end * NG + 2, TAIL_, NG - 1)

            clear(MAIN)
            clear(TAIL_).then_inc(s["used"], 1)
            mm(ps[:, BANKS[0][0], 0:2], k["zeros16"][:], k["zeros16"][:, 0:2], True).then_inc(s["products"], 1)
            mm(ps[:, BANKS[1][0], 0:2], k["zeros16"][:], k["zeros16"][:, 0:2], True).then_inc(s["products"], 1)
            plan(pe, body, after)


def product_c(nc, name, k, c16, c16_dram, c_dram, rounds_, u, u3, y, load):
    NBK = 8
    HALVES = [range(0, 12), range(12, NB)]
    LOT = 5
    with Mem(nc, name) as l:
        rows = [c16[:, b * 2 * N:(b + 1) * 2 * N].bitcast(F32) for b in range(2)]
        c_rows = c16[:, 0:NB * N].rearrange("p (s n) -> p s n", s=NB)
        ps = l.ps("ps", [P, 8, 512])
        s_in, s_pe = [l.sem("in0"), l.sem("in1")], [l.sem("pe0"), l.sem("pe1")]
        s_end, s_y = l.sem("end"), l.sem("y")
        s_c = [l.sem(f"c{q}") for q in range(NB // LOT)]
        s_split, s_half, s_sum = l.sem("split"), l.sem("half"), l.sem("sum")
        block = l.block()
        pairs = NB // 2
        sums = [(h, d, len(HALVES[h][i:i + 2]), (i // 2 + 6 * h) % 8)
                for h in range(2) for i, d in enumerate(HALVES[h]) if i % 2 == 0]

        def paths(eng, narrow, wide):
            rounds = eng.value_load(rounds_, min_val=1, max_val=-(-E // ROUND))
            with eng.If(rounds < 2):
                narrow()
            with eng.If(rounds > 1):
                wide()

        @block.sync
        def _(sp):
            def narrow():
                if load:
                    for q in range(NB // LOT):
                        sp.dma_start(c_rows[:, q * LOT:(q + 1) * LOT, :],
                                     c16_dram[q * LOT * P:(q + 1) * LOT * P, :].rearrange("(s p) n -> p s n", p=P)
                                     ).then_inc(s_c[q], 16)
                    for q in range(NB // LOT):
                        sp.wait_ge(s_c[q], 16)

            def wide():
                def fetch(b, row, i):
                    sp.wait_ge(s_pe[b], i + 1)
                    sp.dma_start(rows[b], c_dram[bass.ds(row * P, P), :]).then_inc(s_in[b], 16)

                with sp.Fori(0, pairs) as i:
                    fetch(0, 2 * i, i)
                    fetch(1, 2 * i + 1, i)
                fetch(0, NB - 1, pairs)
            paths(sp, narrow, wide)

        @block.tensor
        def _(pe):
            def mm(out, lhsT, rhs, start=False):
                return nc.tensor.matmul(out, lhsT, rhs, start=start, stop=True, skip_group_check=True)

            def narrow():
                pe.wait_ge(s_split, 5)
                for h in range(2):
                    mine = [x for x in sums if x[0] == h]
                    for _, d0, n, bk in mine:
                        if h == 1 and bk < 6:
                            pe.wait_ge(s_sum, bk + 1)
                        mm(ps[:, bk, 0:384], k["zeros16"][:], k["zeros16"][:, 0, None].to_broadcast([P, 384]), True)
                    for q in range(NB // LOT):
                        if load and h == 0:
                            pe.wait_ge(s_c[q], 16)
                        with pe.Fori(q * LOT, (q + 1) * LOT) as row:
                            for _, d0, n, bk in mine:
                                for i in range(n):
                                    d = d0 + i
                                    mm(ps[0:W, bk, i * 192:i * 192 + 192],
                                       c_rows[0:W, bass.ds(row, 1), d * W:d * W + W].rearrange("p a w -> p (a w)"),
                                       u3[:, bass.ds(row, 1), :, :].rearrange("p a q f -> p (a q f)"))
                    mm(ps[:, mine[-1][3], 0:2], k["zeros16"][:], k["zeros16"][:, 0:2]).then_inc(s_half, 1)

            def wide():
                def use(b, row, i):
                    pe.wait_ge(s_in[b], 16 * i + 16)
                    for d in range(NB):
                        ins = mm(ps[0:W, d // NBK, d % NBK * F:d % NBK * F + F], rows[b][0:W, d * W:d * W + W],
                                 u[:, bass.ds(row, 1), :])
                    return ins

                for q in range(4):
                    mm(ps[0:W, q, :], k["zeros"][0:W, 0:W], k["zeros"][0:W, :], True)
                for b in range(2):
                    mm(ps[:, 4 + b, 0:2], k["zeros16"][:], k["zeros16"][:, 0:2], True).then_inc(s_pe[b], 1)
                with pe.Fori(0, pairs) as i:
                    use(0, 2 * i, i).then_inc(s_pe[0], 1)
                    use(1, 2 * i + 1, i).then_inc(s_pe[1], 1)
                use(0, NB - 1, pairs).then_inc(s_end, 1)
            paths(pe, narrow, wide)

        @block.vector
        def _(dve):
            def narrow():
                c = Chain(dve, s_split)
                part = [u3[:, :, q, :] for q in range(3)]
                c(nc.vector.tensor_copy(part[0], u[:, :, :]))
                c(nc.vector.tensor_tensor(y[:, :, :], u[:, :, :], part[0], ALU.subtract))
                c(nc.vector.tensor_copy(part[1], y[:, :, :]))
                c(nc.vector.tensor_tensor(y[:, :, :], y[:, :, :], part[1], ALU.subtract))
                c(nc.vector.tensor_copy(part[2], y[:, :, :]))
                for n_, (h, d0, n, bk) in enumerate(sums):
                    dve.wait_ge(s_half, h + 1)
                    nc.vector.tensor_reduce(y[:, d0:d0 + n, :],
                                            ps[0:W, bk, 0:n * 192].rearrange("p (n q f) -> p n f q", n=n, q=3),
                                            AX.X, ALU.add).then_inc(s_sum, 1)
                dve.wait_ge(s_sum, len(sums))

            def wide():
                dve.wait_ge(s_end, 1)
                for q in range(4):
                    n = min(NBK, NB - NBK * q)
                    nc.vector.tensor_copy(y[:, NBK * q:NBK * q + n, :],
                                          ps[0:W, q, 0:n * F].rearrange("p (n f) -> p n f", f=F)).then_inc(s_y, 1)
                dve.wait_ge(s_y, 4)
            paths(dve, narrow, wide)


def product_g(nc, name, k, g_dram, u, y):
    with Mem(nc, name) as l:
        rows = [l.sb(f"row{b}", [P, N]) for b in range(2)]
        ps = l.ps("ps", [W, 2, 512])
        s_in, s_pe, s_y = [l.sem("in0"), l.sem("in1")], [l.sem("pe0"), l.sem("pe1")], [l.sem("y0"), l.sem("y1")]
        first = l.sb("first", [W, 2])
        block = l.block()
        pairs = NB // 2

        def plan(eng, step):
            with eng.Fori(0, pairs) as i:
                step(0, 2 * i, i)
                step(1, 2 * i + 1, i)
            step(0, NB - 1, pairs)

        @block.sync
        def _(sp):
            def load(b, row, i):
                sp.wait_ge(s_pe[b], i + 1)
                sp.dma_start(rows[b][:, :], g_dram[bass.ds(row * P, P), :]).then_inc(s_in[b], 16)
            plan(sp, load)

        @block.tensor
        def _(pe):
            def use(b, row, i):
                pe.wait_ge(s_in[b], 16 * i + 16)
                pe.wait_ge(s_y[b], i + 1)
                for d in range(NB):
                    ins = nc.tensor.matmul(ps[:, b, 0:F], rows[b][0:W, d * W:d * W + W], u[:, d, :],
                                           start=d == 0, stop=d == NB - 1)
                ins.then_inc(s_pe[b], 1)
            for b in range(2):
                nc.tensor.matmul(ps[:, b, 0:2], k["zeros16"][:, 0:W], k["zeros16"][:, 0:2], start=True,
                                 stop=True).then_inc(s_pe[b], 1)
            plan(pe, use)

        @block.vector
        def _(dve):
            def read(b, row, i):
                dve.wait_ge(s_pe[b], i + 2)
                nc.vector.tensor_copy(y[:, bass.ds(row, 1), :], ps[:, b:b + 1, 0:F]).then_inc(s_y[b], 1)
            for b in range(2):
                nc.vector.memset(first[:, b:b + 1], 0.0).then_inc(s_y[b], 1)
            plan(dve, read)
            dve.wait_ge(s_y[0], pairs + 2)
            dve.wait_ge(s_y[1], pairs + 1)


def chain_block(nc, name, steps):
    with Mem(nc, name) as l:
        step = Running("step")
        block = l.block()

        @block.vector
        def _(dve):
            for n, (eng, f) in enumerate(steps):
                if eng == "v":
                    dve.wait_ge(step.sem, step.at(n))
                    f().then_inc(step.sem, 1)
            dve.wait_ge(step.sem, step.at(len(steps)))

        @block.scalar
        def _(act):
            for n, (eng, f) in enumerate(steps):
                if eng == "a":
                    act.wait_ge(step.sem, step.at(n))
                    f().then_inc(step.sem, 1)
        step.close(len(steps))


def four_layers(nc, x, src, dst, edge_attr_16, edge_weight, edge_weight_n2, L0_gnn_W, L0_gnn_b, L0_gnn_deg_coeff,
                L0_gnn_coeff_param, L0_gnn_scale_param, L2_gnn_W1, L2_gnn_b1, L2_gnn_W2, L2_gnn_b2,
                L3_gnn_W_edge, L3_gnn_b_edge, L3_gnn_W_node, L3_gnn_b_node, out):
    v = nc.vector
    by_dst_dram = nc.dram_tensor("by_dst", [EP, 4], F32).ap()
    by_both_dram = nc.dram_tensor("by_both", [R2_ROWS, 4], F32).ap()
    c_dram = nc.dram_tensor("c_blocks", [NB * P, N], F32).ap()
    c16_dram = nc.dram_tensor("c_blocks16", [NB * P, N], BF16).ap()
    g_dram = nc.dram_tensor("g_blocks", [NB * P, N], F32).ap()
    hist_dram = nc.dram_tensor("hist", [P, P], F32).ap()
    prime_dram = nc.dram_tensor("prime", [2, P, 4], F32).ap()
    rn_dram = nc.dram_tensor("rn", [N], F32).ap()
    vec_dram = nc.dram_tensor("vec", [N], F32).ap()
    turn = [nc.dram_tensor(f"turn{i}", [N, F], F32).ap() for i in range(6)]

    with Mem(nc, "k") as top:
        k = {
            "ident": top.sb("ident", [P, P]), "before": top.sb("before", [P, P]), "ones": top.sb("ones", [P, P]),
            "ones16": top.sb("ones16", [P, 2], BF16), "zeros": top.sb("zeros", [P, 512]),
            "zeros16": top.sb("zeros16", [P, P], BF16),
            "numbers": top.sb("numbers", [P, P, CAP * max(GROUPS)], BF16), "codes": top.sb("codes", [P, NB]),
        }
        table = top.sb("table", [1, NB * NB + 7], I32)
        deg, cnt = top.sb("deg", [W, NB]), top.sb("cnt", [W, NB])
        coef = top.sb("coef", [P, 3])
        Running.sems = {n: (top.sem(n), 0) for n in ("moved", "norm_dve", "norm_act", "made", "read_act", "read_dve", "step")}
        constants(nc, top, k)
        sentinels(nc, by_both_dram)

        with Mem(nc, "sort") as m:
            rec = m.sb("rec", [P, T, 4])
            edge_records(nc, rec, src, dst, edge_attr_16, edge_weight, edge_weight_n2, L0_gnn_deg_coeff,
                         L3_gnn_W_edge, L3_gnn_b_edge)
            pos = m.sb("pos", [P, T])
            by_dst = m.sb("by_dst_m", [P, 32, TQ], BF16)
            unordered = table[0:1, NB * NB + 1:NB * NB + 2]
            order_check(nc, k, rec, unordered)
            ranks(nc, "rank_d", k, rec, 1, 1.0 / W, by_dst, pos, W // 2, unordered)
            scatter(nc, "scat_d", k, rec, pos, by_dst_dram, unordered)
            reload(nc, "load_d", rec, by_dst_dram, unordered)
            by_src = m.sb("by_src_m", [P, 32, TQ], BF16)
            ranks(nc, "rank_s", k, rec, 0, 1.0 / CODE, by_src, pos, W // 2)
            scatter(nc, "scat_s", k, rec, pos, by_both_dram)
            key_masks(nc, rec, 1, 1.0 / W, by_dst, W // 2)
            bucket_table(nc, by_src, by_dst, hist_dram, table)

        full = [W, NB, F]
        wide = lambda a: a[:, :, None].to_broadcast(full)
        dis, disS, dis2, t = (top.sb(n, [W, NB]) for n in ("dis", "disS", "dis2", "t"))
        with Mem(nc, "l0") as m:
            xS, whS = (m.sb(n, full) for n in ("xS", "whS"))
            prop = m.sb("prop", [W, NB + 1, F])
            whT = m.sb("whT", [F, N])
            whTs = m.sb("whTs", [F, NB, W])
            whD = m.sb("whD", [W, NB, F])
            rnD, rnS, rn_row = m.sb("rnD", [W, NB]), m.sb("rnS", [W, NB]), m.sb("rn_row", [W, N])
            w0, b_row, b_col = m.sb("w0", [F, F]), m.sb("b_row", [W, F]), m.sb("b_col", [F, 1])
            with Mem(nc, "pre") as q:
                xD, hD, hT = q.sb("xD", full), q.sb("hD", full), q.sb("hT", [F, N])
                copy_dma(nc, "in0", [
                    (xD[:, :, :], d_layout(x)), (xS[:, :, :], s_layout(x)), (w0[:], L0_gnn_W),
                    (b_row[:], L0_gnn_b.rearrange("(a n) -> a n", a=1).to_broadcast([W, F])),
                    (b_col[:], L0_gnn_b.rearrange("(n a) -> n a", a=1))])
                coefficients(nc, L0_gnn_coeff_param, L0_gnn_scale_param, coef)
                layer_norm_relu(nc, "ln0", xD, hD, whS)
                transpose_nodes(nc, "tr0", k, hD, hT)
                dense_T(nc, "whT", w0[:], hT, whT, b_col[:], False)
                dense(nc, "whD", lambda b: hT[:, b * W:b * W + W], w0[:], whD, b_row)
                dense(nc, "whS", lambda b: hT[:, b:N:NB], w0[:], whS, b_row)
            inverse_norms(nc, "rnD", whD, rnD)
            inverse_norms(nc, "rnS", whS, rnS)
            copy_dma(nc, "rnrow", [
                (rn_dram.rearrange("(s i) -> i s", s=NB), rnS[:]),
                (rn_row[:], rn_dram.rearrange("(a n) -> a n", a=1).to_broadcast([W, N]))])
            chain_block(nc, "whTs", [
                ("v", lambda: v.tensor_copy(whTs[:, :, :], whT[:].rearrange("f (i s) -> f s i", s=NB)))])
            build_rows(nc, k, by_both_dram, table, whT, whTs, whD, rnD, rn_row, coef, prop, cnt, deg,
                       c16_dram, c_dram, g_dram, prime_dram)

            chain_block(nc, "x1", [
                ("v", lambda: v.tensor_tensor(xS[:, :, :], xS[:, :, :], prop[:, 1:NB + 1, :], ALU.add)),
                ("v", lambda: v.scalar_tensor_tensor(xS[:, :, :], whS[:, :, :], coef[0:W, 2:3], xS[:, :, :], ALU.mult, ALU.add)),
                ("v", lambda: v.tensor_scalar(t[:], deg[:], 1.0, None, ALU.max)),
                ("a", lambda: nc.scalar.activation(t[:], t[:], ACT.Sqrt)),
                ("v", lambda: v.reciprocal(dis[:], t[:])),
                ("v", lambda: v.tensor_scalar(t[:], deg[:], 0.0, None, ALU.is_gt)),
                ("v", lambda: v.tensor_tensor(dis[:], dis[:], t[:], ALU.mult)),
                ("v", lambda: v.tensor_tensor(dis2[:], dis[:], dis[:], ALU.mult))])
            copy_dma(nc, "turn0", [
                (s_layout(turn[0]), xS[:, :, :]),
                (vec_dram.rearrange("(c p) -> p c", p=W), dis[:]), (disS[:], vec_dram.rearrange("(p c) -> p c", c=NB))])

        with Mem(nc, "l1") as m:
            xD, u, y, acc, xS = (m.sb(n, full) for n in ("xD", "u", "y", "acc", "xS"))
            copy_dma(nc, "in1", [(xD[:, :, :], d_layout(turn[0])), (acc[:, :, :], s_layout(turn[0]))])
            layer_norm_relu(nc, "ln1s", acc, u, y)
            layer_norm_relu(nc, "ln1d", xD, acc, y)
            chain_block(nc, "u0", [("v", lambda: v.tensor_tensor(u[:, :, :], u[:, :, :], wide(disS), ALU.mult))])
            with Mem(nc, "c") as q:
                c16 = q.sb("c16", [P, NB * N + 1], BF16)
                u3 = q.sb("u3", [W, NB, 3, F], BF16)
                rounds_ = table[0:1, NB * NB:NB * NB + 1]
                for i in range(3):
                    product_c(nc, f"gcn{i}", k, c16, c16_dram, c_dram, rounds_, u, u3, y, i == 0)
                    chain_block(nc, f"acc{i}", [
                        ("v", lambda: v.tensor_tensor(u[:, :, :], y[:, :, :], wide(dis), ALU.mult)),
                        ("v", lambda: v.tensor_tensor(acc[:, :, :], acc[:, :, :], u[:, :, :], ALU.add)),
                        ("v", lambda: v.tensor_tensor(y[:, :, :], y[:, :, :], wide(dis2), ALU.mult))])
                    if i < 2:
                        copy_dma(nc, f"turn{i + 1}", [(d_layout(turn[i + 1]), y[:, :, :]), (u[:, :, :], s_layout(turn[i + 1]))])
                chain_block(nc, "x2", [
                    ("v", lambda: v.scalar_tensor_tensor(xD[:, :, :], acc[:, :, :], 0.25, xD[:, :, :], ALU.mult, ALU.add))])

                layer_norm_relu(nc, "ln2", xD, acc, y)
                copy_dma(nc, "turn3", [(d_layout(turn[3]), acc[:, :, :]), (u[:, :, :], s_layout(turn[3]))])
                product_c(nc, "gin", k, c16, c16_dram, c_dram, rounds_, u, u3, y, False)
            with Mem(nc, "l2") as q:
                zT, z1T = q.sb("zT", [F, N]), q.sb("z1T", [F, N])
                w1, w2, b1, b2 = q.sb("w1", [F, F]), q.sb("w2", [F, F]), q.sb("b1", [F, 1]), q.sb("b2", [W, F])
                copy_dma(nc, "in2", [
                    (w1[:], L2_gnn_W1), (w2[:], L2_gnn_W2), (b1[:], L2_gnn_b1.rearrange("(n a) -> n a", a=1)),
                    (b2[:], L2_gnn_b2.rearrange("(a n) -> a n", a=1).to_broadcast([W, F]))])
                chain_block(nc, "z", [("v", lambda: v.tensor_tensor(y[:, :, :], y[:, :, :], acc[:, :, :], ALU.add))])
                transpose_nodes(nc, "tr2", k, y, zT)
                dense_T(nc, "z1", w1[:], zT, z1T, b1[:], True)
                dense(nc, "z2", lambda b: z1T[:, b * W:b * W + W], w2[:], y, b2, relu=True)
                chain_block(nc, "x3", [("v", lambda: v.tensor_tensor(xD[:, :, :], xD[:, :, :], y[:, :, :], ALU.add))])

            layer_norm_relu(nc, "ln3", xD, acc, y)
            copy_dma(nc, "turn4", [(d_layout(turn[4]), xD[:, :, :]), (xS[:, :, :], s_layout(turn[4]))])
            with Mem(nc, "l3") as q:
                hT = q.sb("hT", [F, N])
                wn, wnT, bn = q.sb("wn", [F, F]), q.sb("wnT", [F, F]), q.sb("bn", [W, F])
                wps = q.ps("wps", [F, F])
                copy_dma(nc, "in3", [(wn[:], L3_gnn_W_node),
                                     (bn[:], L3_gnn_b_node.rearrange("(a n) -> a n", a=1).to_broadcast([W, F]))])
                with Mem(nc, "wnT") as l:
                    s_t, s_c = l.sem("t"), l.sem("c")
                    block = l.block()

                    @block.tensor
                    def _(pe):
                        nc.tensor.transpose(wps[:], wn[:], k["ident"][0:F, 0:F]).then_inc(s_t, 1)

                    @block.vector
                    def _(dve):
                        dve.wait_ge(s_t, 1)
                        v.tensor_copy(wnT[:], wps[:]).then_inc(s_c, 1)
                        dve.wait_ge(s_c, 1)
                transpose_nodes(nc, "tr3", k, acc, hT)
                dense(nc, "xp", lambda b: hT[:, b * W:b * W + W], wnT[:], u, bn)
            product_g(nc, "gated", k, g_dram, u, y)
            chain_block(nc, "x4", [
                ("v", lambda: v.tensor_scalar(t[:], cnt[:], 1.0, None, ALU.max)),
                ("v", lambda: v.reciprocal(dis[:], t[:])),
                ("v", lambda: v.tensor_tensor(y[:, :, :], y[:, :, :], wide(dis), ALU.mult)),
                ("v", lambda: v.tensor_tensor(xS[:, :, :], xS[:, :, :], y[:, :, :], ALU.add))])
            copy_dma(nc, "end", [(s_layout(out), xS[:, :, :])])


_INS = ["x", "src", "dst", "edge_attr_16", "edge_weight", "edge_weight_n2", "L0_gnn_W", "L0_gnn_b", "L0_gnn_deg_coeff",
        "L0_gnn_coeff_param", "L0_gnn_scale_param", "L2_gnn_W1", "L2_gnn_b1", "L2_gnn_W2", "L2_gnn_b2",
        "L3_gnn_W_edge", "L3_gnn_b_edge", "L3_gnn_W_node", "L3_gnn_b_node"]


def kernel(**inputs):
    import numpy as _np
    import concourse.bacc as _bacc
    from concourse import mybir as _mybir
    from concourse.bass_utils import run_bass_kernel_spmd as _run

    nc = _bacc.Bacc("TRN2", target_bir_lowering=False, num_devices=1)
    arrays, args = {}, []
    for name in _INS:
        a = _np.ascontiguousarray(inputs[name])
        arrays[f"in_{name}"] = a
        args.append(nc.dram_tensor(f"in_{name}", a.shape, _mybir.dt.from_np(a.dtype), kind="ExternalInput").ap())
    args.append(nc.dram_tensor("out_x", (N, F), F32, kind="ExternalOutput").ap())
    four_layers(nc, *args)
    r = _run(nc, [arrays], core_ids=[0])
    return r.results[0]["out_x"]
```
